# Optimizing a Trainium2 kernel written in Bass

```python
import numpy as np
import jax
import jax.numpy as jnp

def _softmax(x, axis=-1):
    return jax.nn.softmax(x, axis=axis)

def _gelu(x):
    return jax.nn.gelu(x, approximate=True)

def _silu(x):
    return jax.nn.silu(x)

def _sigmoid(x):
    return jax.nn.sigmoid(x)

def _layernorm(x, axis=-1, eps=1e-05):
    m = jnp.mean(x, axis=axis, keepdims=True)
    v = jnp.var(x, axis=axis, keepdims=True)
    return (x - m) / jnp.sqrt(v + eps)

def _scatter_add(tgt, idx, src, axis=0):
    return tgt.at[idx].add(src)

def _segment_sum(src, seg, n):
    return jax.ops.segment_sum(src, seg, n)
kernel_name = 'mk_adaln_d1_jaxref_r4_a8722c'

def setup_inputs(seed: int=0):
    np.random.seed(seed)
    _w = jnp.asarray

    def _L0_attn_setup():
        import math
        import jax, jax.numpy as jnp
        import numpy as np
        D_MODEL = 256
        NUM_SCALES = 4
        STATE_SIZE = 16
        EXPAND = 2
        D_INNER = D_MODEL * EXPAND
        D_PER_SCALE = D_INNER // NUM_SCALES
        BATCH, SEQ = (4, 1024)

        def _make_A_log():
            base = np.arange(1, STATE_SIZE + 1, dtype=np.float32)
            parts = [np.broadcast_to(base * 2.0 ** i, (D_PER_SCALE, STATE_SIZE)) for i in range(NUM_SCALES)]
            A = np.concatenate(parts, axis=0)
            return jnp.asarray(np.log(A))

        def _selective_scan(x_ssm, A, B_mat, C_mat, dt):
            b, L, d = x_ssm.shape
            N = A.shape[1]
            h0 = jnp.zeros((b, d, N), dtype=jnp.float32)

            def step(h, inp):
                dt_t, B_t, C_t, x_t = inp
                A_bar = jnp.exp(jnp.minimum(dt_t[..., None] * A, 20.0))
                B_bar = dt_t[..., None] * B_t[:, None, :]
                h = A_bar * h + B_bar * x_t[..., None]
                y_t = jnp.einsum('bdn,bn->bd', h, C_t)
                return (h, y_t)
            xs = (jnp.swapaxes(dt, 0, 1), jnp.swapaxes(B_mat, 0, 1), jnp.swapaxes(C_mat, 0, 1), jnp.swapaxes(x_ssm, 0, 1))
            _, ys = jax.lax.scan(step, h0, xs)
            return jnp.swapaxes(ys, 0, 1)
        key = jax.random.key(seed)
        ks = jax.random.split(key, 8)
        scale = 0.02
        x = jax.random.normal(ks[0], (BATCH, SEQ, D_MODEL), dtype=jnp.float32)
        W_in = jax.random.normal(ks[1], (2 * D_INNER, D_MODEL), dtype=jnp.float32) * scale
        W_B = jax.random.normal(ks[2], (STATE_SIZE, D_INNER), dtype=jnp.float32) * scale
        W_C = jax.random.normal(ks[3], (STATE_SIZE, D_INNER), dtype=jnp.float32) * scale
        W_dt = jax.random.normal(ks[4], (D_INNER, D_INNER), dtype=jnp.float32) * scale
        u = jax.random.uniform(ks[5], (D_INNER,), dtype=jnp.float32)
        b_dt = u * (math.log(0.1) - math.log(0.001)) + math.log(0.001)
        W_out = jax.random.normal(ks[6], (D_MODEL, D_INNER), dtype=jnp.float32) * scale
        A_log = _make_A_log()
        D = jnp.ones((D_INNER,), dtype=jnp.float32)
        output_gate = jnp.zeros((1,), dtype=jnp.float32)
        return {'x': x, 'W_in': W_in, 'A_log': A_log, 'W_B': W_B, 'W_C': W_C, 'W_dt': W_dt, 'b_dt': b_dt, 'D': D, 'output_gate': output_gate, 'W_out': W_out}
    _L0_attn_in = _L0_attn_setup()

    def _L0_ffn_setup():
        import jax, jax.numpy as jnp
        import numpy as np
        DIM = 256
        DEPTH = 2
        HEADS = 8
        DIM_HEAD = 64
        WINDOW = 128
        INNER = HEADS * DIM_HEAD
        HID = int(DIM * 4 * 2 / 3)
        B, N = (2, 2048)
        QK_SCALE = 8.0

        def shift_token(t):
            t1, t2 = jnp.split(t, 2, axis=-1)
            t2 = jnp.pad(t2, ((0, 0), (1, 0), (0, 0)))[:, :-1]
            return jnp.concatenate([t1, t2], axis=-1)

        def l2norm(t):
            return t / jnp.clip(jnp.linalg.norm(t, axis=-1, keepdims=True), 1e-12)

        def rotate_half(x):
            x1, x2 = jnp.split(x, 2, axis=-1)
            return jnp.concatenate([-x2, x1], axis=-1)

        def rotary_xpos(q, k):
            n = q.shape[-2]
            half_idx = jnp.arange(0, DIM_HEAD, 2, dtype=jnp.float32)
            inv_freq = 1.0 / 10000.0 ** (half_idx / DIM_HEAD)
            t = jnp.arange(n, dtype=jnp.float32)
            freqs = t[:, None] * inv_freq[None, :]
            freqs = jnp.concatenate([freqs, freqs], axis=-1)
            base = (half_idx + 0.4 * DIM_HEAD) / (1.4 * DIM_HEAD)
            power = (t - n // 2) / float(WINDOW // 2)
            scale = base[None, :] ** power[:, None]
            scale = jnp.concatenate([scale, scale], axis=-1)
            cos, sin = (jnp.cos(freqs), jnp.sin(freqs))
            q = q * cos * scale + rotate_half(q) * sin * scale
            k = k * cos / scale + rotate_half(k) * sin / scale
            return (q, k)

        def local_attention(q, k, v):
            b, h, n, d = q.shape
            w = n // WINDOW
            bq = q.reshape(b, h, w, WINDOW, d) * QK_SCALE
            bk = k.reshape(b, h, w, WINDOW, d)
            bv = v.reshape(b, h, w, WINDOW, d)

            def look_around(t):
                p = jnp.pad(t, ((0, 0), (0, 0), (1, 0), (0, 0), (0, 0)))
                return jnp.concatenate([p[:, :, :w], p[:, :, 1:]], axis=3)
            bk, bv = (look_around(bk), look_around(bv))
            bt = jnp.arange(n).reshape(w, WINDOW)
            btp = jnp.pad(bt, ((1, 0), (0, 0)), constant_values=-1)
            btk = jnp.concatenate([btp[:w], btp[1:]], axis=1)
            sim = jnp.einsum('bhwid,bhwjd->bhwij', bq, bk)
            i = bt[:, :, None]
            j = btk[:, None, :]
            mask = (i < j) | (i > j + WINDOW) | (j == -1)
            sim = jnp.where(mask, -jnp.finfo(sim.dtype).max, sim)
            attn = jax.nn.softmax(sim, axis=-1)
            out = jnp.einsum('bhwij,bhwjd->bhwid', attn, bv)
            return out.reshape(b, h, n, d)

        def _layer(x, wqkv, qs, ksc, wo, lg, lb, w1, b1, w2, b2):
            b, n, _ = x.shape
            h = shift_token(x)
            qkv = h @ wqkv
            q, k, v = jnp.split(qkv, 3, axis=-1)
            to_heads = lambda t: t.reshape(b, n, HEADS, DIM_HEAD).transpose(0, 2, 1, 3)
            q, k, v = (to_heads(q), to_heads(k), to_heads(v))
            q = l2norm(q) * qs
            k = l2norm(k) * ksc
            q, k = rotary_xpos(q, k)
            o = local_attention(q, k, v)
            o = o.transpose(0, 2, 1, 3).reshape(b, n, INNER)
            x = x + o @ wo
            h = shift_token(x)
            mu = h.mean(-1, keepdims=True)
            var = h.var(-1, keepdims=True)
            h = (h - mu) / jnp.sqrt(var + 1e-05) * lg + lb
            h = h @ w1 + b1
            a, g = jnp.split(h, 2, axis=-1)
            h = a * jax.nn.gelu(g, approximate=False)
            x = x + h @ w2 + b2
            return x
        key = jax.random.key(seed)
        ks = jax.random.split(key, 6)
        return {'x': jax.random.normal(ks[0], (B, N, DIM), jnp.float32), 'wqkv': jax.random.normal(ks[1], (DEPTH, DIM, 3 * INNER), jnp.float32) * 0.02, 'q_scale': jnp.ones((DEPTH, DIM_HEAD), jnp.float32), 'k_scale': jnp.ones((DEPTH, DIM_HEAD), jnp.float32), 'wo': jax.random.normal(ks[2], (DEPTH, INNER, DIM), jnp.float32) * 0.02, 'ln_g': jnp.ones((DEPTH, DIM), jnp.float32), 'ln_b': jnp.zeros((DEPTH, DIM), jnp.float32), 'w1': jax.random.normal(ks[3], (DEPTH, DIM, 2 * HID), jnp.float32) * 0.02, 'b1': jnp.zeros((DEPTH, 2 * HID), jnp.float32), 'w2': jax.random.normal(ks[4], (DEPTH, HID, DIM), jnp.float32) * 0.02, 'b2': jnp.zeros((DEPTH, DIM), jnp.float32)}
    _L0_ffn_in = _L0_ffn_setup()
    _L0_c = _w((lambda *s: np.random.randn(*s).astype(np.float32) * 0.05)(16, 256))
    _L0_wmod = _w((lambda *s: np.random.randn(*s).astype(np.float32) * 0.05)(256, 6 * 256) * 256 ** (-0.5))
    _d = {'L0_attn_x': _L0_attn_in['x'], 'L0_attn_W_in': _L0_attn_in['W_in'], 'L0_attn_A_log': _L0_attn_in['A_log'], 'L0_attn_W_B': _L0_attn_in['W_B'], 'L0_attn_W_C': _L0_attn_in['W_C'], 'L0_attn_W_dt': _L0_attn_in['W_dt'], 'L0_attn_b_dt': _L0_attn_in['b_dt'], 'L0_attn_D': _L0_attn_in['D'], 'L0_attn_output_gate': _L0_attn_in['output_gate'], 'L0_attn_W_out': _L0_attn_in['W_out'], 'L0_ffn_wqkv': _L0_ffn_in['wqkv'], 'L0_ffn_q_scale': _L0_ffn_in['q_scale'], 'L0_ffn_k_scale': _L0_ffn_in['k_scale'], 'L0_ffn_wo': _L0_ffn_in['wo'], 'L0_ffn_ln_g': _L0_ffn_in['ln_g'], 'L0_ffn_ln_b': _L0_ffn_in['ln_b'], 'L0_ffn_w1': _L0_ffn_in['w1'], 'L0_ffn_b1': _L0_ffn_in['b1'], 'L0_ffn_w2': _L0_ffn_in['w2'], 'L0_ffn_b2': _L0_ffn_in['b2'], 'L0_c': _L0_c, 'L0_wmod': _L0_wmod}
    _x0 = _d['L0_attn_x']
    _d['L0_attn_x'] = jax.random.normal(jax.random.fold_in(jax.random.key(seed), 1), (16, 512, 256), dtype=_x0.dtype)
    del _x0
    return _d

def reference(L0_attn_x, L0_attn_W_in, L0_attn_A_log, L0_attn_W_B, L0_attn_W_C, L0_attn_W_dt, L0_attn_b_dt, L0_attn_D, L0_attn_output_gate, L0_attn_W_out, L0_ffn_wqkv, L0_ffn_q_scale, L0_ffn_k_scale, L0_ffn_wo, L0_ffn_ln_g, L0_ffn_ln_b, L0_ffn_w1, L0_ffn_b1, L0_ffn_w2, L0_ffn_b2, L0_c, L0_wmod):

    def _L0_attn_ref(x, W_in, A_log, W_B, W_C, W_dt, b_dt, D, output_gate, W_out):
        import math
        import jax, jax.numpy as jnp
        import numpy as np
        D_MODEL = 256
        NUM_SCALES = 4
        STATE_SIZE = 16
        EXPAND = 2
        D_INNER = D_MODEL * EXPAND
        D_PER_SCALE = D_INNER // NUM_SCALES
        BATCH, SEQ = (4, 1024)

        def _make_A_log():
            base = np.arange(1, STATE_SIZE + 1, dtype=np.float32)
            parts = [np.broadcast_to(base * 2.0 ** i, (D_PER_SCALE, STATE_SIZE)) for i in range(NUM_SCALES)]
            A = np.concatenate(parts, axis=0)
            return jnp.asarray(np.log(A))

        def _selective_scan(x_ssm, A, B_mat, C_mat, dt):
            b, L, d = x_ssm.shape
            N = A.shape[1]
            h0 = jnp.zeros((b, d, N), dtype=jnp.float32)

            def step(h, inp):
                dt_t, B_t, C_t, x_t = inp
                A_bar = jnp.exp(jnp.minimum(dt_t[..., None] * A, 20.0))
                B_bar = dt_t[..., None] * B_t[:, None, :]
                h = A_bar * h + B_bar * x_t[..., None]
                y_t = jnp.einsum('bdn,bn->bd', h, C_t)
                return (h, y_t)
            xs = (jnp.swapaxes(dt, 0, 1), jnp.swapaxes(B_mat, 0, 1), jnp.swapaxes(C_mat, 0, 1), jnp.swapaxes(x_ssm, 0, 1))
            _, ys = jax.lax.scan(step, h0, xs)
            return jnp.swapaxes(ys, 0, 1)
        xz = jnp.einsum('bld,ed->ble', x, W_in)
        x_ssm, z = jnp.split(xz, 2, axis=-1)
        A = -jnp.exp(A_log.astype(jnp.float32))
        B_mat = jnp.einsum('bld,nd->bln', x_ssm, W_B)
        C_mat = jnp.einsum('bld,nd->bln', x_ssm, W_C)
        dt = jax.nn.softplus(jnp.einsum('bld,ed->ble', x_ssm, W_dt) + b_dt)
        y = _selective_scan(x_ssm.astype(jnp.float32), A, B_mat.astype(jnp.float32), C_mat.astype(jnp.float32), dt.astype(jnp.float32))
        y = y + x_ssm * D[None, None, :]
        y = y * jax.nn.silu(z)
        out = jnp.einsum('ble,de->bld', y, W_out) * jax.nn.sigmoid(output_gate)
        return out

    def _L0_ffn_ref(x, wqkv, q_scale, k_scale, wo, ln_g, ln_b, w1, b1, w2, b2):
        import jax, jax.numpy as jnp
        import numpy as np
        DIM = 256
        DEPTH = 2
        HEADS = 8
        DIM_HEAD = 64
        WINDOW = 128
        INNER = HEADS * DIM_HEAD
        HID = int(DIM * 4 * 2 / 3)
        B, N = (2, 2048)
        QK_SCALE = 8.0

        def shift_token(t):
            t1, t2 = jnp.split(t, 2, axis=-1)
            t2 = jnp.pad(t2, ((0, 0), (1, 0), (0, 0)))[:, :-1]
            return jnp.concatenate([t1, t2], axis=-1)

        def l2norm(t):
            return t / jnp.clip(jnp.linalg.norm(t, axis=-1, keepdims=True), 1e-12)

        def rotate_half(x):
            x1, x2 = jnp.split(x, 2, axis=-1)
            return jnp.concatenate([-x2, x1], axis=-1)

        def rotary_xpos(q, k):
            n = q.shape[-2]
            half_idx = jnp.arange(0, DIM_HEAD, 2, dtype=jnp.float32)
            inv_freq = 1.0 / 10000.0 ** (half_idx / DIM_HEAD)
            t = jnp.arange(n, dtype=jnp.float32)
            freqs = t[:, None] * inv_freq[None, :]
            freqs = jnp.concatenate([freqs, freqs], axis=-1)
            base = (half_idx + 0.4 * DIM_HEAD) / (1.4 * DIM_HEAD)
            power = (t - n // 2) / float(WINDOW // 2)
            scale = base[None, :] ** power[:, None]
            scale = jnp.concatenate([scale, scale], axis=-1)
            cos, sin = (jnp.cos(freqs), jnp.sin(freqs))
            q = q * cos * scale + rotate_half(q) * sin * scale
            k = k * cos / scale + rotate_half(k) * sin / scale
            return (q, k)

        def local_attention(q, k, v):
            b, h, n, d = q.shape
            w = n // WINDOW
            bq = q.reshape(b, h, w, WINDOW, d) * QK_SCALE
            bk = k.reshape(b, h, w, WINDOW, d)
            bv = v.reshape(b, h, w, WINDOW, d)

            def look_around(t):
                p = jnp.pad(t, ((0, 0), (0, 0), (1, 0), (0, 0), (0, 0)))
                return jnp.concatenate([p[:, :, :w], p[:, :, 1:]], axis=3)
            bk, bv = (look_around(bk), look_around(bv))
            bt = jnp.arange(n).reshape(w, WINDOW)
            btp = jnp.pad(bt, ((1, 0), (0, 0)), constant_values=-1)
            btk = jnp.concatenate([btp[:w], btp[1:]], axis=1)
            sim = jnp.einsum('bhwid,bhwjd->bhwij', bq, bk)
            i = bt[:, :, None]
            j = btk[:, None, :]
            mask = (i < j) | (i > j + WINDOW) | (j == -1)
            sim = jnp.where(mask, -jnp.finfo(sim.dtype).max, sim)
            attn = jax.nn.softmax(sim, axis=-1)
            out = jnp.einsum('bhwij,bhwjd->bhwid', attn, bv)
            return out.reshape(b, h, n, d)

        def _layer(x, wqkv, qs, ksc, wo, lg, lb, w1, b1, w2, b2):
            b, n, _ = x.shape
            h = shift_token(x)
            qkv = h @ wqkv
            q, k, v = jnp.split(qkv, 3, axis=-1)
            to_heads = lambda t: t.reshape(b, n, HEADS, DIM_HEAD).transpose(0, 2, 1, 3)
            q, k, v = (to_heads(q), to_heads(k), to_heads(v))
            q = l2norm(q) * qs
            k = l2norm(k) * ksc
            q, k = rotary_xpos(q, k)
            o = local_attention(q, k, v)
            o = o.transpose(0, 2, 1, 3).reshape(b, n, INNER)
            x = x + o @ wo
            h = shift_token(x)
            mu = h.mean(-1, keepdims=True)
            var = h.var(-1, keepdims=True)
            h = (h - mu) / jnp.sqrt(var + 1e-05) * lg + lb
            h = h @ w1 + b1
            a, g = jnp.split(h, 2, axis=-1)
            h = a * jax.nn.gelu(g, approximate=False)
            x = x + h @ w2 + b2
            return x
        for l in range(DEPTH):
            x = _layer(x, wqkv[l], q_scale[l], k_scale[l], wo[l], ln_g[l], ln_b[l], w1[l], b1[l], w2[l], b2[l])
        return x
    x = L0_attn_x
    mod = (_silu(L0_c) @ L0_wmod).reshape(L0_c.shape[0], 6, 1, -1)
    sa, ca, ga, sb, cb, gb = (mod[:, 0], mod[:, 1], mod[:, 2], mod[:, 3], mod[:, 4], mod[:, 5])
    ga = (2 * (ga >= 0) - 1) * jnp.maximum(jnp.abs(ga), 0.25)
    gb = (2 * (gb >= 0) - 1) * jnp.maximum(jnp.abs(gb), 0.25)
    h = _layernorm(x, axis=-1) * (1 + ca) + sa
    x = x + ga * _L0_attn_ref(h, L0_attn_W_in, L0_attn_A_log, L0_attn_W_B, L0_attn_W_C, L0_attn_W_dt, L0_attn_b_dt, L0_attn_D, L0_attn_output_gate, L0_attn_W_out)
    h = _layernorm(x, axis=-1) * (1 + cb) + sb
    x = x + gb * _L0_ffn_ref(h, L0_ffn_wqkv, L0_ffn_q_scale, L0_ffn_k_scale, L0_ffn_wo, L0_ffn_ln_g, L0_ffn_ln_b, L0_ffn_w1, L0_ffn_b1, L0_ffn_w2, L0_ffn_b2)
    return x

_drawn_inputs = setup_inputs


def setup_inputs(seed=0):
    import zlib

    import numpy as np

    out = dict(_drawn_inputs(seed))
    spreads = {'L0_attn_D': (1.0, 0.6),
     'L0_ffn_q_scale': (1.0, 0.6),
     'L0_ffn_k_scale': (1.0, 0.6),
     'L0_ffn_ln_g': (1.0, 0.6),
     'L0_ffn_ln_b': (0.0, 2.0),
     'L0_ffn_b1': (0.0, 2.0),
     'L0_ffn_b2': (0.0, 0.8)}
    factors = {'L0_attn_W_in': 8.0,
     'L0_attn_A_log': 8.0,
     'L0_attn_W_B': 8.0,
     'L0_attn_W_C': 8.0,
     'L0_attn_W_dt': 8.0,
     'L0_attn_b_dt': 8.0,
     'L0_attn_W_out': 8.0,
     'L0_ffn_wqkv': 6.221,
     'L0_ffn_wo': 6.144,
     'L0_ffn_w1': 4.75,
     'L0_ffn_w2': 4.73}
    for name, (base, spread) in spreads.items():
        noise = np.random.default_rng([zlib.crc32(name.encode()), seed]).standard_normal(out[name].shape)
        drawn = base * np.exp(spread * noise) if base else spread * noise
        out[name] = jnp.asarray(drawn.astype(out[name].dtype))
    for name, factor in factors.items():
        out[name] = (out[name] * factor).astype(out[name].dtype)
    return out
```

```python
from contextlib import ExitStack

import numpy as np

import concourse.bass as bass
import concourse.mybir as mybir
from concourse.alu_op_type import AluOpType as ALU

ACT = mybir.ActivationFunctionType
F32 = mybir.dt.float32
BF16 = mybir.dt.bfloat16
I32 = mybir.dt.int32
AX_X = mybir.AxisListType.X

P = 128
BATCH, SEQ, DIM = 16, 512, 256
CHUNKS = DIM // P
TILES = SEQ // P
D_INNER = 512
INNER_CHUNKS = D_INNER // P
STATES = 16
GROUP = 4
GROUPS = STATES // GROUP
UNITS = GROUPS * INNER_CHUNKS
DEPTH, HEADS, DIM_HEAD, WINDOW = 2, 8, 64, 128
INNER = HEADS * DIM_HEAD
PAIRS = HEADS // 2
HID = int(DIM * 4 * 2 / 3)
HID_CHUNKS = -(-HID // P)
QK_SCALE = 8.0
LN_EPS = 1e-5
SERIES_BELOW = 0.02
MASKED = -3.0e38
SCREEN = 2.0 ** 17
EXP_AND_LN = "natural_log_exp_and_others"
MOD_SHIFT_A, MOD_SCALE_A, MOD_GATE_A, MOD_SHIFT_B, MOD_SCALE_B, MOD_GATE_B = range(6)


class Signal:

    def __init__(self, sem, per_pass, unit=1):
        self.sem, self.per_pass, self.unit = sem, per_pass * unit, unit

    def at(self, done, k=0):
        return done * self.per_pass + (k * self.unit + 1)


def start_signals(nc, signals):
    with nc.Block() as block:
        @block.gpsimd
        def _(pool):
            for signal in signals:
                pool.sem_inc(signal.sem, 1)


class Banks:

    def __init__(self, tiles, full, uses):
        self.tiles, self.full = tiles, full
        self.where, self.count, self.before, last = {}, [0] * len(tiles), {}, {}
        for name, bank, signal, k in uses:
            self.where[name] = (bank, self.count[bank])
            self.count[bank] += 1
            self.before[name] = last.get(bank)
            last[bank] = (signal, k)
        for name, bank, _, _ in uses:
            if self.before[name] is None:
                self.before[name] = (last[bank][0], 0)

    def tile(self, name):
        return self.tiles[self.where[name][0]]

    def wait_free(self, eng, done, name):
        signal, k = self.before[name]
        eng.wait_ge(signal.sem, signal.at(done, k))

    def wait_full(self, eng, done, name):
        bank, k = self.where[name]
        eng.wait_ge(self.full[bank], done * self.count[bank] + k + 1)

    def filled(self, instruction, name):
        instruction.then_inc(self.full[self.where[name][0]], 1)


def host_constants():
    eye = np.eye(P, dtype=np.float32)
    mean = np.full((P, P), 1.0 / DIM, np.float32)
    half = np.arange(P) // DIM_HEAD
    head_ones = (half[:, None] == half[None, :]).astype(np.float32)
    d = np.arange(P)
    partner = np.where(d % DIM_HEAD < DIM_HEAD // 2, d + DIM_HEAD // 2, d - DIM_HEAD // 2)
    turn = np.zeros((P, P), np.float32)
    turn[partner, d] = 1.0
    i, j = np.arange(WINDOW)[:, None], np.arange(WINDOW)[None, :]
    mask_back = np.where(j >= i, 0.0, MASKED).astype(np.float32)
    mask_own = np.where(j <= i, 0.0, MASKED).astype(np.float32)
    squares = np.concatenate([eye, mean, head_ones, turn, mask_back, mask_own], axis=1)
    pick = np.zeros((P, 2 * STATES), np.float32)
    pick[np.arange(96), np.arange(96) % (2 * STATES)] = 1.0
    pair = np.stack([half == 0, half == 1], axis=1).astype(np.float32)
    small = np.concatenate([pick, pair], axis=1)
    f32 = np.float32
    half_idx = np.arange(0, DIM_HEAD, 2, dtype=f32)
    inv_freq = f32(1.0) / np.power(f32(10000.0), half_idx / f32(DIM_HEAD), dtype=f32)
    t = np.arange(SEQ, dtype=f32)
    freqs = (t[:, None] * inv_freq[None, :]).astype(f32)
    base = ((half_idx + f32(0.4 * DIM_HEAD)) / f32(1.4 * DIM_HEAD)).astype(f32)
    power = ((t - f32(SEQ // 2)) / f32(WINDOW // 2)).astype(f32)
    scale = np.power(base[None, :], power[:, None], dtype=f32)
    cos, sin = np.cos(freqs, dtype=f32), np.sin(freqs, dtype=f32)
    col = d % (DIM_HEAD // 2)
    sign = np.where(d % DIM_HEAD < DIM_HEAD // 2, -1.0, 1.0).astype(f32)[:, None]
    cos, sin, scale = cos.T[col], sin.T[col] * sign, scale.T[col]
    rotary = np.stack([cos * scale, sin * scale, cos / scale, sin / scale], axis=1).astype(f32)
    return {"c_squares": squares, "c_small": small, "c_rotary": np.ascontiguousarray(rotary)}


def mixer_pass(nc, inp, mod, x1_dram, stack_dram):
    with ExitStack() as ctx:
        def sb(name, shape, dt=F32):
            return ctx.enter_context(nc.sbuf_tensor("a_" + name, shape, dt))

        def sem(name):
            return ctx.enter_context(nc.semaphore("a_" + name))

        signals = []

        def signal(name, per_pass, unit=1):
            signals.append(Signal(sem(name), per_pass, unit))
            return signals[-1]

        banks_all = [ctx.enter_context(nc.psum_tensor(f"a_bank{i}", [P, 512], F32)) for i in range(8)]

        ident = sb("ident", [P, P])
        mean_mat = sb("mean_mat", [P, P])
        pick = sb("pick", [P, 2 * STATES])
        picks = sb("picks", [P, 2 * STATES, P], BF16)
        w_in_t = sb("w_in_t", [P, CHUNKS, 2 * D_INNER])
        w_dt_t = sb("w_dt_t", [P, INNER_CHUNKS, D_INNER])
        w_bc_t = sb("w_bc_t", [P, INNER_CHUNKS, 2 * STATES])
        w_out_t = sb("w_out_t", [P, INNER_CHUNKS, DIM])
        neg_a = sb("neg_a", [P, INNER_CHUNKS, STATES])
        b_dt = sb("b_dt", [P, INNER_CHUNKS])
        skip_d = sb("skip_d", [P, INNER_CHUNKS])
        ln_eps = sb("ln_eps", [P, 1])
        waiter = sb("waiter", [P, 2])

        setup_weights(nc, inp, banks_all, ident, mean_mat, pick, picks, w_in_t, w_dt_t, w_bc_t, w_out_t,
                      neg_a, b_dt, skip_d, mod, ln_eps)

        xt = sb("xt", [P, TILES, DIM])
        x_t = sb("x_t", [P, CHUNKS, SEQ])
        xc = sb("xc", [P, CHUNKS, SEQ])
        sq = sb("sq", [P, CHUNKS, SEQ])
        lnv = sb("lnv", [P, SEQ])
        rstd = sb("rstd", [P, SEQ])
        h_t = sb("h_t", [P, CHUNKS, SEQ])
        xs = sb("xs", [P, INNER_CHUNKS, SEQ])
        sz = sb("sz", [P, INNER_CHUNKS, SEQ])
        dt = sb("dt", [P, INNER_CHUNKS, SEQ])
        u = sb("u", [P, INNER_CHUNKS, SEQ])
        sp_e = sb("sp_e", [P, 2, SEQ])
        sp_ln = sb("sp_ln", [P, 2, SEQ])
        sp_relu = sb("sp_relu", [P, 2, SEQ])
        sp_p = sb("sp_p", [P, 2, SEQ])
        sp_mask = sb("sp_mask", [P, 2, SEQ], I32)
        bc_parts = sb("bc_parts", [P, SEQ], BF16)
        bc_rest = sb("bc_rest", [2 * STATES, SEQ])
        bc_mid = sb("bc_mid", [2 * STATES, SEQ], BF16)
        decay = [sb(f"decay{i}", [P, GROUP, SEQ]) for i in range(2)]
        state = [sb(f"state{i}", [P, GROUP, SEQ]) for i in range(4)]
        b_wide = [sb(f"b_wide{i}", [P, GROUP, SEQ]) for i in range(2)]
        c_wide = [sb(f"c_wide{i}", [P, GROUP, SEQ]) for i in range(2)]
        x1_t = sb("x1_t", [P, CHUNKS, SEQ])
        yv = u

        x_loaded = signal("x_loaded", 1, 16)
        x_t_done = signal("x_t_done", CHUNKS)
        xc_done = signal("xc_done", 2 * CHUNKS)
        sq_done = signal("sq_done", 2)
        lnv_done = signal("lnv_done", 2)
        rstd_done = signal("rstd_done", 2)
        xn_done = signal("xn_done", 2)
        h_done = signal("h_done", 2 * CHUNKS)
        xs_done = signal("xs_done", INNER_CHUNKS)
        sz_done = signal("sz_done", INNER_CHUNKS)
        abs_done = signal("abs_done", INNER_CHUNKS)
        exp_done = signal("exp_done", 2)
        ln_done = signal("ln_done", 2)
        series_done = signal("series_done", 12)
        dt_done = signal("dt_done", 2)
        u_done = signal("u_done", 2)
        parts_done = signal("parts_done", 5)
        b_wide_done = signal("b_wide_done", STATES)
        c_wide_done = signal("c_wide_done", STATES)
        decay_done = signal("decay_done", UNITS)
        input_done = signal("input_done", UNITS)
        scan_done = signal("scan_done", UNITS)
        on_vector = [q for q in range(UNITS) if q % 4 == 3]
        on_pool = [q for q in range(UNITS) if q not in on_vector]
        cmul_pool_done = signal("cmul_pool_done", len(on_pool))
        cmul_vec_done = signal("cmul_vec_done", len(on_vector))
        sum_done = signal("sum_done", UNITS)
        skip_done = signal("skip_done", INNER_CHUNKS)
        gated_done = signal("gated_done", INNER_CHUNKS)
        x1_done = signal("x1_done", CHUNKS)
        stored = signal("stored", 2, 16)

        def ln_uses(j):
            return [(f"mean{j}", 2, xc_done, CHUNKS * (j + 1)), (f"var{j}", 3, lnv_done, j + 1)]

        uses = [("xT0", 0, x_t_done, 1), ("xT1", 1, x_t_done, 2)] + ln_uses(0)
        uses += [(f"xz{m}", m, xs_done, m + 1) for m in range(4)] + [(f"xz{4 + m}", m, sz_done, m + 1) for m in range(4)]
        uses += [(f"dt{m}", m, abs_done, m + 1) for m in range(4)] + [("bc", 0, parts_done, 2)]
        uses += [(f"wide{i}", i % 4, b_wide_done if i % 8 < GROUP else c_wide_done, GROUP * (i // 8) + i % GROUP + 1)
                 for i in range(2 * STATES)]
        uses += [(f"out{m}", m, x1_done, m + 1) for m in range(CHUNKS)] + ln_uses(1)
        work = Banks(banks_all[:4], [sem(f"full{i}") for i in range(4)], uses)
        y_sum = banks_all[4:]

        def wide_order(g):
            return [(f"wide{2 * GROUP * g + i}", i < GROUP, GROUP * g + i % GROUP) for i in range(2 * GROUP)]

        def cmul_wait(eng, done, q):
            if q in on_pool:
                eng.wait_ge(cmul_pool_done.sem, cmul_pool_done.at(done, on_pool.index(q) + 1))
            else:
                eng.wait_ge(cmul_vec_done.sem, cmul_vec_done.at(done, on_vector.index(q) + 1))

        start_signals(nc, signals)
        block = ctx.enter_context(nc.Block())

        @block.sync
        def _(sp):
            def load(b):
                sp.dma_start(xt[:], inp["L0_attn_x"][b].rearrange("(t p) d -> p t d", p=P)).then_inc(x_loaded.sem, 16)

            def store(b):
                sp.wait_ge(x1_done.sem, x1_done.at(b, CHUNKS))
                sp.dma_start(x1_dram[b], x1_t[:]).then_inc(stored.sem, 16)
                sp.wait_ge(h_done.sem, h_done.at(b, 2 * CHUNKS))
                sp.dma_start(stack_dram[b], h_t[:]).then_inc(stored.sem, 16)

            load(0)
            with sp.Fori(0, BATCH - 1) as b:
                sp.wait_ge(x_t_done.sem, x_t_done.at(b, CHUNKS))
                load(b + 1)
                store(b)
            store(BATCH - 1)
            sp.wait_ge(stored.sem, stored.at(BATCH))

        @block.tensor
        def _(pe):
            def layer_norm(b, j, source_done, source):
                pe.wait_ge(source_done.sem, source_done.at(b, CHUNKS))
                work.wait_free(pe, b, f"mean{j}")
                for c in range(CHUNKS):
                    last = nc.tensor.matmul(work.tile(f"mean{j}")[:], mean_mat[:], source[:, c, :],
                                            start=(c == 0), stop=(c == CHUNKS - 1))
                work.filled(last, f"mean{j}")
                pe.wait_ge(sq_done.sem, sq_done.at(b, j + 1))
                work.wait_free(pe, b, f"var{j}")
                for c in range(CHUNKS):
                    last = nc.tensor.matmul(work.tile(f"var{j}")[:], mean_mat[:], sq[:, c, :],
                                            start=(c == 0), stop=(c == CHUNKS - 1))
                work.filled(last, f"var{j}")

            def project(b, name, weights, source, cols, rows=P):
                work.wait_free(pe, b, name)
                n = weights.shape[1]
                for c in range(n):
                    last = nc.tensor.matmul(work.tile(name)[0:rows, :], weights[:, c, cols[0]:cols[1]], source[:, c, :],
                                            start=(c == 0), stop=(c == n - 1))
                work.filled(last, name)

            def spread(b, g):
                for name, _, n in wide_order(g):
                    is_b = int(name[4:]) % (2 * GROUP) < GROUP
                    row = n if is_b else STATES + n
                    work.wait_free(pe, b, name)
                    work.filled(nc.tensor.matmul(work.tile(name)[:], picks[0:96, row, :], bc_parts[0:96, :],
                                                 start=True, stop=True), name)

            with pe.Fori(0, BATCH) as b:
                pe.wait_ge(x_loaded.sem, x_loaded.at(b, 1))
                for c in range(CHUNKS):
                    work.wait_free(pe, b, f"xT{c}")
                    for t in range(TILES):
                        last = nc.tensor.transpose(work.tile(f"xT{c}")[:, t * P:(t + 1) * P],
                                                   xt[:, t, c * P:(c + 1) * P], ident[:])
                    work.filled(last, f"xT{c}")
                layer_norm(b, 0, x_t_done, x_t)
                pe.wait_ge(h_done.sem, h_done.at(b, CHUNKS))
                for m in range(8):
                    project(b, f"xz{m}", w_in_t, h_t, (m * P, (m + 1) * P))
                pe.wait_ge(xs_done.sem, xs_done.at(b, INNER_CHUNKS))
                for m in range(4):
                    project(b, f"dt{m}", w_dt_t, xs, (m * P, (m + 1) * P))
                project(b, "bc", w_bc_t, xs, (0, 2 * STATES), rows=2 * STATES)
                pe.wait_ge(parts_done.sem, parts_done.at(b, 5))
                spread(b, 0)
                pe.wait_ge(gated_done.sem, gated_done.at(b))
                for q in range(UNITS):
                    g, d = divmod(q, INNER_CHUNKS)
                    if d == 1 and g + 1 < GROUPS:
                        spread(b, g + 1)
                    cmul_wait(pe, b, q)
                    for j in range(GROUP):
                        last = nc.tensor.matmul(y_sum[d][:], ident[:], state[q % 4][:, j, :],
                                                start=(g == 0 and j == 0), stop=(g == GROUPS - 1 and j == GROUP - 1))
                    last.then_inc(sum_done.sem, 1)
                pe.wait_ge(gated_done.sem, gated_done.at(b, INNER_CHUNKS))
                for m in range(CHUNKS):
                    project(b, f"out{m}", w_out_t, yv, (m * P, (m + 1) * P))
                layer_norm(b, 1, x1_done, x1_t)

        @block.scalar
        def _(act):
            def layer_norm(b, j, shift, scale):
                act.wait_ge(xc_done.sem, xc_done.at(b, CHUNKS * (j + 1)))
                nc.scalar.activation(sq[:], xc[:], ACT.Square).then_inc(sq_done.sem, 1)
                work.wait_full(act, b, f"var{j}")
                nc.scalar.activation(lnv[:], work.tile(f"var{j}")[:], ACT.Ln, bias=ln_eps[:]).then_inc(lnv_done.sem, 1)
                act.wait_ge(lnv_done.sem, lnv_done.at(b, j + 1))
                nc.scalar.activation(rstd[:], lnv[:], ACT.Exp, scale=-0.5).then_inc(rstd_done.sem, 1)
                act.wait_ge(xn_done.sem, xn_done.at(b, j + 1))
                if j == 0:
                    act.wait_ge(stored.sem, stored.at(b))
                for c in range(CHUNKS):
                    nc.scalar.activation(h_t[:, c, :], xc[:, c, :], ACT.Identity,
                                         bias=mod[:, 2 * shift + c, bass.ds(b, 1)],
                                         scale=mod[:, 2 * scale + c, bass.ds(b, 1)]).then_inc(h_done.sem, 1)

            def spread(b, g):
                if g >= 2:
                    act.wait_ge(input_done.sem, input_done.at(b, INNER_CHUNKS * (g - 1)))
                    act.wait_ge(sum_done.sem, sum_done.at(b, INNER_CHUNKS * (g - 1)))
                for name, is_b, n in wide_order(g):
                    work.wait_full(act, b, name)
                    to, done = (b_wide, b_wide_done) if is_b else (c_wide, c_wide_done)
                    nc.scalar.activation(to[g % 2][:, n % GROUP, :], work.tile(name)[:], ACT.Copy).then_inc(done.sem, 1)

            nc.scalar.preload_act_table_set(EXP_AND_LN)
            with act.Fori(0, BATCH) as b:
                act.wait_ge(x1_done.sem, x1_done.at(b))
                for c in range(CHUNKS):
                    work.wait_full(act, b, f"xT{c}")
                    nc.scalar.activation(x_t[:, c, :], work.tile(f"xT{c}")[:], ACT.Copy).then_inc(x_t_done.sem, 1)
                layer_norm(b, 0, MOD_SHIFT_A, MOD_SCALE_A)
                act.wait_ge(gated_done.sem, gated_done.at(b))
                for m in range(4):
                    work.wait_full(act, b, f"xz{m}")
                    nc.scalar.activation(xs[:, m, :], work.tile(f"xz{m}")[:], ACT.Copy).then_inc(xs_done.sem, 1)
                for m in range(4):
                    work.wait_full(act, b, f"xz{4 + m}")
                    nc.scalar.activation(sz[:, m, :], work.tile(f"xz{4 + m}")[:], ACT.Silu).then_inc(sz_done.sem, 1)
                nc.scalar.preload_act_table_set(EXP_AND_LN)
                for h in range(2):
                    act.wait_ge(u_done.sem, u_done.at(b, h))
                    for m in range(2):
                        name = f"dt{2 * h + m}"
                        work.wait_full(act, b, name)
                        nc.scalar.activation(sp_relu[:, m, :], work.tile(name)[:], ACT.Relu,
                                             bias=b_dt[:, 2 * h + m:2 * h + m + 1])
                        nc.scalar.activation(sp_e[:, m, :], work.tile(name)[:], ACT.Abs,
                                                        bias=b_dt[:, 2 * h + m:2 * h + m + 1]).then_inc(abs_done.sem, 1)
                    act.wait_ge(abs_done.sem, abs_done.at(b, 2 * h + 2))
                    nc.scalar.activation(sp_e[:], sp_e[:], ACT.Exp, scale=-1.0).then_inc(exp_done.sem, 1)
                    act.wait_ge(exp_done.sem, exp_done.at(b, h + 1))
                    nc.scalar.activation(sp_ln[:], sp_e[:], ACT.Ln, bias=1.0).then_inc(ln_done.sem, 1)
                spread(b, 0)
                for q in range(UNITS):
                    g, d = divmod(q, INNER_CHUNKS)
                    if d == 2 and g + 1 < GROUPS:
                        spread(b, g + 1)
                    if g == 0 and d % 2 == 0:
                        act.wait_ge(dt_done.sem, dt_done.at(b, d // 2 + 1))
                    act.wait_ge(scan_done.sem, scan_done.at(b, max(q - 1, 0)))
                    for j in range(GROUP):
                        n = GROUP * g + j
                        last = nc.scalar.activation(decay[q % 2][:, j, 1:SEQ], dt[:, d, 1:SEQ], ACT.Exp,
                                                    scale=neg_a[:, d, n:n + 1])
                    last.then_inc(decay_done.sem, 1)
                layer_norm(b, 1, MOD_SHIFT_B, MOD_SCALE_B)

        @block.vector
        def _(dve):
            def layer_norm(b, j, source):
                if j == 1:
                    dve.wait_ge(h_done.sem, h_done.at(b, CHUNKS))
                else:
                    dve.wait_ge(h_done.sem, h_done.at(b))
                work.wait_full(dve, b, f"mean{j}")
                for c in range(CHUNKS):
                    nc.vector.tensor_tensor(xc[:, c, :], source[:, c, :], work.tile(f"mean{j}")[:],
                                            ALU.subtract).then_inc(xc_done.sem, 1)
                dve.wait_ge(rstd_done.sem, rstd_done.at(b, j + 1))
                dve.wait_ge(sq_done.sem, sq_done.at(b, j + 1))
                nc.vector.tensor_tensor(xc[:], xc[:], rstd[:].unsqueeze(1).to_broadcast([P, CHUNKS, SEQ]),
                                        ALU.mult).then_inc(xn_done.sem, 1)

            for d in decay:
                nc.vector.memset(d[:, :, 0:1], 0.0)
            with dve.Fori(0, BATCH) as b:
                layer_norm(b, 0, x_t)
                work.wait_full(dve, b, "bc")
                bc = work.tile("bc")[0:2 * STATES, :]
                nc.vector.tensor_copy(bc_parts[0:32, :], bc).then_inc(parts_done.sem, 1)
                dve.wait_ge(parts_done.sem, parts_done.at(b, 1))
                nc.vector.tensor_tensor(bc_rest[:], bc, bc_parts[0:32, :], ALU.subtract).then_inc(parts_done.sem, 1)
                dve.wait_ge(parts_done.sem, parts_done.at(b, 2))
                nc.vector.tensor_copy(bc_mid[:], bc_rest[:]).then_inc(parts_done.sem, 1)
                nc.vector.tensor_copy(bc_parts[32:64, :], bc_rest[:]).then_inc(parts_done.sem, 1)
                dve.wait_ge(parts_done.sem, parts_done.at(b, 3))
                nc.vector.tensor_tensor(bc_parts[64:96, :], bc_rest[:], bc_mid[:],
                                        ALU.subtract).then_inc(parts_done.sem, 1)
                for h in range(2):
                    part = slice(2 * h, 2 * h + 2)

                    def step(k):
                        dve.wait_ge(series_done.sem, series_done.at(b, 6 * h + k))

                    dve.wait_ge(exp_done.sem, exp_done.at(b, h + 1))
                    nc.vector.tensor_scalar(sp_mask[:], sp_e[:], SERIES_BELOW, None, ALU.is_gt).then_inc(series_done.sem, 1)
                    nc.vector.tensor_scalar(sp_p[:], sp_e[:], -0.25, 1.0 / 3, ALU.mult, ALU.add).then_inc(series_done.sem, 1)
                    step(2)
                    nc.vector.tensor_tensor(sp_p[:], sp_p[:], sp_e[:], ALU.mult).then_inc(series_done.sem, 1)
                    step(3)
                    nc.vector.scalar_tensor_tensor(sp_p[:], sp_p[:], -0.5, sp_e[:], ALU.add, ALU.mult).then_inc(series_done.sem, 1)
                    step(4)
                    nc.vector.scalar_tensor_tensor(sp_p[:], sp_p[:], 1.0, sp_e[:], ALU.add, ALU.mult).then_inc(series_done.sem, 1)
                    step(5)
                    dve.wait_ge(ln_done.sem, ln_done.at(b, h + 1))
                    nc.vector.memset(waiter[:, h:h + 1], 0.0)
                    nc.vector.copy_predicated(sp_p[:], sp_mask[:], sp_ln[:]).then_inc(series_done.sem, 1)
                    step(6)
                    nc.vector.tensor_tensor(dt[:, part, :], sp_p[:], sp_relu[:], ALU.add).then_inc(dt_done.sem, 1)
                    dve.wait_ge(dt_done.sem, dt_done.at(b, h + 1))
                    dve.wait_ge(xs_done.sem, xs_done.at(b, INNER_CHUNKS))
                    nc.vector.tensor_tensor(u[:, part, :], dt[:, part, :], xs[:, part, :], ALU.mult).then_inc(u_done.sem, 1)

                def scan_input(q):
                    g, d = divmod(q, INNER_CHUNKS)
                    dve.wait_ge(u_done.sem, u_done.at(b, 2))
                    dve.wait_ge(b_wide_done.sem, b_wide_done.at(b, GROUP * (g + 1)))
                    dve.wait_ge(sum_done.sem, sum_done.at(b, max(q - 3, 0)))
                    nc.vector.tensor_tensor(state[q % 4][:], u[:, d, :].unsqueeze(1).to_broadcast([P, GROUP, SEQ]),
                                            b_wide[g % 2][:], ALU.mult).then_inc(input_done.sem, 1)

                scan_input(0)
                for q in range(UNITS):
                    g, d = divmod(q, INNER_CHUNKS)
                    if q + 1 < UNITS:
                        scan_input(q + 1)
                    dve.wait_ge(decay_done.sem, decay_done.at(b, q + 1))
                    dve.wait_ge(input_done.sem, input_done.at(b, q + 1))
                    flat = state[q % 4][:].rearrange("p g s -> p (g s)")
                    nc.vector.tensor_tensor_scan(flat, decay[q % 2][:].rearrange("p g s -> p (g s)"), flat, 0.0,
                                                 ALU.mult, ALU.add).then_inc(scan_done.sem, 1)
                    if q in on_vector:
                        dve.wait_ge(scan_done.sem, scan_done.at(b, q + 1))
                        dve.wait_ge(c_wide_done.sem, c_wide_done.at(b, GROUP * (g + 1)))
                        nc.vector.tensor_tensor(state[q % 4][:], state[q % 4][:], c_wide[g % 2][:],
                                                ALU.mult).then_inc(cmul_vec_done.sem, 1)
                dve.wait_ge(sum_done.sem, sum_done.at(b, UNITS))
                dve.wait_ge(sz_done.sem, sz_done.at(b, INNER_CHUNKS))
                for d in range(INNER_CHUNKS):
                    nc.vector.scalar_tensor_tensor(yv[:, d, :], xs[:, d, :], skip_d[:, d:d + 1], y_sum[d][:],
                                                   ALU.mult, ALU.add).then_inc(skip_done.sem, 1)
                for d in range(INNER_CHUNKS):
                    dve.wait_ge(skip_done.sem, skip_done.at(b, d + 1))
                    nc.vector.tensor_tensor(yv[:, d, :], yv[:, d, :], sz[:, d, :], ALU.mult).then_inc(gated_done.sem, 1)
                dve.wait_ge(stored.sem, stored.at(b))
                for c in range(CHUNKS):
                    work.wait_full(dve, b, f"out{c}")
                    nc.vector.scalar_tensor_tensor(x1_t[:, c, :], work.tile(f"out{c}")[:],
                                                              mod[:, 2 * MOD_GATE_A + c, bass.ds(b, 1)], x_t[:, c, :],
                                                              ALU.mult, ALU.add).then_inc(x1_done.sem, 1)
                layer_norm(b, 1, x1_t)

        @block.gpsimd
        def _(pool):
            with pool.Fori(0, BATCH) as b:
                for q in on_pool:
                    g = q // INNER_CHUNKS
                    pool.wait_ge(c_wide_done.sem, c_wide_done.at(b, GROUP * (g + 1)))
                    pool.wait_ge(scan_done.sem, scan_done.at(b, q + 1))
                    nc.gpsimd.tensor_tensor(state[q % 4][:], state[q % 4][:], c_wide[g % 2][:],
                                            ALU.mult).then_inc(cmul_pool_done.sem, 1)


STAGE = {"raw": 1, "turn": 1, "norm": 1, "kt": 1, "v": 1, "ssq": 1, "rate": 1,
         "score": 2, "mask": 2, "exp": 2, "pt": 2, "att": 2, "onorm": 2, "ot": 2,
         "wo": 3, "mean": 3, "sq": 3, "var": 3, "xn": 3, "hn": 3, "ga": 3, "wd": 3}
LEAD = {1: 1, 2: 0, 3: -1}
ORDER = """
wo:0 score:0 mask:0 exp:0 wo:1 mean:0 score:1 mask:1 sq:0 raw:0 pt:0.0 raw:1 pt:0.1 var:0 turn:0 norm:0 att:0 xn:0 exp:1
raw:2 onorm:0 score:2 mask:2 hn:0 turn:1 norm:1 kt:0 ot:0
pt:1.0 raw:3 pt:1.1 turn:2 norm:2 kt:1 pt:1.2 raw:4 pt:1.3 turn:3 norm:3 kt:2 att:1 exp:2 onorm:1 score:3 mask:3 raw:5 ot:1 kt:3
turn:4 exp:3
pt:2.0 ga:0 pt:2.1 raw:6 pt:2.2 ga:1 pt:2.3 turn:5 att:2 ga:2 onorm:2 raw:7
pt:3.0 ga:3 ot:2 pt:3.1 turn:6 pt:3.2 ga:4 pt:3.3 v:0 att:3 turn:7 ga:5 onorm:3 v:1 ssq:0 v:2 ot:3 wd:0 v:3 wd:1 rate:0
"""
SCHEDULE = [(name, *map(int, at.split("."))) for name, _, at in (step.partition(":") for step in ORDER.split())]


def stack_pass(nc, inp, stack_dram):
    SEQS = DEPTH * BATCH
    with ExitStack() as ctx:
        def sb(name, shape, dt=F32):
            return ctx.enter_context(nc.sbuf_tensor("b_" + name, shape, dt))

        def sem(name):
            return ctx.enter_context(nc.semaphore("b_" + name))

        signals = []

        def signal(name, per_pass, unit=1):
            signals.append(Signal(sem(name), per_pass, unit))
            return signals[-1]

        banks_all = [ctx.enter_context(nc.psum_tensor(f"b_bank{i}", [P, 512], F32)) for i in range(8)]
        s_banks, o_bank = banks_all[4:6], banks_all[7]

        squares = sb("squares", [P, 6, P])
        ident, mean_mat, head_ones, turn = (squares[:, i, :] for i in range(4))
        mask = squares[:, 4:6, :].rearrange("p a b -> p (a b)")
        pair_ones = sb("pair_ones", [P, 2])
        w_qkv = sb("w_qkv", [P, CHUNKS, 3 * INNER])
        w_o = sb("w_o", [P, PAIRS, DIM])
        w_1 = sb("w_1", [P, CHUNKS, 2 * HID])
        w_2 = sb("w_2", [P, HID_CHUNKS, DIM])
        rotary = sb("rotary", [P, 4, SEQ])
        qk_scale = sb("qk_scale", [P, SEQS, 2])
        ln_g = sb("ln_g", [P, SEQS, CHUNKS])
        ln_b = sb("ln_b", [P, SEQS, CHUNKS])
        b_1a = sb("b_1a", [P, SEQS, HID_CHUNKS])
        b_1g = sb("b_1g", [P, SEQS, HID_CHUNKS])
        b_2 = sb("b_2", [P, SEQS, CHUNKS])
        eps_bias = sb("eps_bias", [P, 1])
        k_bias = sb("k_bias", [P, 1])
        q_bias = sb("q_bias", [P, 1])
        waiter = sb("waiter", [P, TILES * PAIRS])

        hx = sb("hx", [P, CHUNKS, SEQ + 1])
        raw = [sb(f"raw{i}", [P, SEQ]) for i in range(2)]
        raw_sq = [sb(f"raw_sq{i}", [P, SEQ]) for i in range(4)]
        by_cos = [sb(f"by_cos{i}", [P, SEQ]) for i in range(2)]
        by_sin = [sb(f"by_sin{i}", [P, SEQ]) for i in range(2)]
        k_norm = [sb(f"k_norm{i}", [P, SEQ]) for i in range(2)]
        q_t = [sb(f"q_t{i}", [P, PAIRS, SEQ]) for i in range(2)]
        k_t = [sb(f"k_t{i}", [P, PAIRS, SEQ]) for i in range(2)]
        v = [sb(f"v{i}", [P, TILES, INNER]) for i in range(2)]
        q_rate = [sb(f"q_rate{i}", [P, TILES, HEADS]) for i in range(2)]
        scores = [sb(f"scores{i}", [P, HEADS, 2 * WINDOW]) for i in range(2)]
        probs_t = [sb(f"probs_t{i}", [P, 2 * HEADS, WINDOW]) for i in range(2)]
        row_max = sb("row_max", [P, TILES, HEADS])
        row_bias = sb("row_bias", [P, TILES, HEADS])
        row_sum = sb("row_sum", [P, TILES, HEADS])
        row_rate = sb("row_rate", [P, TILES, HEADS])
        o = [sb(f"o{i}", [P, INNER]) for i in range(2)]
        o_t = sb("o_t", [P, PAIRS, SEQ])
        x_res = sb("x_res", [P, CHUNKS, SEQ])
        x2 = sb("x2", [P, CHUNKS, SEQ + 1])
        xc = sb("xc", [P, CHUNKS, SEQ])
        rstd = sb("rstd", [P, SEQ])
        hn = sb("hn", [P, CHUNKS, SEQ])
        gelu = [sb(f"gelu{i}", [P, SEQ]) for i in range(2)]
        h2 = sb("h2", [P, HID_CHUNKS, SEQ])
        sq = h2[:, 0:CHUNKS, :]
        x_out = sb("x_out", [P, CHUNKS, SEQ])

        def shifted(x, c):
            return x[:, c, 0:SEQ]

        def plain(x, c):
            return x[:, c, c:c + SEQ]

        def hid_rows(m):
            return min(P, HID - m * P)

        hx_loaded = signal("hx_loaded", CHUNKS, 16)
        raw_done = signal("raw_done", 8)
        raw_sq_done = signal("raw_sq_done", 8)
        by_cos_done = signal("by_cos_done", 8)
        by_sin_done = signal("by_sin_done", 8)
        turned_done = signal("turned_done", 8)
        k_floor_done = signal("k_floor_done", PAIRS)
        k_ln_done = signal("k_ln_done", PAIRS)
        k_norm_done = signal("k_norm_done", PAIRS)
        k_done = signal("k_done", PAIRS)
        q_floor_done = signal("q_floor_done", 1)
        q_ln_done = signal("q_ln_done", 1)
        q_rate_done = signal("q_rate_done", 1)
        v_done = signal("v_done", TILES)
        masked_done = signal("masked_done", TILES * PAIRS)
        row_bias_done = signal("row_bias_done", TILES)
        probs_done = signal("probs_done", TILES * PAIRS)
        row_rate_done = signal("row_rate_done", TILES)
        o_done = signal("o_done", TILES)
        o_t_done = signal("o_t_done", TILES)
        turn_uses = [(w, i) for w in range(TILES) for i in range(4 if w else 2)]
        on_act = [x for n, x in enumerate(turn_uses) if n % 2 == 0]
        on_dve = [x for n, x in enumerate(turn_uses) if n % 2 == 1]
        probs_t_act = signal("probs_t_act", len(on_act))
        probs_t_dve = signal("probs_t_dve", len(on_dve))
        x_res_loaded = signal("x_res_loaded", 1, 16)
        x2_done = signal("x2_done", CHUNKS)
        xc_done = signal("xc_done", CHUNKS)
        sq_done = signal("sq_done", 1)
        ln_done = signal("ln_done", 1)
        rstd_done = signal("rstd_done", 1)
        xn_done = signal("xn_done", 1)
        hn_done = signal("hn_done", CHUNKS)
        gelu_done = signal("gelu_done", HID_CHUNKS)
        h2_done = signal("h2_done", HID_CHUNKS)
        x_out_done = signal("x_out_done", CHUNKS)
        stored = signal("stored", 1, 16)
        const_loaded, qkv_loaded, mlp_loaded = sem("const_loaded"), sem("qkv_loaded"), sem("mlp_loaded")

        def probs_t_signal(w, i):
            return (probs_t_act, on_act.index((w, i)) + 1) if (w, i) in on_act else (probs_t_dve, on_dve.index((w, i)) + 1)

        def probs_t_until(w):
            return (sum(1 for x in on_act if x[0] <= w), sum(1 for x in on_dve if x[0] <= w))

        uses, dense = [], {1: 0, 3: 2}

        def use_dense(stage, name, reader, k):
            uses.append((name, dense[stage], reader, k))
            dense[stage] ^= 1

        for name, k, *i in SCHEDULE:
            if name == "raw":
                use_dense(1, f"raw{k}", raw_done, k + 1)
            elif name == "turn":
                use_dense(1, f"rot{k}", by_sin_done, k + 1)
                if k < PAIRS:
                    use_dense(1, f"ss{k}", k_floor_done, k + 1)
            elif name == "ssq":
                use_dense(1, "ssq", q_floor_done, 1)
            elif name == "v":
                use_dense(1, f"v{k}", v_done, k + 1)
            elif name == "wo":
                use_dense(3, f"wo{k}", x2_done, k + 1)
            elif name == "mean":
                use_dense(3, "mean", xc_done, CHUNKS)
            elif name == "var":
                use_dense(3, "var", ln_done, 1)
            elif name == "ga":
                use_dense(3, f"g{k}", gelu_done, k + 1)
                use_dense(3, f"a{k}", h2_done, k + 1)
            elif name == "wd":
                use_dense(3, f"wd{k}", x_out_done, k + 1)
            elif name == "score":
                for g in range(2):
                    uses += [(f"s{k}_{g}_{h}", 4 + h, masked_done, PAIRS * k + 2 * g + h + 1) for h in range(2)]
            elif name == "pt":
                uses.append((f"pt{k}_{i[0]}", 6, *probs_t_signal(k, i[0])))
            elif name == "ot":
                uses.append((f"ot{k}", 6, o_t_done, k + 1))
            elif name == "att":
                uses.append((f"o{k}", 7, o_done, k + 1))
        psum = Banks(banks_all, [sem(f"full{i}") for i in range(8)], uses)

        def blocks_of(w, i):
            return [(2 * i + h, blk) for h in range(2) for blk in range(2)] if w else [(4 * i + h, 1) for h in range(4)]

        def keys_of(w):
            return (0, 2 * WINDOW) if w else (WINDOW, 2 * WINDOW)

        def pipeline(eng, steps):
            def one_pass(i, parity, stages):
                for name, *at in SCHEDULE:
                    lead = LEAD[STAGE[name]]
                    if STAGE[name] in stages and name in steps:
                        steps[name](i + lead, (parity + lead) % 2, *at)

            one_pass(-1, 1, (1,))
            one_pass(0, 0, (1, 2))
            with eng.Fori(0, SEQS // 2 - 1) as j:
                one_pass(2 * j + 1, 1, (1, 2, 3))
                one_pass(2 * j + 2, 0, (1, 2, 3))
            one_pass(SEQS - 1, 1, (2, 3))
            one_pass(SEQS, 0, (3,))

        load_stack_vectors(nc, inp, squares, pair_ones, rotary, qk_scale, ln_g, ln_b, b_1a, b_1g, b_2)
        with nc.Block() as block:
            @block.vector
            def _(dve):
                nc.vector.memset(eps_bias[:], LN_EPS)
                nc.vector.memset(k_bias[:], 0.5 * float(np.log(SCREEN)))
                nc.vector.memset(q_bias[:], 0.5 * float(np.log(SCREEN)) + float(np.log(QK_SCALE)))
                nc.vector.memset(hx[:, 1, 0:1], 0.0)
                nc.vector.memset(x2[:, 1, 0:1], 0.0)
                nc.vector.memset(row_sum[:], 0.0)

        start_signals(nc, signals)
        block = ctx.enter_context(nc.Block())

        @block.sync
        def _(sp):
            def load_qkv(l):
                sp.dma_start(w_qkv[:], inp["L0_ffn_wqkv"][l].rearrange("(c p) f -> p c f", p=P)).then_inc(qkv_loaded, 16)
                sp.wait_ge(qkv_loaded, 16 * (l + 1))

            def load_mlp(l):
                whole = HID // P
                sp.dma_start(w_o[:], inp["L0_ffn_wo"][l].rearrange("(c p) f -> p c f", p=P)).then_inc(mlp_loaded, 16)
                sp.dma_start(w_1[:], inp["L0_ffn_w1"][l].rearrange("(c p) f -> p c f", p=P)).then_inc(mlp_loaded, 16)
                sp.dma_start(w_2[:, 0:whole, :], inp["L0_ffn_w2"][l, 0:whole * P].rearrange("(c p) f -> p c f", p=P))\
                    .then_inc(mlp_loaded, 16)
                sp.dma_start(w_2[0:HID - whole * P, whole, :], inp["L0_ffn_w2"][l, whole * P:HID]).then_inc(mlp_loaded, 16)
                sp.wait_ge(mlp_loaded, 16 * 4 * (l + 1))

            def load_hx(s):
                sp.wait_ge(v_done.sem, v_done.at(s))
                for c in range(CHUNKS):
                    sp.dma_start(plain(hx, c), stack_dram[s, :, c, :]).then_inc(hx_loaded.sem, 16)

            def load_res(s):
                sp.wait_ge(x2_done.sem, x2_done.at(s))
                sp.dma_start(x_res[:], stack_dram[s]).then_inc(x_res_loaded.sem, 16)

            def store(s):
                sp.wait_ge(x_out_done.sem, x_out_done.at(s, CHUNKS))
                sp.dma_start(stack_dram[s + BATCH], x_out[:]).then_inc(stored.sem, 16)

            load_qkv(0)
            load_hx(0)
            load_mlp(0)
            load_hx(1)
            load_res(0)
            load_hx(2)
            with sp.Fori(1, BATCH - 2) as i:
                load_res(i)
                load_hx(i + 2)
                store(i - 1)
            load_res(BATCH - 2)
            sp.wait_ge(v_done.sem, v_done.at(BATCH))
            load_qkv(1)
            sp.wait_ge(stored.sem, stored.at(1))
            load_hx(BATCH)
            store(BATCH - 3)
            load_res(BATCH - 1)
            sp.wait_ge(stored.sem, stored.at(2))
            load_hx(BATCH + 1)
            store(BATCH - 2)
            sp.wait_ge(stored.sem, stored.at(3))
            load_hx(BATCH + 2)
            store(BATCH - 1)
            load_mlp(1)
            load_res(BATCH)
            with sp.Fori(BATCH + 1, SEQS - 2) as i:
                load_res(i)
                sp.wait_ge(stored.sem, stored.at(i + 3 - BATCH))
                load_hx(i + 2)
                store(i - 1)
            for i in range(SEQS - 2, SEQS):
                load_res(i)
                store(i - 1)
            store(SEQS - 1)
            sp.wait_ge(stored.sem, stored.at(SEQS))

        @block.tensor
        def _(pe):
            def product(s, name, weights, cols, sources, rows=P):
                psum.wait_free(pe, s, name)
                for c, source in enumerate(sources):
                    last = nc.tensor.matmul(psum.tile(name)[0:rows, :], weights[0:source.shape[0], c, cols:cols + rows], source,
                                            start=(c == 0), stop=(c == len(sources) - 1))
                psum.filled(last, name)

            def raw_pair(s, slot, r):
                if r == 0:
                    pe.wait_ge(hx_loaded.sem, hx_loaded.at(s, CHUNKS))
                product(s, f"raw{r}", w_qkv, INNER + r * P if r < PAIRS else (r - PAIRS) * P,
                        [shifted(hx, c) for c in range(CHUNKS)])

            def turn_pair(s, slot, r):
                pe.wait_ge(raw_done.sem, raw_done.at(s, r + 1))
                psum.wait_free(pe, s, f"rot{r}")
                psum.filled(nc.tensor.matmul(psum.tile(f"rot{r}")[:], turn, raw[r % 2][:], start=True, stop=True), f"rot{r}")
                if r < PAIRS:
                    pe.wait_ge(raw_sq_done.sem, raw_sq_done.at(s, r + 1))
                    psum.wait_free(pe, s, f"ss{r}")
                    psum.filled(nc.tensor.matmul(psum.tile(f"ss{r}")[:], head_ones, raw_sq[r % 4][:], start=True, stop=True),
                                f"ss{r}")

            def q_norms(s, slot, _):
                pe.wait_ge(raw_sq_done.sem, raw_sq_done.at(s, 8))
                psum.wait_free(pe, s, "ssq")
                for p in range(PAIRS):
                    for w in range(TILES):
                        at = w * HEADS + 2 * p
                        last = nc.tensor.matmul(psum.tile("ssq")[:, at:at + 2], raw_sq[p][:, w * WINDOW:(w + 1) * WINDOW],
                                                pair_ones[:], start=True, stop=True)
                psum.filled(last, "ssq")

            def values(s, slot, t):
                psum.wait_free(pe, s, f"v{t}")
                for c in range(CHUNKS):
                    last = nc.tensor.matmul(psum.tile(f"v{t}")[:], hx[:, c, t * P:(t + 1) * P],
                                            w_qkv[:, c, 2 * INNER:3 * INNER], start=(c == 0), stop=(c == CHUNKS - 1))
                psum.filled(last, f"v{t}")

            def score(s, slot, w):
                lo, hi = keys_of(w)
                if w == 0:
                    pe.wait_ge(k_done.sem, k_done.at(s, PAIRS))
                    pe.wait_ge(turned_done.sem, turned_done.at(s, 8))
                first = w * WINDOW - (WINDOW - lo)
                for g in range(2):
                    for h in range(2):
                        psum.wait_free(pe, s, f"s{w}_{g}_{h}")
                    for n in range(2):
                        for h in range(2):
                            at, p = slice(h * DIM_HEAD, (h + 1) * DIM_HEAD), 2 * g + n
                            last = nc.tensor.matmul(s_banks[h][:, n * 2 * WINDOW + lo:n * 2 * WINDOW + hi],
                                                    q_t[slot][at, p, w * WINDOW:(w + 1) * WINDOW],
                                                    k_t[slot][at, p, first:first + hi - lo], start=True, stop=True)
                            if n:
                                psum.filled(last, f"s{w}_{g}_{h}")

            def turn_probs(s, slot, w, i):
                name, blocks = f"pt{w}_{i}", blocks_of(w, i)
                psum.wait_free(pe, s, name)
                pe.wait_ge(probs_done.sem, probs_done.at(s, PAIRS * w + blocks[-1][0] // 2 + 1))
                for n, (h, blk) in enumerate(blocks):
                    last = nc.tensor.transpose(psum.tile(name)[:, n * P:(n + 1) * P],
                                               scores[w % 2][:, h, blk * WINDOW:(blk + 1) * WINDOW], ident)
                psum.filled(last, name)

            def attend(s, slot, w):
                by_act, by_dve = probs_t_until(w)
                pe.wait_ge(probs_t_act.sem, probs_t_act.at(s, by_act))
                pe.wait_ge(probs_t_dve.sem, probs_t_dve.at(s, by_dve))
                if w == 0:
                    pe.wait_ge(v_done.sem, v_done.at(s, TILES))
                psum.wait_free(pe, s, f"o{w}")
                for h in range(HEADS):
                    blocks = (0, 1) if w else (1,)
                    for blk in blocks:
                        last = nc.tensor.matmul(o_bank[:, h * DIM_HEAD:(h + 1) * DIM_HEAD], probs_t[w % 2][:, 2 * h + blk, :],
                                                v[slot][:, w - 1 + blk, h * DIM_HEAD:(h + 1) * DIM_HEAD],
                                                start=(blk == blocks[0]), stop=(blk == 1))
                psum.filled(last, f"o{w}")

            def turn_output(s, slot, w):
                pe.wait_ge(o_done.sem, o_done.at(s, w + 1))
                psum.wait_free(pe, s, f"ot{w}")
                for p in range(PAIRS):
                    last = nc.tensor.transpose(psum.tile(f"ot{w}")[:, p * P:(p + 1) * P], o[w % 2][:, p * P:(p + 1) * P], ident)
                psum.filled(last, f"ot{w}")

            def project_out(s, slot, m):
                if m == 0:
                    pe.wait_ge(o_t_done.sem, o_t_done.at(s, TILES))
                    pe.wait_ge(x_res_loaded.sem, x_res_loaded.at(s, 1))
                product(s, f"wo{m}", w_o, m * P, [o_t[:, p, :] for p in range(PAIRS)])

            def mean(s, slot, _):
                pe.wait_ge(x2_done.sem, x2_done.at(s, CHUNKS))
                psum.wait_free(pe, s, "mean")
                for c in range(CHUNKS):
                    last = nc.tensor.matmul(psum.tile("mean")[:], mean_mat, shifted(x2, c), start=(c == 0), stop=(c == CHUNKS - 1))
                psum.filled(last, "mean")

            def var(s, slot, _):
                pe.wait_ge(sq_done.sem, sq_done.at(s, 1))
                psum.wait_free(pe, s, "var")
                for c in range(CHUNKS):
                    last = nc.tensor.matmul(psum.tile("var")[:], mean_mat, sq[:, c, :], start=(c == 0), stop=(c == CHUNKS - 1))
                psum.filled(last, "var")

            def gate_and_value(s, slot, m):
                if m == 0:
                    pe.wait_ge(hn_done.sem, hn_done.at(s, CHUNKS))
                for stem, at in (("g", HID), ("a", 0)):
                    product(s, f"{stem}{m}", w_1, at + m * P, [hn[:, c, :] for c in range(CHUNKS)], rows=hid_rows(m))

            def project_down(s, slot, m):
                if m == 0:
                    pe.wait_ge(h2_done.sem, h2_done.at(s, HID_CHUNKS))
                product(s, f"wd{m}", w_2, m * P, [h2[0:hid_rows(k), k, :] for k in range(HID_CHUNKS)])

            pipeline(pe, {"raw": raw_pair, "turn": turn_pair, "ssq": q_norms, "v": values, "score": score, "pt": turn_probs,
                          "att": attend, "ot": turn_output, "wo": project_out, "mean": mean, "var": var,
                          "ga": gate_and_value, "wd": project_down})

        @block.scalar
        def _(act):
            def from_pair(s, slot, r):
                act.wait_ge(by_cos_done.sem, by_cos_done.at(s, max(r - 1, 0)))
                act.wait_ge(by_sin_done.sem, by_sin_done.at(s, max(r - 1, 0)))
                if r < PAIRS:
                    act.wait_ge(q_floor_done.sem, q_floor_done.at(s))
                else:
                    act.wait_ge(k_floor_done.sem, k_floor_done.at(s, r - 3))
                psum.wait_full(act, s, f"raw{r}")
                nc.scalar.activation(raw_sq[r % 4][:], psum.tile(f"raw{r}")[:], ACT.Square).then_inc(raw_sq_done.sem, 1)
                nc.scalar.activation(raw[r % 2][:], psum.tile(f"raw{r}")[:], ACT.Identity,
                                     scale=qk_scale[:, bass.ds(s, 1), 1 if r < PAIRS else 0]).then_inc(raw_done.sem, 1)

            def norm_k(s, slot, r):
                x = k_norm[r % 2][:]
                act.wait_ge(k_floor_done.sem, k_floor_done.at(s, r + 1))
                nc.scalar.activation(x, x, ACT.Ln, scale=SCREEN).then_inc(k_ln_done.sem, 1)
                act.wait_ge(k_ln_done.sem, k_ln_done.at(s, r + 1))
                nc.scalar.activation(x, x, ACT.Exp, scale=-0.5, bias=k_bias[:]).then_inc(k_norm_done.sem, 1)

            def values(s, slot, t):
                psum.wait_full(act, s, f"v{t}")
                nc.scalar.activation(v[slot][:, t, :], psum.tile(f"v{t}")[:], ACT.Copy).then_inc(v_done.sem, 1)

            def rate_q(s, slot, _):
                x = q_rate[slot][:]
                act.wait_ge(q_floor_done.sem, q_floor_done.at(s, 1))
                nc.scalar.activation(x, x, ACT.Ln, scale=SCREEN).then_inc(q_ln_done.sem, 1)
                act.wait_ge(q_ln_done.sem, q_ln_done.at(s, 1))
                nc.scalar.activation(x, x, ACT.Exp, scale=-0.5, bias=q_bias[:]).then_inc(q_rate_done.sem, 1)

            def exponentials(s, slot, w):
                lo, hi = keys_of(w)
                act.wait_ge(row_bias_done.sem, row_bias_done.at(s, w + 1))
                for h in range(HEADS):
                    e = nc.scalar.activation(scores[w % 2][:, h, lo:hi], scores[w % 2][:, h, lo:hi], ACT.Exp,
                                             scale=q_rate[slot][:, w, h:h + 1], bias=row_bias[:, w, h:h + 1],
                                             accum_out=row_sum[:, w, h:h + 1])
                    if h % 2:
                        e.then_inc(probs_done.sem, 1)

            def copy_turned(s, slot, w, i):
                if (w, i) in on_act:
                    name = f"pt{w}_{i}"
                    psum.wait_full(act, s, name)
                    act.wait_ge(o_done.sem, o_done.at(s, max(w - 1, 0)))
                    to = probs_t[w % 2][:, 4 * i:4 * i + 4, :] if w else probs_t[0][:, 8 * i + 1:8 * i + 8:2, :]
                    nc.scalar.activation(to, psum.tile(name)[:].rearrange("p (n c) -> p n c", c=P), ACT.Copy)\
                        .then_inc(probs_t_act.sem, 1)

            def copy_output(s, slot, w):
                psum.wait_full(act, s, f"ot{w}")
                act.wait_ge(x2_done.sem, x2_done.at(s))
                nc.scalar.activation(o_t[:, :, w * WINDOW:(w + 1) * WINDOW],
                                     psum.tile(f"ot{w}")[:].rearrange("p (n c) -> p n c", c=P), ACT.Copy).then_inc(o_t_done.sem, 1)

            def square(s, slot, _):
                act.wait_ge(x_out_done.sem, x_out_done.at(s))
                act.wait_ge(xc_done.sem, xc_done.at(s, CHUNKS))
                nc.scalar.activation(sq, xc[:], ACT.Square).then_inc(sq_done.sem, 1)

            def deviation(s, slot, _):
                act.wait_ge(xn_done.sem, xn_done.at(s))
                psum.wait_full(act, s, "var")
                nc.scalar.activation(rstd[:], psum.tile("var")[:], ACT.Ln, bias=eps_bias[:]).then_inc(ln_done.sem, 1)
                act.wait_ge(ln_done.sem, ln_done.at(s, 1))
                nc.scalar.activation(rstd[:], rstd[:], ACT.Exp, scale=-0.5).then_inc(rstd_done.sem, 1)

            def affine(s, slot, _):
                act.wait_ge(h2_done.sem, h2_done.at(s))
                act.wait_ge(xn_done.sem, xn_done.at(s, 1))
                for c in range(CHUNKS):
                    nc.scalar.activation(hn[:, c, :], xc[:, c, :], ACT.Identity, scale=ln_g[:, bass.ds(s, 1), c],
                                         bias=ln_b[:, bass.ds(s, 1), c]).then_inc(hn_done.sem, 1)

            def gate(s, slot, m):
                rows = hid_rows(m)
                act.wait_ge(h2_done.sem, h2_done.at(s, max(m - 1, 0)))
                psum.wait_full(act, s, f"g{m}")
                nc.scalar.activation(gelu[m % 2][0:rows, :], psum.tile(f"g{m}")[0:rows, :], ACT.Gelu,
                                     bias=b_1g[0:rows, bass.ds(s, 1), m]).then_inc(gelu_done.sem, 1)
                if m == HID_CHUNKS - 1:
                    nc.scalar.preload_act_table_set(EXP_AND_LN)

            nc.scalar.preload_act_table_set(EXP_AND_LN)
            pipeline(act, {"raw": from_pair, "norm": norm_k, "v": values, "rate": rate_q, "exp": exponentials, "pt": copy_turned,
                           "ot": copy_output, "sq": square, "var": deviation, "hn": affine, "ga": gate})

        @block.gpsimd
        def _(pool):
            def times_cos(s, slot, r):
                pool.wait_ge(raw_done.sem, raw_done.at(s, r + 1))
                pool.wait_ge(turned_done.sem, turned_done.at(s, max(r - 1, 0)))
                nc.gpsimd.tensor_tensor(by_cos[r % 2][:], raw[r % 2][:], rotary[:, 2 if r < PAIRS else 0, :],
                                        ALU.mult).then_inc(by_cos_done.sem, 1)

            pipeline(pool, {"turn": times_cos})

        @block.vector
        def _(dve):
            def turn_pair(s, slot, r):
                at = r % 2
                dve.wait_ge(turned_done.sem, turned_done.at(s, max(r - 1, 0)))
                if 2 <= r < PAIRS + 2:
                    dve.wait_ge(k_done.sem, k_done.at(s, r - 1))
                psum.wait_full(dve, s, f"rot{r}")
                nc.vector.tensor_tensor(by_sin[at][:], psum.tile(f"rot{r}")[:], rotary[:, 3 if r < PAIRS else 1, :],
                                        ALU.mult).then_inc(by_sin_done.sem, 1)
                if r < PAIRS:
                    dve.wait_ge(k_done.sem, k_done.at(s, max(r - 1, 0)))
                    psum.wait_full(dve, s, f"ss{r}")
                    nc.vector.tensor_scalar(k_norm[at][:], psum.tile(f"ss{r}")[:], 1e-24, None, ALU.max).then_inc(k_floor_done.sem, 1)
                dve.wait_ge(by_cos_done.sem, by_cos_done.at(s, r + 1))
                dve.wait_ge(by_sin_done.sem, by_sin_done.at(s, r + 1))
                to = by_sin[at][:] if r < PAIRS else q_t[slot][:, r - PAIRS, :]
                nc.vector.tensor_tensor(to, by_cos[at][:], by_sin[at][:], ALU.add).then_inc(turned_done.sem, 1)

            def finish_k(s, slot, r):
                dve.wait_ge(k_norm_done.sem, k_norm_done.at(s, r + 1))
                dve.wait_ge(turned_done.sem, turned_done.at(s, r + 1))
                nc.vector.tensor_tensor(k_t[slot][:, r, :], by_sin[r % 2][:], k_norm[r % 2][:], ALU.mult).then_inc(k_done.sem, 1)

            def floor_q(s, slot, _):
                psum.wait_full(dve, s, "ssq")
                nc.vector.tensor_scalar(q_rate[slot][:].rearrange("p w h -> p (w h)"), psum.tile("ssq")[:, 0:TILES * HEADS],
                                        1e-24, None, ALU.max).then_inc(q_floor_done.sem, 1)

            def mask_scores(s, slot, w):
                lo, hi = keys_of(w)
                by_act, by_dve = probs_t_until(w - 2)
                dve.wait_ge(probs_t_act.sem, probs_t_act.at(s, by_act))
                dve.wait_ge(probs_t_dve.sem, probs_t_dve.at(s, by_dve))
                for g in range(2):
                    for h in range(2):
                        psum.wait_full(dve, s, f"s{w}_{g}_{h}")
                        n = 4 * w + 2 * g + h
                        nc.vector.memset(waiter[:, n:n + 1], 0.0)
                        for n in range(2):
                            at, head = n * 2 * WINDOW, 2 * (2 * g + n) + h
                            last = nc.vector.tensor_tensor_reduce(
                                out=scores[w % 2][:, head, lo:hi], in0=s_banks[h][:, at + lo:at + hi], in1=mask[:, lo:hi],
                                scale=1.0, scalar=MASKED, op0=ALU.add, op1=ALU.max, accum_out=row_max[:, w, head:head + 1])
                        last.then_inc(masked_done.sem, 1)
                dve.wait_ge(masked_done.sem, masked_done.at(s, PAIRS * (w + 1)))
                if w == 0:
                    dve.wait_ge(q_rate_done.sem, q_rate_done.at(s, 1))
                nc.vector.scalar_tensor_tensor(row_bias[:, w, :], row_max[:, w, :], -1.0, q_rate[slot][:, w, :],
                                               ALU.mult, ALU.mult).then_inc(row_bias_done.sem, 1)

            def copy_turned(s, slot, w, i):
                if (w, i) in on_dve:
                    psum.wait_full(dve, s, f"pt{w}_{i}")
                    to = probs_t[w % 2][:, 4 * i:4 * i + 4, :] if w else probs_t[0][:, 8 * i + 1:8 * i + 8:2, :]
                    nc.vector.tensor_copy(to, psum.tile(f"pt{w}_{i}")[:].rearrange("p (n c) -> p n c", c=P)).then_inc(probs_t_dve.sem, 1)

            def normalise(s, slot, w):
                dve.wait_ge(probs_done.sem, probs_done.at(s, PAIRS * (w + 1)))
                nc.vector.reciprocal(row_rate[:, w, :], row_sum[:, w, :]).then_inc(row_rate_done.sem, 1)
                dve.wait_ge(row_rate_done.sem, row_rate_done.at(s, w + 1))
                dve.wait_ge(o_t_done.sem, o_t_done.at(s, max(w - 1, 0)))
                psum.wait_full(dve, s, f"o{w}")
                nc.vector.tensor_tensor(o[w % 2][:].rearrange("p (h d) -> p h d", h=HEADS),
                                        o_bank[:].rearrange("p (h d) -> p h d", h=HEADS),
                                        row_rate[:, w, :].unsqueeze(2).to_broadcast([P, HEADS, DIM_HEAD]),
                                        ALU.mult).then_inc(o_done.sem, 1)

            def add_residual(s, slot, c):
                dve.wait_ge(x_res_loaded.sem, x_res_loaded.at(s, 1))
                psum.wait_full(dve, s, f"wo{c}")
                nc.vector.tensor_tensor(plain(x2, c), psum.tile(f"wo{c}")[:], x_res[:, c, :], ALU.add).then_inc(x2_done.sem, 1)

            def centre(s, slot, _):
                dve.wait_ge(x2_done.sem, x2_done.at(s, CHUNKS))
                dve.wait_ge(hn_done.sem, hn_done.at(s))
                psum.wait_full(dve, s, "mean")
                for c in range(CHUNKS):
                    nc.vector.tensor_tensor(xc[:, c, :], shifted(x2, c), psum.tile("mean")[:], ALU.subtract).then_inc(xc_done.sem, 1)

            def normalise_tokens(s, slot, _):
                dve.wait_ge(rstd_done.sem, rstd_done.at(s, 1))
                dve.wait_ge(sq_done.sem, sq_done.at(s, 1))
                nc.vector.tensor_tensor(xc[:], xc[:], rstd[:].unsqueeze(1).to_broadcast([P, CHUNKS, SEQ]),
                                        ALU.mult).then_inc(xn_done.sem, 1)

            def gated(s, slot, m):
                rows = hid_rows(m)
                dve.wait_ge(gelu_done.sem, gelu_done.at(s, m + 1))
                psum.wait_full(dve, s, f"a{m}")
                nc.vector.scalar_tensor_tensor(h2[0:rows, m, :], psum.tile(f"a{m}")[0:rows, :], b_1a[0:rows, bass.ds(s, 1), m],
                                               gelu[m % 2][0:rows, :], ALU.add, ALU.mult).then_inc(h2_done.sem, 1)

            def finish(s, slot, c):
                dve.wait_ge(stored.sem, stored.at(s))
                psum.wait_full(dve, s, f"wd{c}")
                nc.vector.scalar_tensor_tensor(x_out[:, c, :], psum.tile(f"wd{c}")[:], b_2[:, bass.ds(s, 1), c],
                                               plain(x2, c), ALU.add, ALU.add).then_inc(x_out_done.sem, 1)

            pipeline(dve, {"turn": turn_pair, "kt": finish_k, "ssq": floor_q, "mask": mask_scores, "pt": copy_turned,
                           "onorm": normalise, "wo": add_residual, "mean": centre, "xn": normalise_tokens,
                           "ga": gated, "wd": finish})


def load_stack_vectors(nc, inp, squares, pair_ones, rotary, qk_scale, ln_g, ln_b, b_1a, b_1g, b_2):
    with ExitStack() as ctx:
        loaded = ctx.enter_context(nc.semaphore("v_loaded"))
        small = [ctx.enter_context(nc.sbuf_tensor(f"v_small{i}", [P, DEPTH, x.shape[2]], F32))
                 for i, x in enumerate((qk_scale, ln_g, ln_b, b_2, b_1a, b_1g))]
        qk, g, b, b2, b1a, b1g = small
        n_loads = 3 + 4 + 6 + 8
        with nc.Block() as block:
            @block.sync
            def _(sp):
                with nc.allow_non_contiguous_dma(reason="short vectors onto partitions"):
                    def put(to, src):
                        sp.dma_start(to, src).then_inc(loaded, 16)

                    put(squares[:], inp["c_squares"].rearrange("p (s c) -> p s c", c=P))
                    put(pair_ones[:], inp["c_small"][:, 2 * STATES:2 * STATES + 2])
                    put(rotary[:], inp["c_rotary"])
                    for i, name in enumerate(("L0_ffn_q_scale", "L0_ffn_k_scale")):
                        for half in range(2):
                            put(qk[half * DIM_HEAD:(half + 1) * DIM_HEAD, :, i], inp[name].rearrange("l d -> d l"))
                    for to, name in ((g, "L0_ffn_ln_g"), (b, "L0_ffn_ln_b"), (b2, "L0_ffn_b2")):
                        for l in range(DEPTH):
                            put(to[:, l, :], inp[name][l].rearrange("(c p) -> p c", p=P))
                    whole = HID // P
                    for to, at in ((b1a, 0), (b1g, HID)):
                        for l in range(DEPTH):
                            put(to[:, l, 0:whole], inp["L0_ffn_b1"][l, at:at + whole * P].rearrange("(c p) -> p c", p=P))
                            put(to[0:HID - whole * P, l, whole:whole + 1],
                                inp["L0_ffn_b1"][l, at + whole * P:at + HID].rearrange("(p c) -> p c", c=1))

            @block.vector
            def _(dve):
                dve.wait_ge(loaded, 16 * n_loads)
                whole, rest = HID // P, HID % P
                for to, src in ((qk_scale, qk), (ln_g, g), (ln_b, b), (b_2, b2)):
                    for l in range(DEPTH):
                        part = to[:, l * BATCH:(l + 1) * BATCH, :]
                        nc.vector.tensor_copy(part, src[:, l, :].unsqueeze(1).to_broadcast(list(part.shape)))
                for to, src in ((b_1a, b1a), (b_1g, b1g)):
                    for l in range(DEPTH):
                        part = to[:, l * BATCH:(l + 1) * BATCH, 0:whole]
                        nc.vector.tensor_copy(part, src[:, l, 0:whole].unsqueeze(1).to_broadcast(list(part.shape)))
                        part = to[0:rest, l * BATCH:(l + 1) * BATCH, whole:whole + 1]
                        nc.vector.tensor_copy(part, src[0:rest, l, whole:whole + 1].unsqueeze(1).to_broadcast(list(part.shape)))


def final_pass(nc, inp, mod, x1_dram, stack_dram, out):
    with ExitStack() as ctx:
        def sb(name, shape):
            return ctx.enter_context(nc.sbuf_tensor("c_" + name, shape, F32))

        def sem(name):
            return ctx.enter_context(nc.semaphore("c_" + name))

        signals = []

        def signal(name, per_pass, unit=1):
            signals.append(Signal(sem(name), per_pass, unit))
            return signals[-1]

        banks = [ctx.enter_context(nc.psum_tensor(f"c_bank{i}", [P, 512], F32)) for i in range(2)]
        ident = sb("ident", [P, P])
        x1 = sb("x1", [P, CHUNKS, SEQ])
        f = sb("f", [P, CHUNKS, SEQ])
        y = sb("y", [P, CHUNKS, SEQ])
        tokens = sb("tokens", [P, TILES, DIM])
        ident_loaded = sem("ident_loaded")
        loaded = signal("loaded", 2, 16)
        y_done = signal("y_done", CHUNKS)
        turned = [signal(f"turned{i}", 1) for i in range(2)]
        tokens_done = signal("tokens_done", 2)
        stored = signal("stored", 1, 16)

        start_signals(nc, signals)
        block = ctx.enter_context(nc.Block())

        @block.sync
        def _(sp):
            sp.dma_start(ident[:], inp["c_squares"][:, 0:P]).then_inc(ident_loaded, 16)
            with sp.Fori(0, BATCH) as b:
                sp.wait_ge(y_done.sem, y_done.at(b))
                sp.dma_start(x1[:], x1_dram[b]).then_inc(loaded.sem, 16)
                sp.dma_start(f[:], stack_dram[DEPTH * BATCH + b]).then_inc(loaded.sem, 16)

        @block.scalar
        def _(act):
            with act.Fori(0, BATCH) as b:
                act.wait_ge(tokens_done.sem, tokens_done.at(b, 2))
                act.dma_start(out[b].rearrange("(t p) d -> p t d", p=P), tokens[:]).then_inc(stored.sem, 16)
            act.wait_ge(stored.sem, stored.at(BATCH))

        @block.vector
        def _(dve):
            with dve.Fori(0, BATCH) as b:
                dve.wait_ge(loaded.sem, loaded.at(b, 2))
                dve.wait_ge(tokens_done.sem, tokens_done.at(b))
                for c in range(CHUNKS):
                    nc.vector.scalar_tensor_tensor(y[:, c, :], f[:, c, :], mod[:, 2 * MOD_GATE_B + c, bass.ds(b, 1)],
                                                   x1[:, c, :], ALU.mult, ALU.add).then_inc(y_done.sem, 1)
                dve.wait_ge(stored.sem, stored.at(b))
                for i in range(2):
                    dve.wait_ge(turned[i].sem, turned[i].at(b, 1))
                    nc.vector.tensor_copy(tokens[:, 2 * i:2 * i + 2, :], banks[i][:].rearrange("p (t d) -> p t d", d=DIM))\
                        .then_inc(tokens_done.sem, 1)

        @block.tensor
        def _(pe):
            pe.wait_ge(ident_loaded, 16)
            with pe.Fori(0, BATCH) as b:
                pe.wait_ge(y_done.sem, y_done.at(b, CHUNKS))
                for t in range(TILES):
                    if t % 2 == 0:
                        pe.wait_ge(tokens_done.sem, tokens_done.at(b, 0))
                    for c in range(CHUNKS):
                        at = (t % 2) * DIM + c * P
                        last = nc.tensor.transpose(banks[t // 2][:, at:at + P], y[:, c, t * P:(t + 1) * P], ident[:])
                    if t % 2:
                        last.then_inc(turned[t // 2].sem, 1)


def setup_weights(nc, inp, banks, ident, mean_mat, pick, picks, w_in_t, w_dt_t, w_bc_t, w_out_t,
                  neg_a, b_dt, skip_d, mod, ln_eps):
    with ExitStack() as ctx:
        def sb(name, shape, dt=F32):
            return ctx.enter_context(nc.sbuf_tensor("s_" + name, shape, dt))

        def sem(name):
            return ctx.enter_context(nc.semaphore("s_" + name))

        w_in = sb("w_in", [P, 8, DIM])
        w_dt = sb("w_dt", [P, INNER_CHUNKS, D_INNER])
        w_out = sb("w_out", [P, CHUNKS, D_INNER])
        w_bc = sb("w_bc", [2 * STATES, D_INNER])
        cond = sb("cond", [BATCH, DIM])
        cond_t = sb("cond_t", [P, CHUNKS, BATCH])
        w_mod = sb("w_mod", [P, CHUNKS, 6 * DIM])
        a_log = sb("a_log", [P, INNER_CHUNKS, STATES])
        gate = sb("gate", [P, 1])
        sign = sb("sign", [P, 2 * CHUNKS, BATCH])
        size = sb("size", [P, 2 * CHUNKS, BATCH])

        squares_loaded, w_in_loaded, w_dt_loaded = sem("squares_loaded"), sem("w_in_loaded"), sem("w_dt_loaded")
        w_out_loaded, w_bc_loaded, small_loaded = sem("w_out_loaded"), sem("w_bc_loaded"), sem("small_loaded")
        cond_loaded, w_mod_loaded = sem("cond_loaded"), sem("w_mod_loaded")
        turned, copied = sem("turned"), sem("copied")
        silu_done, cond_turned, cond_copied = sem("silu_done"), sem("cond_turned"), sem("cond_copied")
        mod_full, mod_copied, gate_step = sem("mod_full"), sem("mod_copied"), sem("gate_step")
        mod_step, a_step = sem("mod_step"), sem("a_step")

        turns = []
        for c in range(CHUNKS):
            for half in range(2):
                turns.append((w_in_loaded, [w_in[:, 4 * half + m, c * P:(c + 1) * P] for m in range(4)],
                              w_in_t[:, c, half * 512:(half + 1) * 512], P))
        for k in range(INNER_CHUNKS):
            turns.append((w_dt_loaded, [w_dt[:, m, k * P:(k + 1) * P] for m in range(4)], w_dt_t[:, k, :], P))
        for k in range(INNER_CHUNKS):
            turns.append((w_out_loaded, [w_out[:, o, k * P:(k + 1) * P] for o in range(CHUNKS)], w_out_t[:, k, :], P))
        for k in range(INNER_CHUNKS):
            turns.append((w_bc_loaded, [w_bc[:, k * P:(k + 1) * P]], w_bc_t[:, k, :], 2 * STATES))

        with nc.Block() as block:
            @block.sync
            def _(sp):
                sp.dma_start(ident[:], inp["c_squares"][:, 0:P]).then_inc(squares_loaded, 16)
                sp.dma_start(mean_mat[:], inp["c_squares"][:, P:2 * P]).then_inc(squares_loaded, 16)
                sp.dma_start(w_in[:], inp["L0_attn_W_in"].rearrange("(m p) d -> p m d", p=P)).then_inc(w_in_loaded, 16)
                sp.dma_start(cond[:], inp["L0_c"]).then_inc(cond_loaded, 16)
                sp.dma_start(w_dt[:], inp["L0_attn_W_dt"].rearrange("(m p) d -> p m d", p=P)).then_inc(w_dt_loaded, 16)
                sp.dma_start(w_out[:], inp["L0_attn_W_out"].rearrange("(m p) d -> p m d", p=P)).then_inc(w_out_loaded, 16)
                sp.dma_start(w_bc[0:STATES, :], inp["L0_attn_W_B"]).then_inc(w_bc_loaded, 16)
                sp.dma_start(w_bc[STATES:, :], inp["L0_attn_W_C"]).then_inc(w_bc_loaded, 16)
                sp.dma_start(w_mod[:], inp["L0_wmod"].rearrange("(c p) f -> p c f", p=P)).then_inc(w_mod_loaded, 16)

            @block.scalar
            def _(act):
                act.dma_start(pick[:], inp["c_small"][:, 0:2 * STATES]).then_inc(small_loaded, 16)
                act.dma_start(a_log[:], inp["L0_attn_A_log"].rearrange("(c p) n -> p c n", p=P)).then_inc(small_loaded, 16)
                with nc.allow_non_contiguous_dma(reason="three short vectors"):
                    act.dma_start(b_dt[:], inp["L0_attn_b_dt"].rearrange("(c p) -> p c", p=P)).then_inc(small_loaded, 16)
                    act.dma_start(skip_d[:], inp["L0_attn_D"].rearrange("(c p) -> p c", p=P)).then_inc(small_loaded, 16)
                    act.dma_start(gate[:], inp["L0_attn_output_gate"].rearrange("(a b) -> a b", a=1)
                                  .to_broadcast([P, 1])).then_inc(small_loaded, 16)
                act.wait_ge(cond_loaded, 16)
                nc.scalar.activation(cond[:], cond[:], ACT.Silu).then_inc(silu_done, 1)
                act.wait_ge(small_loaded, 16 * 5)
                nc.scalar.activation(gate[:], gate[:], ACT.Sigmoid).then_inc(gate_step, 1)
                nc.scalar.activation(a_log[:], a_log[:], ACT.Exp).then_inc(a_step, 1)

            @block.tensor
            def _(pe):
                pe.wait_ge(squares_loaded, 32)
                pe.wait_ge(silu_done, 1)
                for c in range(CHUNKS):
                    last = nc.tensor.transpose(banks[7][:, c * BATCH:(c + 1) * BATCH], cond[:, c * P:(c + 1) * P],
                                               ident[0:BATCH, 0:BATCH])
                last.then_inc(cond_turned, 1)
                for i, (loaded, sources, _, rows) in enumerate(turns):
                    pe.wait_ge(loaded, 32 if loaded is w_bc_loaded else 16)
                    if i >= 6:
                        pe.wait_ge(copied, i - 5)
                    for m, s in enumerate(sources):
                        last = nc.tensor.transpose(banks[i % 6][:, m * rows:(m + 1) * rows], s, ident[0:rows, 0:rows])
                    last.then_inc(turned, 1)
                pe.wait_ge(w_mod_loaded, 16)
                pe.wait_ge(cond_copied, 1)
                for f in range(12):
                    for c in range(CHUNKS):
                        last = nc.tensor.matmul(banks[6][:, f * BATCH:(f + 1) * BATCH], w_mod[:, c, f * P:(f + 1) * P],
                                                cond_t[:, c, :], start=(c == 0), stop=(c == CHUNKS - 1))
                last.then_inc(mod_full, 1)

            @block.vector
            def _(dve):
                nc.vector.memset(ln_eps[:], LN_EPS)
                dve.wait_ge(cond_turned, 1)
                nc.vector.tensor_copy(cond_t[:].rearrange("p c b -> p (c b)"), banks[7][:, 0:CHUNKS * BATCH]).then_inc(cond_copied, 1)
                for i, (_, sources, target, rows) in enumerate(turns):
                    dve.wait_ge(turned, i + 1)
                    nc.vector.tensor_copy(target, banks[i % 6][:, 0:len(sources) * rows]).then_inc(copied, 1)
                dve.wait_ge(a_step, 1)
                nc.vector.tensor_scalar(neg_a[:], a_log[:], -1.0, None, ALU.mult)
                nc.vector.tensor_copy(picks[0:96], pick[0:96].unsqueeze(2).to_broadcast([96, 2 * STATES, P]))
                dve.wait_ge(mod_full, 1)
                nc.vector.tensor_copy(mod[:].rearrange("p f b -> p (f b)"), banks[6][:, 0:12 * BATCH]).then_inc(mod_copied, 1)
                dve.wait_ge(mod_copied, 1)
                for s in (MOD_SCALE_A, MOD_SCALE_B):
                    part = mod[:, 2 * s:2 * s + 2, :]
                    nc.vector.tensor_scalar(part, part, 1.0, None, ALU.add)
                for i, g in enumerate((MOD_GATE_A, MOD_GATE_B)):
                    part, at = mod[:, 2 * g:2 * g + 2, :], slice(2 * i, 2 * i + 2)
                    nc.vector.tensor_scalar(sign[:, at], part, 0.0, 2.0, ALU.is_ge, ALU.mult).then_inc(mod_step, 1)
                    nc.vector.scalar_tensor_tensor(size[:, at], part, -1.0, part, ALU.mult, ALU.max).then_inc(mod_step, 1)
                dve.wait_ge(mod_step, 4)
                nc.vector.tensor_scalar(sign[:], sign[:], 1.0, None, ALU.subtract).then_inc(mod_step, 1)
                nc.vector.tensor_scalar(size[:], size[:], 0.25, None, ALU.max).then_inc(mod_step, 1)
                dve.wait_ge(mod_step, 6)
                dve.wait_ge(gate_step, 1)
                nc.vector.scalar_tensor_tensor(mod[:, 2 * MOD_GATE_A:2 * MOD_GATE_A + 2, :], sign[:, 0:2], gate[:, 0:1],
                                               size[:, 0:2], ALU.mult, ALU.mult)
                nc.vector.tensor_tensor(mod[:, 2 * MOD_GATE_B:2 * MOD_GATE_B + 2, :], sign[:, 2:4], size[:, 2:4], ALU.mult)


def build(nc, inp, out):
    x1_dram = nc.dram_tensor("x1_rows", (BATCH, P, CHUNKS, SEQ), F32, kind="Internal").ap()
    stack_dram = nc.dram_tensor("stack_rows", ((DEPTH + 1) * BATCH, P, CHUNKS, SEQ), F32, kind="Internal").ap()
    with nc.sbuf_tensor("mod", [P, 12, BATCH], F32) as mod:
        mixer_pass(nc, inp, mod, x1_dram, stack_dram)
        stack_pass(nc, inp, stack_dram)
        final_pass(nc, inp, mod, x1_dram, stack_dram, out)


NAMES = ["L0_attn_x", "L0_attn_W_in", "L0_attn_A_log", "L0_attn_W_B", "L0_attn_W_C", "L0_attn_W_dt", "L0_attn_b_dt",
         "L0_attn_D", "L0_attn_output_gate", "L0_attn_W_out", "L0_ffn_wqkv", "L0_ffn_q_scale", "L0_ffn_k_scale",
         "L0_ffn_wo", "L0_ffn_ln_g", "L0_ffn_ln_b", "L0_ffn_w1", "L0_ffn_b1", "L0_ffn_w2", "L0_ffn_b2", "L0_c", "L0_wmod"]


def kernel(**inputs):
    import concourse.bacc as bacc
    from concourse.bass_utils import run_bass_kernel_spmd

    nc = bacc.Bacc("TRN2", target_bir_lowering=False, num_devices=1)
    arrays = {name: np.ascontiguousarray(inputs[name]) for name in NAMES}
    arrays.update(host_constants())
    inp = {name: nc.dram_tensor("in_" + name, a.shape, mybir.dt.from_np(a.dtype), kind="ExternalInput").ap()
           for name, a in arrays.items()}
    out = nc.dram_tensor("out_rows", (BATCH, SEQ, DIM), F32, kind="ExternalOutput").ap()
    build(nc, inp, out)
    result = run_bass_kernel_spmd(nc, [{"in_" + name: a for name, a in arrays.items()}], core_ids=[0])
    return result.results[0]["out_rows"]
```

```python
from contextlib import ExitStack

import numpy as np

import concourse.bass as bass
import concourse.mybir as mybir
from concourse.alu_op_type import AluOpType as ALU

ACT = mybir.ActivationFunctionType
F32 = mybir.dt.float32
BF16 = mybir.dt.bfloat16
I32 = mybir.dt.int32
AX_X = mybir.AxisListType.X

P = 128
BATCH, SEQ, DIM = 16, 512, 256
CHUNKS = DIM // P
TILES = SEQ // P
D_INNER = 512
INNER_CHUNKS = D_INNER // P
STATES = 16
GROUP = 2
GROUPS = STATES // GROUP
UNITS = GROUPS * INNER_CHUNKS
DECAY_SLOTS, STATE_SLOTS = 4, 8
DEPTH, HEADS, DIM_HEAD, WINDOW = 2, 8, 64, 128
INNER = HEADS * DIM_HEAD
PAIRS = HEADS // 2
HID = int(DIM * 4 * 2 / 3)
HID_CHUNKS = -(-HID // P)
QK_SCALE = 8.0
LN_EPS = 1e-5
SERIES_BELOW = 0.02
MASKED = -3.0e38
SCREEN = 2.0 ** 17
EXP_AND_LN = "natural_log_exp_and_others"
MOD_SHIFT_A, MOD_SCALE_A, MOD_GATE_A, MOD_SHIFT_B, MOD_SCALE_B, MOD_GATE_B = range(6)


class Signal:

    def __init__(self, sem, per_pass, unit=1):
        self.sem, self.per_pass, self.unit = sem, per_pass * unit, unit

    def at(self, done, k=0):
        return done * self.per_pass + (k * self.unit + 1)


def start_signals(nc, signals):
    with nc.Block() as block:
        @block.gpsimd
        def _(pool):
            for signal in signals:
                pool.sem_inc(signal.sem, 1)


class Banks:

    def __init__(self, tiles, full, uses):
        self.tiles, self.full = tiles, full
        self.where, self.count, self.before, last = {}, [0] * len(tiles), {}, {}
        for name, bank, signal, k in uses:
            self.where[name] = (bank, self.count[bank])
            self.count[bank] += 1
            self.before[name] = last.get(bank)
            last[bank] = (signal, k)
        for name, bank, _, _ in uses:
            if self.before[name] is None:
                signal, k = last[bank]
                self.before[name] = (signal, k - signal.per_pass)

    def tile(self, name):
        return self.tiles[self.where[name][0]]

    def wait_free(self, eng, done, name):
        signal, k = self.before[name]
        if not (isinstance(done, int) and done == 0 and k < 0):
            eng.wait_ge(signal.sem, signal.at(done, k))

    def wait_full(self, eng, done, name):
        bank, k = self.where[name]
        eng.wait_ge(self.full[bank], done * self.count[bank] + k + 1)

    def filled(self, instruction, name):
        instruction.then_inc(self.full[self.where[name][0]], 1)


def host_constants():
    eye = np.eye(P, dtype=np.float32)
    mean = np.full((P, P), 1.0 / DIM, np.float32)
    i, j = np.arange(WINDOW)[:, None], np.arange(WINDOW)[None, :]
    mask_back = np.where(j >= i, 0.0, MASKED).astype(np.float32)
    mask_own = np.where(j <= i, 0.0, MASKED).astype(np.float32)
    squares = np.concatenate([eye, mean, mask_back, mask_own], axis=1)
    pick = np.zeros((P, 2 * STATES), np.float32)
    pick[np.arange(96), np.arange(96) % (2 * STATES)] = 1.0
    f32 = np.float32
    half_idx = np.arange(0, DIM_HEAD, 2, dtype=f32)
    inv_freq = f32(1.0) / np.power(f32(10000.0), half_idx / f32(DIM_HEAD), dtype=f32)
    t = np.arange(SEQ, dtype=f32)
    freqs = (t[:, None] * inv_freq[None, :]).astype(f32)
    base = ((half_idx + f32(0.4 * DIM_HEAD)) / f32(1.4 * DIM_HEAD)).astype(f32)
    power = ((t - f32(SEQ // 2)) / f32(WINDOW // 2)).astype(f32)
    scale = np.power(base[None, :], power[:, None], dtype=f32)
    cos, sin = np.cos(freqs, dtype=f32), np.sin(freqs, dtype=f32)
    two = lambda x: np.concatenate([x, x], axis=1)
    cos, sin, scale = two(cos), np.concatenate([-sin, sin], axis=1), two(scale)
    tables = np.stack([np.stack([f32(QK_SCALE) * cos * scale, cos / scale], axis=1),
                       np.stack([f32(QK_SCALE) * sin * scale, sin / scale], axis=1)], axis=1).astype(f32)
    rotary = tables.reshape(TILES, P, 2, 2, DIM_HEAD).transpose(1, 0, 2, 3, 4)
    return {"c_squares": squares, "c_pick": pick, "c_rotary": np.ascontiguousarray(rotary)}


MIXER_STAGE = {"xT": "head", "xcopy": "head", "mean1": "head", "cen1": "head", "sq1": "head", "var1": "head", "dev1": "head",
               "xn1": "head", "h1": "head", "xs": "head", "xscopy": "head", "bc": "head", "cut": "head",
               "dt": "head", "soft": "head", "step": "head", "first": "head",
               "unit": "scan", "wide": "scan", "sum": "scan", "z": "head", "zcopy": "head", "silu": "head",
               "last": "tail", "gate": "tail", "out": "tail", "res": "tail", "mean2": "tail", "cen2": "tail", "sq2": "tail",
               "var2": "tail", "dev2": "tail", "xn2": "tail", "h2": "tail"}
MIXER_LEAD = {"head": 1, "scan": 0, "tail": -1}
MIXER_ORDER = """
unit:0 wide:1.0 last:29
unit:1 wide:1.1 last:30 gate:0
unit:2 wide:1.2 last:31 gate:1
unit:3 wide:1.3 sum:0 gate:2
unit:4 wide:2.0 sum:1 gate:3
unit:5 wide:2.1 sum:2 out:0
unit:6 wide:2.2 sum:3 res:0 out:1
unit:7 wide:2.3 sum:4 xT:0 xT:1 res:1
unit:8 wide:3.0 sum:5 xcopy:0 xcopy:1 mean2:0
unit:9 wide:3.1 sum:6 mean1:0 cen2:0 sq2:0
unit:10 wide:3.2 sum:7 cen1:0 sq1:0 var2:0
unit:11 wide:3.3 sum:8 var1:0 dev2:0
unit:12 wide:4.0 sum:9 dev1:0 xn2:0
unit:13 wide:4.1 sum:10 xn1:0 h2:0
unit:14 wide:4.2 sum:11 h1:0
unit:15 wide:4.3 sum:12 xs:0
unit:16 wide:5.0 sum:13 xs:1 xscopy:0
unit:17 wide:5.1 sum:14 xs:2 xscopy:1
unit:18 wide:5.2 sum:15 xs:3 xscopy:2
unit:19 wide:5.3 sum:16 xscopy:3
unit:20 wide:6.0 sum:17 bc:0 dt:0
unit:21 wide:6.1 sum:18 soft:0 cut:0 dt:1
unit:22 wide:6.2 sum:19 step:0
unit:23 wide:6.3 sum:20 soft:1 dt:2
unit:24 wide:7.0 sum:21 step:1 soft:2 dt:3
unit:25 wide:7.1 sum:22 step:2 soft:3 z:0
unit:26 wide:7.2 sum:23 zcopy:0 step:3 z:1
unit:27 wide:7.3 sum:24 zcopy:1 z:2
unit:28 sum:25 zcopy:2 z:3
unit:29 sum:26 zcopy:3
unit:30 sum:27 silu:0 first:0
unit:31 sum:28
"""


def steps_of(order):
    return [(name, *map(int, at.split("."))) for name, _, at in (step.partition(":") for step in order.split())]


MIXER_SCHEDULE = steps_of(MIXER_ORDER)


def mixer_pass(nc, inp, mod, x1_dram, stack_dram):
    with ExitStack() as ctx:
        def sb(name, shape, dt=F32):
            return ctx.enter_context(nc.sbuf_tensor("a_" + name, shape, dt))

        def sem(name):
            return ctx.enter_context(nc.semaphore("a_" + name))

        signals = []

        def signal(name, per_pass, unit=1):
            signals.append(Signal(sem(name), per_pass, unit))
            return signals[-1]

        banks_all = [ctx.enter_context(nc.psum_tensor(f"a_bank{i}", [P, 512], F32)) for i in range(8)]

        ident = sb("ident", [P, P])
        mean_mat = sb("mean_mat", [P, P])
        pick = sb("pick", [P, 2 * STATES])
        picks = sb("picks", [P, 2 * STATES, P], BF16)
        w_in_t = sb("w_in_t", [P, CHUNKS, 2 * D_INNER])
        w_dt_t = sb("w_dt_t", [P, INNER_CHUNKS, D_INNER])
        w_bc_t = sb("w_bc_t", [P, INNER_CHUNKS, 2 * STATES])
        w_out_t = sb("w_out_t", [P, INNER_CHUNKS, DIM])
        neg_a = sb("neg_a", [P, INNER_CHUNKS, STATES])
        b_dt = sb("b_dt", [P, INNER_CHUNKS])
        skip_d = sb("skip_d", [P, INNER_CHUNKS])
        ln_eps = sb("ln_eps", [P, 1])
        waiter = sb("waiter", [P, INNER_CHUNKS])

        setup_weights(nc, inp, banks_all, ident, mean_mat, pick, picks, w_in_t, w_dt_t, w_bc_t, w_out_t,
                      neg_a, b_dt, skip_d, mod, ln_eps)

        xt = sb("xt", [P, TILES, DIM])
        x_t = [sb(f"x_t{i}", [P, CHUNKS, SEQ]) for i in range(2)]
        xc = sb("xc", [P, CHUNKS, SEQ])
        rstd = sb("rstd", [P, SEQ])
        h_t = sb("h_t", [P, CHUNKS, SEQ])
        sq = h_t
        xs = [sb(f"xs{i}", [P, INNER_CHUNKS, SEQ]) for i in range(2)]
        sz = [sb(f"sz{i}", [P, INNER_CHUNKS, SEQ]) for i in range(2)]
        dt = [sb(f"dt{i}", [P, INNER_CHUNKS, SEQ]) for i in range(2)]
        u = [sb(f"u{i}", [P, INNER_CHUNKS, SEQ]) for i in range(2)]
        sp_e = sb("sp_e", [P, SEQ])
        sp_ln = sb("sp_ln", [P, SEQ])
        sp_relu = sb("sp_relu", [P, SEQ])
        sp_p = sb("sp_p", [P, SEQ])
        sp_mask = sb("sp_mask", [P, SEQ], I32)
        bc_parts = [sb(f"bc_parts{i}", [P, SEQ], BF16) for i in range(2)]
        bc_rest = sp_p[0:2 * STATES, :]
        bc_mid = sb("bc_mid", [2 * STATES, SEQ], BF16)
        decay = [sb(f"decay{i}", [P, GROUP, SEQ]) for i in range(DECAY_SLOTS)]
        state = [sb(f"state{i}", [P, GROUP, SEQ]) for i in range(STATE_SLOTS)]
        b_wide = [sb(f"b_wide{i}", [P, GROUP, SEQ]) for i in range(2)]
        c_wide = [sb(f"c_wide{i}", [P, GROUP, SEQ]) for i in range(2)]
        yv = u
        x1_t = sb("x1_t", [P, CHUNKS, SEQ])
        xc2 = sb("xc2", [P, CHUNKS, SEQ])
        rstd2 = sb("rstd2", [P, SEQ])
        h2_t = sb("h2_t", [P, CHUNKS, SEQ])
        sq2 = h2_t

        x_loaded = signal("x_loaded", 1, 16)
        x_t_done = signal("x_t_done", CHUNKS)
        xc_done = signal("xc_done", CHUNKS)
        sq_done = signal("sq_done", 1)
        ln_done = signal("ln_done", 1)
        rstd_done = signal("rstd_done", 1)
        xn_done = signal("xn_done", 1)
        h_done = signal("h_done", CHUNKS)
        xs_done = signal("xs_done", INNER_CHUNKS)
        z_done = signal("z_done", INNER_CHUNKS)
        silu_done = signal("silu_done", 1)
        parts_done = signal("parts_done", 5)
        abs_done = signal("abs_done", INNER_CHUNKS)
        exp_done = signal("exp_done", INNER_CHUNKS)
        log_done = signal("log_done", INNER_CHUNKS)
        series_done = signal("series_done", 6 * INNER_CHUNKS)
        dt_done = signal("dt_done", INNER_CHUNKS)
        u_done = signal("u_done", INNER_CHUNKS)
        b_wide_done = signal("b_wide_done", STATES)
        c_wide_done = signal("c_wide_done", STATES)
        decay_done = signal("decay_done", UNITS)
        input_done = signal("input_done", UNITS)
        scan_done = signal("scan_done", UNITS)
        on_vector = [q for q in range(UNITS) if q % 8 == 3]
        on_pool = [q for q in range(UNITS) if q not in on_vector]
        cmul_pool_done = signal("cmul_pool_done", len(on_pool))
        cmul_vec_done = signal("cmul_vec_done", len(on_vector))
        sum_done = signal("sum_done", UNITS)
        skip_done = signal("skip_done", INNER_CHUNKS)
        gated_done = signal("gated_done", INNER_CHUNKS)
        x1_done = signal("x1_done", CHUNKS)
        xc2_done = signal("xc2_done", CHUNKS)
        sq2_done = signal("sq2_done", 1)
        ln2_done = signal("ln2_done", 1)
        rstd2_done = signal("rstd2_done", 1)
        xn2_done = signal("xn2_done", 1)
        h2_done = signal("h2_done", CHUNKS)
        stored = signal("stored", 2, 16)

        def wide_name(g, i):
            return f"wide{g}_{i}"

        def wide_signal(i):
            return (b_wide_done, i) if i < GROUP else (c_wide_done, i - GROUP)

        uses, head_uses = [], 0
        for name, k, *i in MIXER_SCHEDULE:
            if name == "wide":
                done, n = wide_signal(i[0])
                uses.append((wide_name(k, i[0]), 2, done, GROUP * k + n + 1))
            elif name in ("out", "mean2", "var2"):
                reader, count = {"out": (x1_done, k + 1), "mean2": (xc2_done, CHUNKS), "var2": (ln2_done, 1)}[name]
                uses.append((f"out{k}" if name == "out" else name, 3, reader, count))
            else:
                mine = {"xT": [(f"xT{k}", x_t_done, k + 1)],
                        "mean1": [("mean1", xc_done, CHUNKS)],
                        "var1": [("var1", ln_done, 1)],
                        "xs": [(f"xs{k}", xs_done, k + 1)],
                        "z": [(f"z{k}", z_done, k + 1)],
                        "bc": [("bc", parts_done, 2)],
                        "dt": [(f"dt{k}", abs_done, k + 1)],
                        "first": [(wide_name(0, n), wide_signal(n)[0], wide_signal(n)[1] + 1) for n in range(2 * GROUP)]}
                for use, reader, count in mine.get(name, []):
                    uses.append((use, head_uses % 2, reader, count))
                    head_uses += 1
        work = Banks(banks_all[:4], [sem(f"full{i}") for i in range(4)], uses)
        y_sum = banks_all[4:]

        def cmul_until(eng, s, n):
            eng.wait_ge(cmul_pool_done.sem, cmul_pool_done.at(s, sum(q < n for q in on_pool)))
            eng.wait_ge(cmul_vec_done.sem, cmul_vec_done.at(s, sum(q < n for q in on_vector)))

        def cmul_wait(eng, s, q):
            if q in on_pool:
                eng.wait_ge(cmul_pool_done.sem, cmul_pool_done.at(s, on_pool.index(q) + 1))
            else:
                eng.wait_ge(cmul_vec_done.sem, cmul_vec_done.at(s, on_vector.index(q) + 1))

        def slot_free(eng, s, done):
            if not (isinstance(s, int) and s < 2):
                eng.wait_ge(done.sem, done.at(s - 1))

        def unit_slot_free(eng, s, q, slots, done):
            if not (isinstance(s, int) and s == 0 and q < slots):
                eng.wait_ge(done.sem, done.at(s, q - slots + 1))

        def pipeline(eng, steps):
            def one_pass(i, parity, stages):
                for name, *at in MIXER_SCHEDULE:
                    lead = MIXER_LEAD[MIXER_STAGE[name]]
                    if MIXER_STAGE[name] in stages and name in steps:
                        steps[name](i + lead, (parity + lead) % 2, *at)

            one_pass(-1, 1, ("head",))
            one_pass(0, 0, ("head", "scan"))
            with eng.Fori(0, BATCH // 2 - 1) as j:
                one_pass(2 * j + 1, 1, ("head", "scan", "tail"))
                one_pass(2 * j + 2, 0, ("head", "scan", "tail"))
            one_pass(BATCH - 1, 1, ("scan", "tail"))
            one_pass(BATCH, 0, ("tail",))

        with nc.Block() as block:
            @block.vector
            def _(dve):
                for d in decay:
                    nc.vector.memset(d[:, :, 0:1], 0.0)

        start_signals(nc, signals)
        block = ctx.enter_context(nc.Block())

        @block.sync
        def _(sp):
            def load(s):
                sp.wait_ge(x_t_done.sem, x_t_done.at(s))
                sp.dma_start(xt[:], inp["L0_attn_x"][s].rearrange("(t p) d -> p t d", p=P)).then_inc(x_loaded.sem, 16)

            def store(s):
                sp.wait_ge(x1_done.sem, x1_done.at(s, CHUNKS))
                sp.dma_start(x1_dram[s], x1_t[:]).then_inc(stored.sem, 16)
                sp.wait_ge(h2_done.sem, h2_done.at(s, CHUNKS))
                sp.dma_start(stack_dram[s], h2_t[:]).then_inc(stored.sem, 16)

            for s in range(3):
                load(s)
            with sp.Fori(3, BATCH) as s:
                load(s)
                store(s - 3)
            for s in range(BATCH - 3, BATCH):
                store(s)
            sp.wait_ge(stored.sem, stored.at(BATCH))

        @block.tensor
        def _(pe):
            def product(s, name, weights, sources, rows=P):
                work.wait_free(pe, s, name)
                for c, source in enumerate(sources):
                    last = nc.tensor.matmul(work.tile(name)[0:rows, :], weights[c], source,
                                            start=(c == 0), stop=(c == len(sources) - 1))
                work.filled(last, name)

            def cols(weights, at, n=P):
                return [weights[:, c, at:at + n] for c in range(weights.shape[1])]

            def chunks(x):
                return [x[:, c, :] for c in range(x.shape[1])]

            means = [mean_mat[:]] * CHUNKS

            def turn_input(s, slot, c):
                pe.wait_ge(x_loaded.sem, x_loaded.at(s, 1))
                work.wait_free(pe, s, f"xT{c}")
                for t in range(TILES):
                    last = nc.tensor.transpose(work.tile(f"xT{c}")[:, t * P:(t + 1) * P], xt[:, t, c * P:(c + 1) * P], ident[:])
                work.filled(last, f"xT{c}")

            def mean_head(s, slot, _):
                pe.wait_ge(x_t_done.sem, x_t_done.at(s, CHUNKS))
                product(s, "mean1", means, chunks(x_t[slot]))

            def var_head(s, slot, _):
                pe.wait_ge(sq_done.sem, sq_done.at(s, 1))
                product(s, "var1", means, chunks(sq))

            def project_x(s, slot, m):
                pe.wait_ge(h_done.sem, h_done.at(s, CHUNKS))
                product(s, f"xs{m}", cols(w_in_t, m * P), chunks(h_t))

            def project_z(s, slot, m):
                product(s, f"z{m}", cols(w_in_t, D_INNER + m * P), chunks(h_t))

            def project_bc(s, slot, _):
                pe.wait_ge(xs_done.sem, xs_done.at(s, INNER_CHUNKS))
                product(s, "bc", cols(w_bc_t, 0, 2 * STATES), chunks(xs[slot]), rows=2 * STATES)

            def project_dt(s, slot, m):
                pe.wait_ge(xs_done.sem, xs_done.at(s, INNER_CHUNKS))
                product(s, f"dt{m}", cols(w_dt_t, m * P), chunks(xs[slot]))

            def spread(s, slot, g, i):
                row = GROUP * g + i if i < GROUP else STATES + GROUP * g + i - GROUP
                product(s, wide_name(g, i), [picks[0:96, row, :]], [bc_parts[slot][0:96, :]])

            def spread_first(s, slot, _):
                pe.wait_ge(parts_done.sem, parts_done.at(s, 5))
                for i in range(2 * GROUP):
                    spread(s, slot, 0, i)

            def sum_states(s, slot, q):
                g, d = divmod(q, INNER_CHUNKS)
                if g == 0 and not (isinstance(s, int) and s == 0):
                    pe.wait_ge(skip_done.sem, skip_done.at(s - 1, d + 1))
                cmul_wait(pe, s, q)
                for j in range(GROUP):
                    last = nc.tensor.matmul(y_sum[d][:], ident[:], state[q % STATE_SLOTS][:, j, :],
                                            start=(g == 0 and j == 0), stop=(g == GROUPS - 1 and j == GROUP - 1))
                last.then_inc(sum_done.sem, 1)

            def project_out(s, slot, m):
                pe.wait_ge(gated_done.sem, gated_done.at(s, INNER_CHUNKS))
                product(s, f"out{m}", cols(w_out_t, m * P), chunks(yv[slot]))

            def mean_tail(s, slot, _):
                pe.wait_ge(x1_done.sem, x1_done.at(s, CHUNKS))
                product(s, "mean2", means, chunks(x1_t))

            def var_tail(s, slot, _):
                pe.wait_ge(sq2_done.sem, sq2_done.at(s, 1))
                product(s, "var2", means, chunks(sq2))

            pipeline(pe, {"xT": turn_input, "mean1": mean_head, "var1": var_head, "xs": project_x, "z": project_z, "bc": project_bc,
                          "dt": project_dt, "first": spread_first, "wide": spread, "sum": sum_states, "last": sum_states,
                          "out": project_out, "mean2": mean_tail, "var2": var_tail})

        @block.scalar
        def _(act):
            def deviation(s, name, to, read, ln, done):
                act.wait_ge(read.sem, read.at(s))
                work.wait_full(act, s, name)
                nc.scalar.activation(to[:], work.tile(name)[:], ACT.Ln, bias=ln_eps[:]).then_inc(ln.sem, 1)
                act.wait_ge(ln.sem, ln.at(s, 1))
                nc.scalar.activation(to[:], to[:], ACT.Exp, scale=-0.5).then_inc(done.sem, 1)

            def modulate(s, to, x, shift, scale, done):
                for c in range(CHUNKS):
                    nc.scalar.activation(to[:, c, :], x[:, c, :], ACT.Identity, bias=mod[:, 2 * shift + c, bass.ds(s, 1)],
                                         scale=mod[:, 2 * scale + c, bass.ds(s, 1)]).then_inc(done.sem, 1)

            def copy_input(s, slot, c):
                slot_free(act, s, x1_done)
                work.wait_full(act, s, f"xT{c}")
                nc.scalar.activation(x_t[slot][:, c, :], work.tile(f"xT{c}")[:], ACT.Copy).then_inc(x_t_done.sem, 1)

            def square_head(s, slot, _):
                act.wait_ge(xc_done.sem, xc_done.at(s, CHUNKS))
                nc.scalar.activation(sq[:], xc[:], ACT.Square).then_inc(sq_done.sem, 1)

            def deviation_head(s, slot, _):
                deviation(s, "var1", rstd, xn_done, ln_done, rstd_done)

            def modulate_head(s, slot, _):
                act.wait_ge(xn_done.sem, xn_done.at(s, 1))
                modulate(s, h_t, xc, MOD_SHIFT_A, MOD_SCALE_A, h_done)

            def copy_x(s, slot, m):
                slot_free(act, s, gated_done)
                work.wait_full(act, s, f"xs{m}")
                nc.scalar.activation(xs[slot][:, m, :], work.tile(f"xs{m}")[:], ACT.Copy).then_inc(xs_done.sem, 1)

            def copy_z(s, slot, m):
                slot_free(act, s, gated_done)
                work.wait_full(act, s, f"z{m}")
                nc.scalar.activation(sz[slot][:, m, :], work.tile(f"z{m}")[:], ACT.Copy).then_inc(z_done.sem, 1)

            def silu(s, slot, _):
                act.wait_ge(z_done.sem, z_done.at(s, INNER_CHUNKS))
                nc.scalar.activation(sz[slot][:], sz[slot][:], ACT.Silu).then_inc(silu_done.sem, 1)
                nc.scalar.preload_act_table_set(EXP_AND_LN)

            def softplus(s, slot, m):
                bias = b_dt[:, m:m + 1]
                act.wait_ge(dt_done.sem, dt_done.at(s, m))
                work.wait_full(act, s, f"dt{m}")
                nc.scalar.activation(sp_relu[:], work.tile(f"dt{m}")[:], ACT.Relu, bias=bias)
                nc.scalar.activation(sp_e[:], work.tile(f"dt{m}")[:], ACT.Abs, bias=bias).then_inc(abs_done.sem, 1)
                act.wait_ge(abs_done.sem, abs_done.at(s, m + 1))
                nc.scalar.activation(sp_e[:], sp_e[:], ACT.Exp, scale=-1.0).then_inc(exp_done.sem, 1)
                act.wait_ge(exp_done.sem, exp_done.at(s, m + 1))
                nc.scalar.activation(sp_ln[:], sp_e[:], ACT.Ln, bias=1.0).then_inc(log_done.sem, 1)

            def copy_wide(s, slot, g, i):
                if g >= 1:
                    before, units = s, INNER_CHUNKS * (g - 1)
                else:
                    before, units = s - 1, INNER_CHUNKS * (GROUPS - 1)
                if not (isinstance(s, int) and s == 0 and g < 1):
                    if i < GROUP:
                        act.wait_ge(input_done.sem, input_done.at(before, units))
                    else:
                        cmul_until(act, before, units)
                work.wait_full(act, s, wide_name(g, i))
                done, n = wide_signal(i)
                to = b_wide if i < GROUP else c_wide
                nc.scalar.activation(to[g % 2][:, n, :], work.tile(wide_name(g, i))[:], ACT.Copy).then_inc(done.sem, 1)

            def copy_first(s, slot, _):
                for i in range(2 * GROUP):
                    copy_wide(s, slot, 0, i)

            def decays(s, slot, q):
                for k in (0, 1, 2) if q == 0 else (q + 2,) if q + 2 < UNITS else ():
                    g, d = divmod(k, INNER_CHUNKS)
                    act.wait_ge(dt_done.sem, dt_done.at(s, INNER_CHUNKS))
                    unit_slot_free(act, s, k, DECAY_SLOTS, scan_done)
                    for j in range(GROUP):
                        n = GROUP * g + j
                        last = nc.scalar.activation(decay[k % DECAY_SLOTS][:, j, 1:SEQ], dt[slot][:, d, 1:SEQ], ACT.Exp,
                                                    scale=neg_a[:, d, n:n + 1])
                    last.then_inc(decay_done.sem, 1)

            def square_tail(s, slot, _):
                act.wait_ge(stored.sem, stored.at(s))
                act.wait_ge(xc2_done.sem, xc2_done.at(s, CHUNKS))
                nc.scalar.activation(sq2[:], xc2[:], ACT.Square).then_inc(sq2_done.sem, 1)

            def deviation_tail(s, slot, _):
                deviation(s, "var2", rstd2, xn2_done, ln2_done, rstd2_done)

            def modulate_tail(s, slot, _):
                act.wait_ge(xn2_done.sem, xn2_done.at(s, 1))
                modulate(s, h2_t, xc2, MOD_SHIFT_B, MOD_SCALE_B, h2_done)

            nc.scalar.preload_act_table_set(EXP_AND_LN)
            pipeline(act, {"xcopy": copy_input, "sq1": square_head, "dev1": deviation_head, "h1": modulate_head, "xscopy": copy_x, "zcopy": copy_z,
                           "silu": silu, "soft": softplus, "first": copy_first, "wide": copy_wide, "unit": decays,
                           "sq2": square_tail, "dev2": deviation_tail, "h2": modulate_tail})

        @block.vector
        def _(dve):
            def centre(s, name, to, source, read, done):
                dve.wait_ge(read.sem, read.at(s))
                work.wait_full(dve, s, name)
                for c in range(CHUNKS):
                    nc.vector.tensor_tensor(to[:, c, :], source[:, c, :], work.tile(name)[:], ALU.subtract).then_inc(done.sem, 1)

            def normalise(s, x, rate, rate_done, squared, done):
                dve.wait_ge(rate_done.sem, rate_done.at(s, 1))
                dve.wait_ge(squared.sem, squared.at(s, 1))
                nc.vector.tensor_tensor(x[:], x[:], rate[:].unsqueeze(1).to_broadcast([P, CHUNKS, SEQ]), ALU.mult)\
                    .then_inc(done.sem, 1)

            def centre_head(s, slot, _):
                centre(s, "mean1", xc, x_t[slot], h_done, xc_done)

            def normalise_head(s, slot, _):
                normalise(s, xc, rstd, rstd_done, sq_done, xn_done)

            def cut_bc(s, slot, _):
                parts = bc_parts[slot]
                slot_free(dve, s, c_wide_done)
                work.wait_full(dve, s, "bc")
                bc = work.tile("bc")[0:2 * STATES, :]
                nc.vector.tensor_copy(parts[0:32, :], bc).then_inc(parts_done.sem, 1)
                dve.wait_ge(parts_done.sem, parts_done.at(s, 1))
                nc.vector.tensor_tensor(bc_rest, bc, parts[0:32, :], ALU.subtract).then_inc(parts_done.sem, 1)
                dve.wait_ge(parts_done.sem, parts_done.at(s, 2))
                nc.vector.tensor_copy(bc_mid[:], bc_rest).then_inc(parts_done.sem, 1)
                nc.vector.tensor_copy(parts[32:64, :], bc_rest).then_inc(parts_done.sem, 1)
                dve.wait_ge(parts_done.sem, parts_done.at(s, 3))
                nc.vector.tensor_tensor(parts[64:96, :], bc_rest, bc_mid[:], ALU.subtract).then_inc(parts_done.sem, 1)

            def step_size(s, slot, m):
                def step(k):
                    dve.wait_ge(series_done.sem, series_done.at(s, 6 * m + k))

                if m == 0:
                    slot_free(dve, s, x1_done)
                    dve.wait_ge(parts_done.sem, parts_done.at(s, 5))
                dve.wait_ge(exp_done.sem, exp_done.at(s, m + 1))
                nc.vector.tensor_scalar(sp_mask[:], sp_e[:], SERIES_BELOW, None, ALU.is_gt).then_inc(series_done.sem, 1)
                nc.vector.tensor_scalar(sp_p[:], sp_e[:], -0.25, 1.0 / 3, ALU.mult, ALU.add).then_inc(series_done.sem, 1)
                step(2)
                nc.vector.tensor_tensor(sp_p[:], sp_p[:], sp_e[:], ALU.mult).then_inc(series_done.sem, 1)
                step(3)
                nc.vector.scalar_tensor_tensor(sp_p[:], sp_p[:], -0.5, sp_e[:], ALU.add, ALU.mult).then_inc(series_done.sem, 1)
                step(4)
                nc.vector.scalar_tensor_tensor(sp_p[:], sp_p[:], 1.0, sp_e[:], ALU.add, ALU.mult).then_inc(series_done.sem, 1)
                step(5)
                dve.wait_ge(log_done.sem, log_done.at(s, m + 1))
                nc.vector.memset(waiter[:, m:m + 1], 0.0)
                nc.vector.copy_predicated(sp_p[:], sp_mask[:], sp_ln[:]).then_inc(series_done.sem, 1)
                step(6)
                nc.vector.tensor_tensor(dt[slot][:, m, :], sp_p[:], sp_relu[:], ALU.add).then_inc(dt_done.sem, 1)
                dve.wait_ge(dt_done.sem, dt_done.at(s, m + 1))
                dve.wait_ge(xs_done.sem, xs_done.at(s, INNER_CHUNKS))
                nc.vector.tensor_tensor(u[slot][:, m, :], dt[slot][:, m, :], xs[slot][:, m, :], ALU.mult).then_inc(u_done.sem, 1)

            def scan_input(s, slot, q):
                g, d = divmod(q, INNER_CHUNKS)
                dve.wait_ge(u_done.sem, u_done.at(s, INNER_CHUNKS))
                dve.wait_ge(b_wide_done.sem, b_wide_done.at(s, GROUP * (g + 1)))
                unit_slot_free(dve, s, q, STATE_SLOTS, sum_done)
                nc.vector.tensor_tensor(state[q % STATE_SLOTS][:], u[slot][:, d, :].unsqueeze(1).to_broadcast([P, GROUP, SEQ]),
                                        b_wide[g % 2][:], ALU.mult).then_inc(input_done.sem, 1)

            def scan(s, slot, q):
                g, d = divmod(q, INNER_CHUNKS)
                for k in (0, 1) if q == 0 else (q + 1,) if q + 1 < UNITS else ():
                    scan_input(s, slot, k)
                dve.wait_ge(decay_done.sem, decay_done.at(s, q + 1))
                dve.wait_ge(input_done.sem, input_done.at(s, q + 1))
                h = state[q % STATE_SLOTS]
                flat = h[:].rearrange("p g s -> p (g s)")
                nc.vector.tensor_tensor_scan(flat, decay[q % DECAY_SLOTS][:].rearrange("p g s -> p (g s)"), flat, 0.0,
                                             ALU.mult, ALU.add).then_inc(scan_done.sem, 1)
                if q in on_vector:
                    dve.wait_ge(scan_done.sem, scan_done.at(s, q + 1))
                    dve.wait_ge(c_wide_done.sem, c_wide_done.at(s, GROUP * (g + 1)))
                    nc.vector.tensor_tensor(h[:], h[:], c_wide[g % 2][:], ALU.mult).then_inc(cmul_vec_done.sem, 1)

            def gate(s, slot, d):
                dve.wait_ge(sum_done.sem, sum_done.at(s, UNITS - INNER_CHUNKS + d + 1))
                dve.wait_ge(silu_done.sem, silu_done.at(s, 1))
                nc.vector.scalar_tensor_tensor(yv[slot][:, d, :], xs[slot][:, d, :], skip_d[:, d:d + 1], y_sum[d][:],
                                               ALU.mult, ALU.add).then_inc(skip_done.sem, 1)
                dve.wait_ge(skip_done.sem, skip_done.at(s, d + 1))
                nc.vector.tensor_tensor(yv[slot][:, d, :], yv[slot][:, d, :], sz[slot][:, d, :], ALU.mult).then_inc(gated_done.sem, 1)

            def residual(s, slot, m):
                dve.wait_ge(stored.sem, stored.at(s))
                work.wait_full(dve, s, f"out{m}")
                nc.vector.scalar_tensor_tensor(x1_t[:, m, :], work.tile(f"out{m}")[:], mod[:, 2 * MOD_GATE_A + m, bass.ds(s, 1)],
                                               x_t[slot][:, m, :], ALU.mult, ALU.add).then_inc(x1_done.sem, 1)

            def centre_tail(s, slot, _):
                centre(s, "mean2", xc2, x1_t, h2_done, xc2_done)

            def normalise_tail(s, slot, _):
                normalise(s, xc2, rstd2, rstd2_done, sq2_done, xn2_done)

            pipeline(dve, {"cen1": centre_head, "xn1": normalise_head, "cut": cut_bc, "step": step_size, "unit": scan,
                           "gate": gate, "res": residual, "cen2": centre_tail, "xn2": normalise_tail})

        @block.gpsimd
        def _(pool):
            def times_c(s, slot, q):
                if q in on_pool:
                    g = q // INNER_CHUNKS
                    pool.wait_ge(c_wide_done.sem, c_wide_done.at(s, GROUP * (g + 1)))
                    pool.wait_ge(scan_done.sem, scan_done.at(s, q + 1))
                    h = state[q % STATE_SLOTS]
                    nc.gpsimd.tensor_tensor(h[:], h[:], c_wide[g % 2][:], ALU.mult).then_inc(cmul_pool_done.sem, 1)

            pipeline(pool, {"unit": times_c})


STAGE = {"pq": 1, "pk": 1, "psq": 1, "pss": 1, "prate": 1, "pnorm": 1, "prot": 1, "padd": 1, "ptr": 1, "ptc": 1, "v": 1, "vc": 1,
         "score": 2, "mask": 2, "exp": 2, "pt": 2, "att": 2, "onorm": 2, "ot": 2, "otc": 2,
         "wo": 3, "add": 3, "mean": 3, "cen": 3, "sq": 3, "var": 3, "dev": 3, "xn": 3, "hn": 3, "ga": 3, "gelu": 3, "gated": 3,
         "wd": 3, "fin": 3}
LEAD = {1: 1, 2: 0, 3: -1}
ORDER = """
wo:0 score:0.0 mask:0.0 add:0 wo:1 score:0.1 mask:0.1 add:1 pq:0 pk:0 exp:0 mean:0 psq:0 cen:0 score:1.0 mask:1.0 sq:0 pss:0 pt:0.0 prate:0 pt:0.1
score:1.1 mask:1.1 pnorm:0 var:0 dev:0 prot:0 v:0 vc:0 att:0 xn:0 exp:1 onorm:0 padd:0 hn:0 ptr:0 ot:0 pq:1 pk:1 ptc:0 otc:0 psq:1
score:2.0 mask:2.0 pss:1 pt:1.0 pt:1.1 prate:1 score:2.1 mask:2.1 pnorm:1 pt:1.2 pt:1.3 prot:1 v:1 vc:1 exp:2 att:1 padd:1 onorm:1
ptr:1 ot:1 pq:2 pk:2 ptc:1 otc:1 psq:2
score:3.0 mask:3.0 pss:2 pt:2.0 pt:2.1 prate:2 score:3.1 mask:3.1 pnorm:2 pt:2.2 pt:2.3 prot:2 v:2 vc:2 exp:3 att:2 padd:2 onorm:2
ptr:2 ot:2 pq:3 pk:3 ptc:2 otc:2 psq:3
ga:0 pss:3 prate:3 gelu:0 pt:3.0 pnorm:3 pt:3.1 gated:0 ga:1 prot:3 pt:3.2 pt:3.3 gelu:1 v:3 gated:1 ga:2 vc:3 padd:3 gelu:2 att:3
gated:2 ga:3 ptr:3 onorm:3 gelu:3 ptc:3 gated:3 ga:4 ot:3 otc:3 gelu:4 gated:4 ga:5 gelu:5 gated:5 wd:0 wd:1 fin:0 fin:1
"""
SCHEDULE = steps_of(ORDER)


def stack_pass(nc, inp, stack_dram):
    SEQS = DEPTH * BATCH
    with ExitStack() as ctx:
        def sb(name, shape, dt=F32):
            return ctx.enter_context(nc.sbuf_tensor("b_" + name, shape, dt))

        def sem(name):
            return ctx.enter_context(nc.semaphore("b_" + name))

        signals = []

        def signal(name, per_pass, unit=1):
            signals.append(Signal(sem(name), per_pass, unit))
            return signals[-1]

        banks_all = [ctx.enter_context(nc.psum_tensor(f"b_bank{i}", [P, 512], F32)) for i in range(8)]
        s_banks = banks_all[4:6]

        squares = sb("squares", [P, 4, P])
        ident, mean_mat = (squares[:, i, :] for i in range(2))
        mask = squares[:, 2:4, :].rearrange("p a b -> p (a b)")
        w_qkv = sb("w_qkv", [P, CHUNKS, 3 * INNER])
        w_o = sb("w_o", [P, PAIRS, DIM])
        w_1 = sb("w_1", [P, CHUNKS, 2 * HID])
        w_2 = sb("w_2", [P, HID_CHUNKS, DIM])
        rotary = [sb(f"rotary{l}", [P, TILES, 2, 2, DIM_HEAD]) for l in range(DEPTH)]
        ln_g = sb("ln_g", [P, SEQS, CHUNKS])
        ln_b = sb("ln_b", [P, SEQS, CHUNKS])
        b_1a = sb("b_1a", [P, SEQS, HID_CHUNKS])
        b_1g = sb("b_1g", [P, SEQS, HID_CHUNKS])
        b_2 = sb("b_2", [P, SEQS, CHUNKS])
        eps_bias = sb("eps_bias", [P, 1])
        norm_bias = sb("norm_bias", [P, 1])
        waiter = sb("waiter", [P, TILES * PAIRS])

        hx = sb("hx", [P, CHUNKS, SEQ + 1])
        qk_sq = sb("qk_sq", [P, 2, INNER])
        qk_rate = sb("qk_rate", [P, 2, HEADS])
        qk = sb("qk", [P, 2, INNER])
        by_cos = sb("by_cos", [P, 2, INNER])
        qk_rot = sb("qk_rot", [P, 2, INNER])
        q_t = [sb(f"q_t{i}", [P, PAIRS, SEQ]) for i in range(2)]
        k_t = [sb(f"k_t{i}", [P, PAIRS, SEQ]) for i in range(2)]
        v = [sb(f"v{i}", [P, TILES, INNER]) for i in range(2)]
        scores = [sb(f"scores{i}", [P, HEADS, 2 * WINDOW]) for i in range(2)]
        probs_t = [sb(f"probs_t{i}", [P, 2 * HEADS, WINDOW]) for i in range(2)]
        row_max = sb("row_max", [P, TILES, HEADS])
        row_bias = sb("row_bias", [P, TILES, HEADS])
        row_sum = sb("row_sum", [P, TILES, HEADS])
        row_rate = sb("row_rate", [P, TILES, HEADS])
        o = [sb(f"o{i}", [P, INNER]) for i in range(2)]
        o_t = sb("o_t", [P, PAIRS, SEQ])
        x_res = sb("x_res", [P, CHUNKS, SEQ])
        x2 = sb("x2", [P, CHUNKS, SEQ + 1])
        xc = sb("xc", [P, CHUNKS, SEQ])
        rstd = sb("rstd", [P, SEQ])
        hn = sb("hn", [P, CHUNKS, SEQ])
        gelu = [sb(f"gelu{i}", [P, SEQ]) for i in range(2)]
        h2 = sb("h2", [P, HID_CHUNKS, SEQ])
        sq = h2[:, 0:CHUNKS, :]
        x_out = sb("x_out", [P, CHUNKS, SEQ])

        def shifted(x, c):
            return x[:, c, 0:SEQ]

        def plain(x, c):
            return x[:, c, c:c + SEQ]

        def by_head(x):
            return x[:].rearrange("p x (h d) -> p x h d", d=DIM_HEAD)

        def for_heads(table, width):
            return table.unsqueeze(2).to_broadcast([P, 2, HEADS, width])

        def hid_rows(m):
            return min(P, HID - m * P)

        hx_loaded = signal("hx_loaded", CHUNKS, 16)
        qk_sq_done = signal("qk_sq_done", 2 * TILES)
        qk_sum_done = signal("qk_sum_done", TILES)
        qk_floor_done = signal("qk_floor_done", TILES)
        qk_ln_done = signal("qk_ln_done", TILES)
        qk_rate_done = signal("qk_rate_done", TILES)
        qk_done = signal("qk_done", 2 * TILES)
        by_cos_done = signal("by_cos_done", TILES)
        by_sin_done = signal("by_sin_done", 2 * TILES)
        qk_rot_done = signal("qk_rot_done", TILES)
        q_t_done = signal("q_t_done", TILES)
        k_t_done = signal("k_t_done", TILES)
        v_done = signal("v_done", TILES)
        masked_done = signal("masked_done", TILES * PAIRS)
        row_bias_done = signal("row_bias_done", TILES)
        probs_done = signal("probs_done", TILES * PAIRS)
        row_rate_done = signal("row_rate_done", TILES)
        o_done = signal("o_done", TILES)
        o_t_done = signal("o_t_done", TILES)
        turn_uses = [(w, i) for w in range(TILES) for i in range(4 if w else 2)]
        on_act = [x for n, x in enumerate(turn_uses) if n % 2 == 0]
        on_dve = [x for n, x in enumerate(turn_uses) if n % 2 == 1]
        probs_t_act = signal("probs_t_act", len(on_act))
        probs_t_dve = signal("probs_t_dve", len(on_dve))
        x_res_loaded = signal("x_res_loaded", 1, 16)
        x2_done = signal("x2_done", CHUNKS)
        xc_done = signal("xc_done", CHUNKS)
        sq_done = signal("sq_done", 1)
        ln_done = signal("ln_done", 1)
        rstd_done = signal("rstd_done", 1)
        xn_done = signal("xn_done", 1)
        hn_done = signal("hn_done", CHUNKS)
        gelu_done = signal("gelu_done", HID_CHUNKS)
        h2_done = signal("h2_done", HID_CHUNKS)
        x_out_done = signal("x_out_done", CHUNKS)
        stored = signal("stored", 1, 16)
        const_loaded, qkv_loaded, mlp_loaded = sem("const_loaded"), sem("qkv_loaded"), sem("mlp_loaded")

        def probs_t_signal(w, i):
            return (probs_t_act, on_act.index((w, i)) + 1) if (w, i) in on_act else (probs_t_dve, on_dve.index((w, i)) + 1)

        def probs_t_until(w):
            return (sum(1 for x in on_act if x[0] <= w), sum(1 for x in on_dve if x[0] <= w))

        uses, next_bank = [], {1: 0, 2: 6, 3: 2}

        def use_next(stage, name, reader, k):
            uses.append((name, next_bank[stage], reader, k))
            next_bank[stage] ^= 1

        for name, k, *i in SCHEDULE:
            if name in ("pq", "pk"):
                use_next(1, f"{name[1]}{k}", qk_done, 2 * k + (1 if name == "pq" else 2))
            elif name == "ptr":
                use_next(1, f"q_t{k}", q_t_done, k + 1)
                use_next(1, f"k_t{k}", k_t_done, k + 1)
            elif name == "v":
                use_next(1, f"v{k}", v_done, k + 1)
            elif name == "wo":
                use_next(3, f"wo{k}", x2_done, k + 1)
            elif name == "mean":
                use_next(3, "mean", xc_done, CHUNKS)
            elif name == "var":
                use_next(3, "var", ln_done, 1)
            elif name == "ga":
                use_next(3, f"g{k}", gelu_done, k + 1)
                use_next(3, f"a{k}", h2_done, k + 1)
            elif name == "wd":
                use_next(3, f"wd{k}", x_out_done, k + 1)
            elif name == "score":
                g = i[0]
                uses += [(f"s{k}_{g}_{h}", 4 + h, masked_done, PAIRS * k + 2 * g + h + 1) for h in range(2)]
            elif name == "pt":
                use_next(2, f"pt{k}_{i[0]}", *probs_t_signal(k, i[0]))
            elif name == "ot":
                use_next(2, f"ot{k}", o_t_done, k + 1)
            elif name == "att":
                use_next(2, f"o{k}", o_done, k + 1)
        psum = Banks(banks_all, [sem(f"full{i}") for i in range(8)], uses)

        def blocks_of(w, i):
            return [(2 * i + h, blk) for h in range(2) for blk in range(2)] if w else [(4 * i + h, 1) for h in range(4)]

        def keys_of(w):
            return (0, 2 * WINDOW) if w else (WINDOW, 2 * WINDOW)

        def pipeline(eng, steps):
            def one_pass(i, parity, stages, layer):
                for name, *at in SCHEDULE:
                    stage, lead = STAGE[name], LEAD[STAGE[name]]
                    if stage in stages and name in steps:
                        of = [layer] if stage == 1 else []
                        steps[name](i + lead, (parity + lead) % 2, *of, *at)

            one_pass(-1, 1, (1,), 0)
            one_pass(0, 0, (1, 2), 0)
            for layer, (first, end) in enumerate(((1, BATCH - 1), (BATCH - 1, SEQS - 1))):
                with eng.Fori(first // 2, end // 2) as j:
                    one_pass(2 * j + 1, 1, (1, 2, 3), layer)
                    one_pass(2 * j + 2, 0, (1, 2, 3), layer)
            one_pass(SEQS - 1, 1, (2, 3), DEPTH - 1)
            one_pass(SEQS, 0, (3,), DEPTH - 1)

        load_stack_vectors(nc, inp, squares, rotary, ln_g, ln_b, b_1a, b_1g, b_2)
        with nc.Block() as block:
            @block.vector
            def _(dve):
                nc.vector.memset(eps_bias[:], LN_EPS)
                nc.vector.memset(norm_bias[:], 0.5 * float(np.log(SCREEN)))
                nc.vector.memset(hx[:, 1, 0:1], 0.0)
                nc.vector.memset(x2[:, 1, 0:1], 0.0)
                nc.vector.memset(row_sum[:], 0.0)

        start_signals(nc, signals)
        block = ctx.enter_context(nc.Block())

        @block.sync
        def _(sp):
            def load_qkv(l):
                sp.dma_start(w_qkv[:], inp["L0_ffn_wqkv"][l].rearrange("(c p) f -> p c f", p=P)).then_inc(qkv_loaded, 16)
                sp.wait_ge(qkv_loaded, 16 * (l + 1))

            def load_mlp(l):
                whole = HID // P
                sp.dma_start(w_o[:], inp["L0_ffn_wo"][l].rearrange("(c p) f -> p c f", p=P)).then_inc(mlp_loaded, 16)
                sp.dma_start(w_1[:], inp["L0_ffn_w1"][l].rearrange("(c p) f -> p c f", p=P)).then_inc(mlp_loaded, 16)
                sp.dma_start(w_2[:, 0:whole, :], inp["L0_ffn_w2"][l, 0:whole * P].rearrange("(c p) f -> p c f", p=P))\
                    .then_inc(mlp_loaded, 16)
                sp.dma_start(w_2[0:HID - whole * P, whole, :], inp["L0_ffn_w2"][l, whole * P:HID]).then_inc(mlp_loaded, 16)
                sp.wait_ge(mlp_loaded, 16 * 4 * (l + 1))

            def load_hx(s):
                sp.wait_ge(v_done.sem, v_done.at(s))
                for c in range(CHUNKS):
                    sp.dma_start(plain(hx, c), stack_dram[s, :, c, :]).then_inc(hx_loaded.sem, 16)

            def load_res(s):
                sp.wait_ge(x2_done.sem, x2_done.at(s))
                sp.dma_start(x_res[:], stack_dram[s]).then_inc(x_res_loaded.sem, 16)

            def store(s):
                sp.wait_ge(x_out_done.sem, x_out_done.at(s, CHUNKS))
                sp.dma_start(stack_dram[s + BATCH], x_out[:]).then_inc(stored.sem, 16)

            load_qkv(0)
            load_hx(0)
            load_mlp(0)
            load_hx(1)
            load_res(0)
            load_hx(2)
            with sp.Fori(1, BATCH - 2) as i:
                load_res(i)
                load_hx(i + 2)
                store(i - 1)
            load_res(BATCH - 2)
            sp.wait_ge(v_done.sem, v_done.at(BATCH))
            load_qkv(1)
            sp.wait_ge(stored.sem, stored.at(1))
            load_hx(BATCH)
            store(BATCH - 3)
            load_res(BATCH - 1)
            sp.wait_ge(stored.sem, stored.at(2))
            load_hx(BATCH + 1)
            store(BATCH - 2)
            sp.wait_ge(stored.sem, stored.at(3))
            load_hx(BATCH + 2)
            store(BATCH - 1)
            load_mlp(1)
            load_res(BATCH)
            with sp.Fori(BATCH + 1, SEQS - 2) as i:
                load_res(i)
                sp.wait_ge(stored.sem, stored.at(i + 3 - BATCH))
                load_hx(i + 2)
                store(i - 1)
            for i in range(SEQS - 2, SEQS):
                load_res(i)
                store(i - 1)
            store(SEQS - 1)
            sp.wait_ge(stored.sem, stored.at(SEQS))

        @block.tensor
        def _(pe):
            def product(s, name, weights, cols, sources, rows=P):
                psum.wait_free(pe, s, name)
                for c, source in enumerate(sources):
                    last = nc.tensor.matmul(psum.tile(name)[0:rows, :], weights[0:source.shape[0], c, cols:cols + rows], source,
                                            start=(c == 0), stop=(c == len(sources) - 1))
                psum.filled(last, name)

            def by_token(s, name, w, cols):
                psum.wait_free(pe, s, name)
                for c in range(CHUNKS):
                    last = nc.tensor.matmul(psum.tile(name)[:], hx[:, c, w * P:(w + 1) * P], w_qkv[:, c, cols:cols + INNER],
                                            start=(c == 0), stop=(c == CHUNKS - 1))
                psum.filled(last, name)

            def project_q(s, slot, layer, w):
                if w == 0:
                    pe.wait_ge(hx_loaded.sem, hx_loaded.at(s, CHUNKS))
                by_token(s, f"q{w}", w, 0)

            def project_k(s, slot, layer, w):
                by_token(s, f"k{w}", w, INNER)

            def turn_qk(s, slot, layer, w):
                pe.wait_ge(qk_rot_done.sem, qk_rot_done.at(s, w + 1))
                for i, stem in enumerate("qk"):
                    psum.wait_free(pe, s, f"{stem}_t{w}")
                    for p in range(PAIRS):
                        last = nc.tensor.transpose(psum.tile(f"{stem}_t{w}")[:, p * P:(p + 1) * P],
                                                   qk_rot[:, i, p * P:(p + 1) * P], ident)
                    psum.filled(last, f"{stem}_t{w}")

            def values(s, slot, layer, w):
                by_token(s, f"v{w}", w, 2 * INNER)

            def score(s, slot, w, g):
                lo, hi = keys_of(w)
                if w == 0 and g == 0:
                    pe.wait_ge(q_t_done.sem, q_t_done.at(s, TILES))
                    pe.wait_ge(k_t_done.sem, k_t_done.at(s, TILES))
                first = w * WINDOW - (WINDOW - lo)
                for h in range(2):
                    psum.wait_free(pe, s, f"s{w}_{g}_{h}")
                for n in range(2):
                    for h in range(2):
                        at, p = slice(h * DIM_HEAD, (h + 1) * DIM_HEAD), 2 * g + n
                        last = nc.tensor.matmul(s_banks[h][:, n * 2 * WINDOW + lo:n * 2 * WINDOW + hi],
                                                q_t[slot][at, p, w * WINDOW:(w + 1) * WINDOW],
                                                k_t[slot][at, p, first:first + hi - lo], start=True, stop=True)
                        if n:
                            psum.filled(last, f"s{w}_{g}_{h}")

            def turn_probs(s, slot, w, i):
                name, blocks = f"pt{w}_{i}", blocks_of(w, i)
                psum.wait_free(pe, s, name)
                pe.wait_ge(probs_done.sem, probs_done.at(s, PAIRS * w + blocks[-1][0] // 2 + 1))
                for n, (h, blk) in enumerate(blocks):
                    last = nc.tensor.transpose(psum.tile(name)[:, n * P:(n + 1) * P],
                                               scores[w % 2][:, h, blk * WINDOW:(blk + 1) * WINDOW], ident)
                psum.filled(last, name)

            def attend(s, slot, w):
                by_act, by_dve = probs_t_until(w)
                pe.wait_ge(probs_t_act.sem, probs_t_act.at(s, by_act))
                pe.wait_ge(probs_t_dve.sem, probs_t_dve.at(s, by_dve))
                if w == 0:
                    pe.wait_ge(v_done.sem, v_done.at(s, TILES))
                psum.wait_free(pe, s, f"o{w}")
                for h in range(HEADS):
                    blocks = (0, 1) if w else (1,)
                    for blk in blocks:
                        last = nc.tensor.matmul(psum.tile(f"o{w}")[:, h * DIM_HEAD:(h + 1) * DIM_HEAD], probs_t[w % 2][:, 2 * h + blk, :],
                                                v[slot][:, w - 1 + blk, h * DIM_HEAD:(h + 1) * DIM_HEAD],
                                                start=(blk == blocks[0]), stop=(blk == 1))
                psum.filled(last, f"o{w}")

            def turn_output(s, slot, w):
                pe.wait_ge(o_done.sem, o_done.at(s, w + 1))
                psum.wait_free(pe, s, f"ot{w}")
                for p in range(PAIRS):
                    last = nc.tensor.transpose(psum.tile(f"ot{w}")[:, p * P:(p + 1) * P], o[w % 2][:, p * P:(p + 1) * P], ident)
                psum.filled(last, f"ot{w}")

            def project_out(s, slot, m):
                if m == 0:
                    pe.wait_ge(o_t_done.sem, o_t_done.at(s, TILES))
                    pe.wait_ge(x_res_loaded.sem, x_res_loaded.at(s, 1))
                product(s, f"wo{m}", w_o, m * P, [o_t[:, p, :] for p in range(PAIRS)])

            def mean(s, slot, _):
                pe.wait_ge(x2_done.sem, x2_done.at(s, CHUNKS))
                psum.wait_free(pe, s, "mean")
                for c in range(CHUNKS):
                    last = nc.tensor.matmul(psum.tile("mean")[:], mean_mat, shifted(x2, c), start=(c == 0), stop=(c == CHUNKS - 1))
                psum.filled(last, "mean")

            def var(s, slot, _):
                pe.wait_ge(sq_done.sem, sq_done.at(s, 1))
                psum.wait_free(pe, s, "var")
                for c in range(CHUNKS):
                    last = nc.tensor.matmul(psum.tile("var")[:], mean_mat, sq[:, c, :], start=(c == 0), stop=(c == CHUNKS - 1))
                psum.filled(last, "var")

            def gate_and_value(s, slot, m):
                if m == 0:
                    pe.wait_ge(hn_done.sem, hn_done.at(s, CHUNKS))
                for stem, at in (("g", HID), ("a", 0)):
                    product(s, f"{stem}{m}", w_1, at + m * P, [hn[:, c, :] for c in range(CHUNKS)], rows=hid_rows(m))

            def project_down(s, slot, m):
                psum.wait_free(pe, s, f"wd{m}")
                for k in range(HID_CHUNKS):
                    pe.wait_ge(h2_done.sem, h2_done.at(s, k + 1))
                    last = nc.tensor.matmul(psum.tile(f"wd{m}")[:], w_2[0:hid_rows(k), k, m * P:(m + 1) * P],
                                            h2[0:hid_rows(k), k, :], start=(k == 0), stop=(k == HID_CHUNKS - 1))
                psum.filled(last, f"wd{m}")

            pipeline(pe, {"pq": project_q, "pk": project_k, "ptr": turn_qk, "v": values, "score": score, "pt": turn_probs,
                          "att": attend, "ot": turn_output, "wo": project_out, "mean": mean, "var": var,
                          "ga": gate_and_value, "wd": project_down})

        @block.scalar
        def _(act):
            def square_qk(s, slot, layer, w):
                act.wait_ge(qk_sum_done.sem, qk_sum_done.at(s, w))
                for i, stem in enumerate("qk"):
                    psum.wait_full(act, s, f"{stem}{w}")
                    nc.scalar.activation(qk_sq[:, i, :], psum.tile(f"{stem}{w}")[:], ACT.Square).then_inc(qk_sq_done.sem, 1)

            def rate_qk(s, slot, layer, w):
                act.wait_ge(qk_floor_done.sem, qk_floor_done.at(s, w + 1))
                nc.scalar.activation(qk_rate[:], qk_rate[:], ACT.Ln, scale=SCREEN).then_inc(qk_ln_done.sem, 1)
                act.wait_ge(qk_ln_done.sem, qk_ln_done.at(s, w + 1))
                nc.scalar.activation(qk_rate[:], qk_rate[:], ACT.Exp, scale=-0.5, bias=norm_bias[:]).then_inc(qk_rate_done.sem, 1)

            def copy_q(s, slot, layer, w):
                psum.wait_full(act, s, f"q_t{w}")
                nc.scalar.activation(q_t[slot][:, :, w * P:(w + 1) * P],
                                     psum.tile(f"q_t{w}")[:].rearrange("p (n c) -> p n c", c=P), ACT.Copy).then_inc(q_t_done.sem, 1)

            def values(s, slot, layer, t):
                psum.wait_full(act, s, f"v{t}")
                nc.scalar.activation(v[slot][:, t, :], psum.tile(f"v{t}")[:], ACT.Copy).then_inc(v_done.sem, 1)

            def exponentials(s, slot, w):
                lo, hi = keys_of(w)
                act.wait_ge(row_bias_done.sem, row_bias_done.at(s, w + 1))
                for h in range(HEADS):
                    e = nc.scalar.activation(scores[w % 2][:, h, lo:hi], scores[w % 2][:, h, lo:hi], ACT.Exp,
                                             bias=row_bias[:, w, h:h + 1], accum_out=row_sum[:, w, h:h + 1])
                    if h % 2:
                        e.then_inc(probs_done.sem, 1)

            def copy_turned(s, slot, w, i):
                if (w, i) in on_act:
                    name = f"pt{w}_{i}"
                    psum.wait_full(act, s, name)
                    act.wait_ge(o_done.sem, o_done.at(s, max(w - 1, 0)))
                    to = probs_t[w % 2][:, 4 * i:4 * i + 4, :] if w else probs_t[0][:, 8 * i + 1:8 * i + 8:2, :]
                    nc.scalar.activation(to, psum.tile(name)[:].rearrange("p (n c) -> p n c", c=P), ACT.Copy)\
                        .then_inc(probs_t_act.sem, 1)

            def copy_output(s, slot, w):
                psum.wait_full(act, s, f"ot{w}")
                act.wait_ge(x2_done.sem, x2_done.at(s))
                nc.scalar.activation(o_t[:, :, w * WINDOW:(w + 1) * WINDOW],
                                     psum.tile(f"ot{w}")[:].rearrange("p (n c) -> p n c", c=P), ACT.Copy).then_inc(o_t_done.sem, 1)

            def square(s, slot, _):
                act.wait_ge(x_out_done.sem, x_out_done.at(s))
                act.wait_ge(xc_done.sem, xc_done.at(s, CHUNKS))
                nc.scalar.activation(sq, xc[:], ACT.Square).then_inc(sq_done.sem, 1)

            def deviation(s, slot, _):
                act.wait_ge(xn_done.sem, xn_done.at(s))
                psum.wait_full(act, s, "var")
                nc.scalar.activation(rstd[:], psum.tile("var")[:], ACT.Ln, bias=eps_bias[:]).then_inc(ln_done.sem, 1)
                act.wait_ge(ln_done.sem, ln_done.at(s, 1))
                nc.scalar.activation(rstd[:], rstd[:], ACT.Exp, scale=-0.5).then_inc(rstd_done.sem, 1)

            def affine(s, slot, _):
                act.wait_ge(h2_done.sem, h2_done.at(s))
                act.wait_ge(xn_done.sem, xn_done.at(s, 1))
                for c in range(CHUNKS):
                    nc.scalar.activation(hn[:, c, :], xc[:, c, :], ACT.Identity, scale=ln_g[:, bass.ds(s, 1), c],
                                         bias=ln_b[:, bass.ds(s, 1), c]).then_inc(hn_done.sem, 1)

            def gate(s, slot, m):
                rows = hid_rows(m)
                act.wait_ge(h2_done.sem, h2_done.at(s, max(m - 1, 0)))
                psum.wait_full(act, s, f"g{m}")
                nc.scalar.activation(gelu[m % 2][0:rows, :], psum.tile(f"g{m}")[0:rows, :], ACT.Gelu,
                                     bias=b_1g[0:rows, bass.ds(s, 1), m]).then_inc(gelu_done.sem, 1)
                if m == HID_CHUNKS - 1:
                    nc.scalar.preload_act_table_set(EXP_AND_LN)

            nc.scalar.preload_act_table_set(EXP_AND_LN)
            pipeline(act, {"psq": square_qk, "prate": rate_qk, "ptc": copy_q, "vc": values, "exp": exponentials, "pt": copy_turned,
                           "otc": copy_output, "sq": square, "dev": deviation, "hn": affine, "gelu": gate})

        @block.gpsimd
        def _(pool):
            def times_cos(s, slot, layer, w):
                pool.wait_ge(qk_rot_done.sem, qk_rot_done.at(s, w))
                pool.wait_ge(qk_done.sem, qk_done.at(s, 2 * w + 2))
                nc.gpsimd.tensor_tensor(by_head(by_cos), by_head(qk), for_heads(rotary[layer][:, w, 0], DIM_HEAD), ALU.mult)\
                    .then_inc(by_cos_done.sem, 1)

            pipeline(pool, {"prot": times_cos})

        @block.vector
        def _(dve):
            def sum_squares(s, slot, layer, w):
                dve.wait_ge(qk_sq_done.sem, qk_sq_done.at(s, 2 * w + 2))
                nc.vector.tensor_reduce(qk_rate[:].rearrange("p x h -> p (x h)"),
                                        qk_sq[:].rearrange("p x (h d) -> p (x h) d", d=DIM_HEAD), AX_X, ALU.add)\
                    .then_inc(qk_sum_done.sem, 1)
                dve.wait_ge(qk_sum_done.sem, qk_sum_done.at(s, w + 1))
                nc.vector.tensor_scalar(qk_rate[:], qk_rate[:], 1e-24, None, ALU.max).then_inc(qk_floor_done.sem, 1)

            def normalise_qk(s, slot, layer, w):
                dve.wait_ge(by_cos_done.sem, by_cos_done.at(s, w))
                dve.wait_ge(qk_rate_done.sem, qk_rate_done.at(s, w + 1))
                for i, stem in enumerate("qk"):
                    psum.wait_full(dve, s, f"{stem}{w}")
                    nc.vector.tensor_tensor(qk[:, i, :].rearrange("p (h d) -> p h d", d=DIM_HEAD),
                                            psum.tile(f"{stem}{w}")[:].rearrange("p (h d) -> p h d", d=DIM_HEAD),
                                            qk_rate[:, i, :].unsqueeze(2).to_broadcast([P, HEADS, DIM_HEAD]),
                                            ALU.mult).then_inc(qk_done.sem, 1)

            def times_sin(s, slot, layer, w):
                half = DIM_HEAD // 2
                dve.wait_ge(qk_done.sem, qk_done.at(s, 2 * w + 2))
                for i in range(2):
                    to, source = slice(i * half, (i + 1) * half), slice((1 - i) * half, (2 - i) * half)
                    nc.vector.tensor_tensor(by_head(qk_rot)[:, :, :, to], by_head(qk)[:, :, :, source],
                                            for_heads(rotary[layer][:, w, 1, :, to], half), ALU.mult).then_inc(by_sin_done.sem, 1)

            def add_rotated(s, slot, layer, w):
                dve.wait_ge(by_cos_done.sem, by_cos_done.at(s, w + 1))
                dve.wait_ge(by_sin_done.sem, by_sin_done.at(s, 2 * w + 2))
                nc.vector.tensor_tensor(qk_rot[:], qk_rot[:], by_cos[:], ALU.add).then_inc(qk_rot_done.sem, 1)

            def copy_k(s, slot, layer, w):
                psum.wait_full(dve, s, f"k_t{w}")
                nc.vector.tensor_copy(k_t[slot][:, :, w * P:(w + 1) * P],
                                      psum.tile(f"k_t{w}")[:].rearrange("p (n c) -> p n c", c=P)).then_inc(k_t_done.sem, 1)

            def mask_scores(s, slot, w, g):
                lo, hi = keys_of(w)
                if g == 0:
                    by_act, by_dve = probs_t_until(w - 2)
                    dve.wait_ge(probs_t_act.sem, probs_t_act.at(s, by_act))
                    dve.wait_ge(probs_t_dve.sem, probs_t_dve.at(s, by_dve))
                for h in range(2):
                    psum.wait_full(dve, s, f"s{w}_{g}_{h}")
                    n = 4 * w + 2 * g + h
                    nc.vector.memset(waiter[:, n:n + 1], 0.0)
                    for n in range(2):
                        at, head = n * 2 * WINDOW, 2 * (2 * g + n) + h
                        last = nc.vector.tensor_tensor_reduce(
                            out=scores[w % 2][:, head, lo:hi], in0=s_banks[h][:, at + lo:at + hi], in1=mask[:, lo:hi],
                            scale=1.0, scalar=MASKED, op0=ALU.add, op1=ALU.max, accum_out=row_max[:, w, head:head + 1])
                    last.then_inc(masked_done.sem, 1)
                if g == 1:
                    dve.wait_ge(masked_done.sem, masked_done.at(s, PAIRS * (w + 1)))
                    nc.vector.tensor_scalar(row_bias[:, w, :], row_max[:, w, :], -1.0, None, ALU.mult).then_inc(row_bias_done.sem, 1)

            def copy_turned(s, slot, w, i):
                if (w, i) in on_dve:
                    psum.wait_full(dve, s, f"pt{w}_{i}")
                    to = probs_t[w % 2][:, 4 * i:4 * i + 4, :] if w else probs_t[0][:, 8 * i + 1:8 * i + 8:2, :]
                    nc.vector.tensor_copy(to, psum.tile(f"pt{w}_{i}")[:].rearrange("p (n c) -> p n c", c=P)).then_inc(probs_t_dve.sem, 1)

            def normalise(s, slot, w):
                dve.wait_ge(probs_done.sem, probs_done.at(s, PAIRS * (w + 1)))
                nc.vector.reciprocal(row_rate[:, w, :], row_sum[:, w, :]).then_inc(row_rate_done.sem, 1)
                dve.wait_ge(row_rate_done.sem, row_rate_done.at(s, w + 1))
                dve.wait_ge(o_t_done.sem, o_t_done.at(s, max(w - 1, 0)))
                psum.wait_full(dve, s, f"o{w}")
                nc.vector.tensor_tensor(o[w % 2][:].rearrange("p (h d) -> p h d", h=HEADS),
                                        psum.tile(f"o{w}")[:].rearrange("p (h d) -> p h d", h=HEADS),
                                        row_rate[:, w, :].unsqueeze(2).to_broadcast([P, HEADS, DIM_HEAD]),
                                        ALU.mult).then_inc(o_done.sem, 1)

            def add_residual(s, slot, c):
                dve.wait_ge(x_res_loaded.sem, x_res_loaded.at(s, 1))
                psum.wait_full(dve, s, f"wo{c}")
                nc.vector.tensor_tensor(plain(x2, c), psum.tile(f"wo{c}")[:], x_res[:, c, :], ALU.add).then_inc(x2_done.sem, 1)

            def centre(s, slot, _):
                dve.wait_ge(x2_done.sem, x2_done.at(s, CHUNKS))
                dve.wait_ge(hn_done.sem, hn_done.at(s))
                psum.wait_full(dve, s, "mean")
                for c in range(CHUNKS):
                    nc.vector.tensor_tensor(xc[:, c, :], shifted(x2, c), psum.tile("mean")[:], ALU.subtract).then_inc(xc_done.sem, 1)

            def normalise_tokens(s, slot, _):
                dve.wait_ge(rstd_done.sem, rstd_done.at(s, 1))
                dve.wait_ge(sq_done.sem, sq_done.at(s, 1))
                nc.vector.tensor_tensor(xc[:], xc[:], rstd[:].unsqueeze(1).to_broadcast([P, CHUNKS, SEQ]),
                                        ALU.mult).then_inc(xn_done.sem, 1)

            def gated(s, slot, m):
                rows = hid_rows(m)
                dve.wait_ge(gelu_done.sem, gelu_done.at(s, m + 1))
                psum.wait_full(dve, s, f"a{m}")
                nc.vector.scalar_tensor_tensor(h2[0:rows, m, :], psum.tile(f"a{m}")[0:rows, :], b_1a[0:rows, bass.ds(s, 1), m],
                                               gelu[m % 2][0:rows, :], ALU.add, ALU.mult).then_inc(h2_done.sem, 1)

            def finish(s, slot, c):
                dve.wait_ge(stored.sem, stored.at(s))
                psum.wait_full(dve, s, f"wd{c}")
                nc.vector.scalar_tensor_tensor(x_out[:, c, :], psum.tile(f"wd{c}")[:], b_2[:, bass.ds(s, 1), c],
                                               plain(x2, c), ALU.add, ALU.add).then_inc(x_out_done.sem, 1)

            pipeline(dve, {"pss": sum_squares, "pnorm": normalise_qk, "prot": times_sin, "padd": add_rotated, "ptc": copy_k,
                           "mask": mask_scores, "pt": copy_turned, "onorm": normalise, "add": add_residual, "cen": centre,
                           "xn": normalise_tokens, "gated": gated, "fin": finish})



def load_stack_vectors(nc, inp, squares, rotary, ln_g, ln_b, b_1a, b_1g, b_2):
    with ExitStack() as ctx:
        loaded = ctx.enter_context(nc.semaphore("v_loaded"))
        small = [ctx.enter_context(nc.sbuf_tensor(f"v_small{i}", [P, DEPTH, x.shape[2]], F32))
                 for i, x in enumerate((ln_g, ln_b, b_2, b_1a, b_1g))]
        g, b, b2, b1a, b1g = small
        tables = ctx.enter_context(nc.sbuf_tensor("v_tables", [P, TILES, 2, 2, DIM_HEAD], F32))
        scales = ctx.enter_context(nc.sbuf_tensor("v_scales", [P, DEPTH, 2, 2, DIM_HEAD], F32))
        half = DIM_HEAD // 2
        n_loads = 2 + 6 * DEPTH + 6 + 8
        with nc.Block() as block:
            @block.sync
            def _(sp):
                with nc.allow_non_contiguous_dma(reason="short vectors onto partitions"):
                    def put(to, src):
                        sp.dma_start(to, src).then_inc(loaded, 16)

                    put(squares[:], inp["c_squares"].rearrange("p (s c) -> p s c", c=P))
                    put(tables[:], inp["c_rotary"])
                    for l in range(DEPTH):
                        for i, name in enumerate(("L0_ffn_q_scale", "L0_ffn_k_scale")):
                            row = inp[name][l:l + 1]
                            put(scales[:, l, 0, i, :], row.to_broadcast([P, DIM_HEAD]))
                            put(scales[:, l, 1, i, 0:half], row[:, half:].to_broadcast([P, half]))
                            put(scales[:, l, 1, i, half:], row[:, 0:half].to_broadcast([P, half]))
                    for to, name in ((g, "L0_ffn_ln_g"), (b, "L0_ffn_ln_b"), (b2, "L0_ffn_b2")):
                        for l in range(DEPTH):
                            put(to[:, l, :], inp[name][l].rearrange("(c p) -> p c", p=P))
                    whole = HID // P
                    for to, at in ((b1a, 0), (b1g, HID)):
                        for l in range(DEPTH):
                            put(to[:, l, 0:whole], inp["L0_ffn_b1"][l, at:at + whole * P].rearrange("(c p) -> p c", p=P))
                            put(to[0:HID - whole * P, l, whole:whole + 1],
                                inp["L0_ffn_b1"][l, at + whole * P:at + HID].rearrange("(p c) -> p c", c=1))

            @block.vector
            def _(dve):
                dve.wait_ge(loaded, 16 * n_loads)
                whole, rest = HID // P, HID % P
                for l in range(DEPTH):
                    nc.vector.tensor_tensor(rotary[l][:].rearrange("p w a b d -> p w (a b d)"),
                                            tables[:].rearrange("p w a b d -> p w (a b d)"),
                                            scales[:, l].rearrange("p a b d -> p (a b d)").unsqueeze(1)
                                            .to_broadcast([P, TILES, 4 * DIM_HEAD]), ALU.mult)
                for to, src in ((ln_g, g), (ln_b, b), (b_2, b2)):
                    for l in range(DEPTH):
                        part = to[:, l * BATCH:(l + 1) * BATCH, :]
                        nc.vector.tensor_copy(part, src[:, l, :].unsqueeze(1).to_broadcast(list(part.shape)))
                for to, src in ((b_1a, b1a), (b_1g, b1g)):
                    for l in range(DEPTH):
                        part = to[:, l * BATCH:(l + 1) * BATCH, 0:whole]
                        nc.vector.tensor_copy(part, src[:, l, 0:whole].unsqueeze(1).to_broadcast(list(part.shape)))
                        part = to[0:rest, l * BATCH:(l + 1) * BATCH, whole:whole + 1]
                        nc.vector.tensor_copy(part, src[0:rest, l, whole:whole + 1].unsqueeze(1).to_broadcast(list(part.shape)))


def final_pass(nc, inp, mod, x1_dram, stack_dram, out):
    with ExitStack() as ctx:
        def sb(name, shape):
            return ctx.enter_context(nc.sbuf_tensor("c_" + name, shape, F32))

        def sem(name):
            return ctx.enter_context(nc.semaphore("c_" + name))

        signals = []

        def signal(name, per_pass, unit=1):
            signals.append(Signal(sem(name), per_pass, unit))
            return signals[-1]

        banks = [ctx.enter_context(nc.psum_tensor(f"c_bank{i}", [P, 512], F32)) for i in range(2)]
        ident = sb("ident", [P, P])
        x1 = sb("x1", [P, CHUNKS, SEQ])
        f = sb("f", [P, CHUNKS, SEQ])
        y = sb("y", [P, CHUNKS, SEQ])
        tokens = sb("tokens", [P, TILES, DIM])
        ident_loaded = sem("ident_loaded")
        loaded = signal("loaded", 2, 16)
        y_done = signal("y_done", CHUNKS)
        turned = [signal(f"turned{i}", 1) for i in range(2)]
        tokens_done = signal("tokens_done", 2)
        stored = signal("stored", 1, 16)

        start_signals(nc, signals)
        block = ctx.enter_context(nc.Block())

        @block.sync
        def _(sp):
            sp.dma_start(ident[:], inp["c_squares"][:, 0:P]).then_inc(ident_loaded, 16)
            with sp.Fori(0, BATCH) as b:
                sp.wait_ge(y_done.sem, y_done.at(b))
                sp.dma_start(x1[:], x1_dram[b]).then_inc(loaded.sem, 16)
                sp.dma_start(f[:], stack_dram[DEPTH * BATCH + b]).then_inc(loaded.sem, 16)

        @block.scalar
        def _(act):
            with act.Fori(0, BATCH) as b:
                act.wait_ge(tokens_done.sem, tokens_done.at(b, 2))
                act.dma_start(out[b].rearrange("(t p) d -> p t d", p=P), tokens[:]).then_inc(stored.sem, 16)
            act.wait_ge(stored.sem, stored.at(BATCH))

        @block.vector
        def _(dve):
            with dve.Fori(0, BATCH) as b:
                dve.wait_ge(loaded.sem, loaded.at(b, 2))
                dve.wait_ge(tokens_done.sem, tokens_done.at(b))
                for c in range(CHUNKS):
                    nc.vector.scalar_tensor_tensor(y[:, c, :], f[:, c, :], mod[:, 2 * MOD_GATE_B + c, bass.ds(b, 1)],
                                                   x1[:, c, :], ALU.mult, ALU.add).then_inc(y_done.sem, 1)
                dve.wait_ge(stored.sem, stored.at(b))
                for i in range(2):
                    dve.wait_ge(turned[i].sem, turned[i].at(b, 1))
                    nc.vector.tensor_copy(tokens[:, 2 * i:2 * i + 2, :], banks[i][:].rearrange("p (t d) -> p t d", d=DIM))\
                        .then_inc(tokens_done.sem, 1)

        @block.tensor
        def _(pe):
            pe.wait_ge(ident_loaded, 16)
            with pe.Fori(0, BATCH) as b:
                pe.wait_ge(y_done.sem, y_done.at(b, CHUNKS))
                for t in range(TILES):
                    if t % 2 == 0:
                        pe.wait_ge(tokens_done.sem, tokens_done.at(b, 0))
                    for c in range(CHUNKS):
                        at = (t % 2) * DIM + c * P
                        last = nc.tensor.transpose(banks[t // 2][:, at:at + P], y[:, c, t * P:(t + 1) * P], ident[:])
                    if t % 2:
                        last.then_inc(turned[t // 2].sem, 1)


def setup_weights(nc, inp, banks, ident, mean_mat, pick, picks, w_in_t, w_dt_t, w_bc_t, w_out_t,
                  neg_a, b_dt, skip_d, mod, ln_eps):
    with ExitStack() as ctx:
        def sb(name, shape, dt=F32):
            return ctx.enter_context(nc.sbuf_tensor("s_" + name, shape, dt))

        def sem(name):
            return ctx.enter_context(nc.semaphore("s_" + name))

        w_in = sb("w_in", [P, 8, DIM])
        w_dt = sb("w_dt", [P, INNER_CHUNKS, D_INNER])
        w_out = sb("w_out", [P, CHUNKS, D_INNER])
        w_bc = sb("w_bc", [2 * STATES, D_INNER])
        cond = sb("cond", [BATCH, DIM])
        cond_t = sb("cond_t", [P, CHUNKS, BATCH])
        w_mod = sb("w_mod", [P, CHUNKS, 6 * DIM])
        a_log = sb("a_log", [P, INNER_CHUNKS, STATES])
        gate = sb("gate", [P, 1])
        sign = sb("sign", [P, 2 * CHUNKS, BATCH])
        size = sb("size", [P, 2 * CHUNKS, BATCH])

        squares_loaded, w_in_loaded, w_dt_loaded = sem("squares_loaded"), sem("w_in_loaded"), sem("w_dt_loaded")
        w_out_loaded, w_bc_loaded, small_loaded = sem("w_out_loaded"), sem("w_bc_loaded"), sem("small_loaded")
        cond_loaded, w_mod_loaded = sem("cond_loaded"), sem("w_mod_loaded")
        turned, copied = sem("turned"), sem("copied")
        silu_done, cond_turned, cond_copied = sem("silu_done"), sem("cond_turned"), sem("cond_copied")
        mod_full, mod_copied, gate_step = sem("mod_full"), sem("mod_copied"), sem("gate_step")
        mod_step, a_step = sem("mod_step"), sem("a_step")

        turns = []
        for c in range(CHUNKS):
            for half in range(2):
                turns.append((w_in_loaded, [w_in[:, 4 * half + m, c * P:(c + 1) * P] for m in range(4)],
                              w_in_t[:, c, half * 512:(half + 1) * 512], P))
        for k in range(INNER_CHUNKS):
            turns.append((w_dt_loaded, [w_dt[:, m, k * P:(k + 1) * P] for m in range(4)], w_dt_t[:, k, :], P))
        for k in range(INNER_CHUNKS):
            turns.append((w_out_loaded, [w_out[:, o, k * P:(k + 1) * P] for o in range(CHUNKS)], w_out_t[:, k, :], P))
        for k in range(INNER_CHUNKS):
            turns.append((w_bc_loaded, [w_bc[:, k * P:(k + 1) * P]], w_bc_t[:, k, :], 2 * STATES))

        with nc.Block() as block:
            @block.sync
            def _(sp):
                sp.dma_start(ident[:], inp["c_squares"][:, 0:P]).then_inc(squares_loaded, 16)
                sp.dma_start(mean_mat[:], inp["c_squares"][:, P:2 * P]).then_inc(squares_loaded, 16)
                sp.dma_start(w_in[:], inp["L0_attn_W_in"].rearrange("(m p) d -> p m d", p=P)).then_inc(w_in_loaded, 16)
                sp.dma_start(cond[:], inp["L0_c"]).then_inc(cond_loaded, 16)
                sp.dma_start(w_dt[:], inp["L0_attn_W_dt"].rearrange("(m p) d -> p m d", p=P)).then_inc(w_dt_loaded, 16)
                sp.dma_start(w_out[:], inp["L0_attn_W_out"].rearrange("(m p) d -> p m d", p=P)).then_inc(w_out_loaded, 16)
                sp.dma_start(w_bc[0:STATES, :], inp["L0_attn_W_B"]).then_inc(w_bc_loaded, 16)
                sp.dma_start(w_bc[STATES:, :], inp["L0_attn_W_C"]).then_inc(w_bc_loaded, 16)
                sp.dma_start(w_mod[:], inp["L0_wmod"].rearrange("(c p) f -> p c f", p=P)).then_inc(w_mod_loaded, 16)

            @block.scalar
            def _(act):
                act.dma_start(pick[:], inp["c_pick"]).then_inc(small_loaded, 16)
                act.dma_start(a_log[:], inp["L0_attn_A_log"].rearrange("(c p) n -> p c n", p=P)).then_inc(small_loaded, 16)
                with nc.allow_non_contiguous_dma(reason="three short vectors"):
                    act.dma_start(b_dt[:], inp["L0_attn_b_dt"].rearrange("(c p) -> p c", p=P)).then_inc(small_loaded, 16)
                    act.dma_start(skip_d[:], inp["L0_attn_D"].rearrange("(c p) -> p c", p=P)).then_inc(small_loaded, 16)
                    act.dma_start(gate[:], inp["L0_attn_output_gate"].rearrange("(a b) -> a b", a=1)
                                  .to_broadcast([P, 1])).then_inc(small_loaded, 16)
                act.wait_ge(cond_loaded, 16)
                nc.scalar.activation(cond[:], cond[:], ACT.Silu).then_inc(silu_done, 1)
                act.wait_ge(small_loaded, 16 * 5)
                nc.scalar.activation(gate[:], gate[:], ACT.Sigmoid).then_inc(gate_step, 1)
                nc.scalar.activation(a_log[:], a_log[:], ACT.Exp).then_inc(a_step, 1)

            @block.tensor
            def _(pe):
                pe.wait_ge(squares_loaded, 32)
                pe.wait_ge(silu_done, 1)
                for c in range(CHUNKS):
                    last = nc.tensor.transpose(banks[7][:, c * BATCH:(c + 1) * BATCH], cond[:, c * P:(c + 1) * P],
                                               ident[0:BATCH, 0:BATCH])
                last.then_inc(cond_turned, 1)
                for i, (loaded, sources, _, rows) in enumerate(turns):
                    pe.wait_ge(loaded, 32 if loaded is w_bc_loaded else 16)
                    if i >= 6:
                        pe.wait_ge(copied, i - 5)
                    for m, s in enumerate(sources):
                        last = nc.tensor.transpose(banks[i % 6][:, m * rows:(m + 1) * rows], s, ident[0:rows, 0:rows])
                    last.then_inc(turned, 1)
                pe.wait_ge(w_mod_loaded, 16)
                pe.wait_ge(cond_copied, 1)
                for f in range(12):
                    for c in range(CHUNKS):
                        last = nc.tensor.matmul(banks[6][:, f * BATCH:(f + 1) * BATCH], w_mod[:, c, f * P:(f + 1) * P],
                                                cond_t[:, c, :], start=(c == 0), stop=(c == CHUNKS - 1))
                last.then_inc(mod_full, 1)

            @block.vector
            def _(dve):
                nc.vector.memset(ln_eps[:], LN_EPS)
                dve.wait_ge(cond_turned, 1)
                nc.vector.tensor_copy(cond_t[:].rearrange("p c b -> p (c b)"), banks[7][:, 0:CHUNKS * BATCH]).then_inc(cond_copied, 1)
                for i, (_, sources, target, rows) in enumerate(turns):
                    dve.wait_ge(turned, i + 1)
                    nc.vector.tensor_copy(target, banks[i % 6][:, 0:len(sources) * rows]).then_inc(copied, 1)
                dve.wait_ge(a_step, 1)
                nc.vector.tensor_scalar(neg_a[:], a_log[:], -1.0, None, ALU.mult)
                nc.vector.tensor_copy(picks[0:96], pick[0:96].unsqueeze(2).to_broadcast([96, 2 * STATES, P]))
                dve.wait_ge(mod_full, 1)
                nc.vector.tensor_copy(mod[:].rearrange("p f b -> p (f b)"), banks[6][:, 0:12 * BATCH]).then_inc(mod_copied, 1)
                dve.wait_ge(mod_copied, 1)
                for s in (MOD_SCALE_A, MOD_SCALE_B):
                    part = mod[:, 2 * s:2 * s + 2, :]
                    nc.vector.tensor_scalar(part, part, 1.0, None, ALU.add)
                for i, g in enumerate((MOD_GATE_A, MOD_GATE_B)):
                    part, at = mod[:, 2 * g:2 * g + 2, :], slice(2 * i, 2 * i + 2)
                    nc.vector.tensor_scalar(sign[:, at], part, 0.0, 2.0, ALU.is_ge, ALU.mult).then_inc(mod_step, 1)
                    nc.vector.scalar_tensor_tensor(size[:, at], part, -1.0, part, ALU.mult, ALU.max).then_inc(mod_step, 1)
                dve.wait_ge(mod_step, 4)
                nc.vector.tensor_scalar(sign[:], sign[:], 1.0, None, ALU.subtract).then_inc(mod_step, 1)
                nc.vector.tensor_scalar(size[:], size[:], 0.25, None, ALU.max).then_inc(mod_step, 1)
                dve.wait_ge(mod_step, 6)
                dve.wait_ge(gate_step, 1)
                nc.vector.scalar_tensor_tensor(mod[:, 2 * MOD_GATE_A:2 * MOD_GATE_A + 2, :], sign[:, 0:2], gate[:, 0:1],
                                               size[:, 0:2], ALU.mult, ALU.mult)
                nc.vector.tensor_tensor(mod[:, 2 * MOD_GATE_B:2 * MOD_GATE_B + 2, :], sign[:, 2:4], size[:, 2:4], ALU.mult)


def build(nc, inp, out):
    x1_dram = nc.dram_tensor("x1_rows", (BATCH, P, CHUNKS, SEQ), F32, kind="Internal").ap()
    stack_dram = nc.dram_tensor("stack_rows", ((DEPTH + 1) * BATCH, P, CHUNKS, SEQ), F32, kind="Internal").ap()
    with nc.sbuf_tensor("mod", [P, 12, BATCH], F32) as mod:
        mixer_pass(nc, inp, mod, x1_dram, stack_dram)
        stack_pass(nc, inp, stack_dram)
        final_pass(nc, inp, mod, x1_dram, stack_dram, out)


NAMES = ["L0_attn_x", "L0_attn_W_in", "L0_attn_A_log", "L0_attn_W_B", "L0_attn_W_C", "L0_attn_W_dt", "L0_attn_b_dt",
         "L0_attn_D", "L0_attn_output_gate", "L0_attn_W_out", "L0_ffn_wqkv", "L0_ffn_q_scale", "L0_ffn_k_scale",
         "L0_ffn_wo", "L0_ffn_ln_g", "L0_ffn_ln_b", "L0_ffn_w1", "L0_ffn_b1", "L0_ffn_w2", "L0_ffn_b2", "L0_c", "L0_wmod"]


def kernel(**inputs):
    import concourse.bacc as bacc
    from concourse.bass_utils import run_bass_kernel_spmd

    nc = bacc.Bacc("TRN2", target_bir_lowering=False, num_devices=1)
    arrays = {name: np.ascontiguousarray(inputs[name]) for name in NAMES}
    arrays.update(host_constants())
    inp = {name: nc.dram_tensor("in_" + name, a.shape, mybir.dt.from_np(a.dtype), kind="ExternalInput").ap()
           for name, a in arrays.items()}
    out = nc.dram_tensor("out_rows", (BATCH, SEQ, DIM), F32, kind="ExternalOutput").ap()
    build(nc, inp, out)
    result = run_bass_kernel_spmd(nc, [{"in_" + name: a for name, a in arrays.items()}], core_ids=[0])
    return result.results[0]["out_rows"]
```

```python
from contextlib import ExitStack

import numpy as np

import concourse.bass as bass
import concourse.mybir as mybir
from concourse.alu_op_type import AluOpType as ALU

ACT = mybir.ActivationFunctionType
F32 = mybir.dt.float32
BF16 = mybir.dt.bfloat16
I32 = mybir.dt.int32
F32R = mybir.dt.float32r
AX_X = mybir.AxisListType.X

P = 128
BATCH, SEQ, DIM = 16, 512, 256
CHUNKS = DIM // P
TILES = SEQ // P
D_INNER = 512
INNER_CHUNKS = D_INNER // P
STATES = 16
GROUP = 2
GROUPS = STATES // GROUP
UNITS = GROUPS * INNER_CHUNKS
DECAY_SLOTS, STATE_SLOTS = 4, 8
DEPTH, HEADS, DIM_HEAD, WINDOW = 2, 8, 64, 128
INNER = HEADS * DIM_HEAD
PAIRS = HEADS // 2
HID = int(DIM * 4 * 2 / 3)
HID_CHUNKS = -(-HID // P)
G_TAIL_AT = 64
W_1_COLS = (2 * (HID // P) + 1) * P
QK_SCALE = 8.0
LN_EPS = 1e-5
SERIES_BELOW = 0.02
MASKED = -3.0e38
SCREEN = 2.0 ** 17
EXP_AND_LN = "natural_log_exp_and_others"
MOD_SHIFT_A, MOD_SCALE_A, MOD_GATE_A, MOD_SHIFT_B, MOD_SCALE_B, MOD_GATE_B = range(6)


class Signal:

    def __init__(self, sem, per_pass, unit=1):
        self.sem, self.per_pass, self.unit = sem, per_pass * unit, unit

    def at(self, done, k=0):
        return done * self.per_pass + (k * self.unit + 1)


def start_signals(nc, signals):
    with nc.Block() as block:
        @block.gpsimd
        def _(pool):
            for signal in signals:
                pool.sem_inc(signal.sem, 1)


class Banks:

    def __init__(self, tiles, full, uses):
        self.tiles, self.full = tiles, full
        self.where, self.count, self.before, last = {}, [0] * len(tiles), {}, {}
        for name, bank, signal, k in uses:
            self.where[name] = (bank, self.count[bank])
            self.count[bank] += 1
            self.before[name] = last.get(bank)
            last[bank] = (signal, k)
        for name, bank, _, _ in uses:
            if self.before[name] is None:
                signal, k = last[bank]
                self.before[name] = (signal, k - signal.per_pass)

    def tile(self, name):
        return self.tiles[self.where[name][0]]

    def wait_free(self, eng, done, name):
        signal, k = self.before[name]
        if not (isinstance(done, int) and done == 0 and k < 0):
            eng.wait_ge(signal.sem, signal.at(done, k))

    def wait_full(self, eng, done, name):
        bank, k = self.where[name]
        eng.wait_ge(self.full[bank], done * self.count[bank] + k + 1)

    def filled(self, instruction, name):
        instruction.then_inc(self.full[self.where[name][0]], 1)


def host_constants():
    eye = np.eye(P, dtype=np.float32)
    mean = np.full((P, P), 1.0 / DIM, np.float32)
    i, j = np.arange(WINDOW)[:, None], np.arange(WINDOW)[None, :]
    mask_back = np.where(j >= i, 0.0, MASKED).astype(np.float32)
    mask_own = np.where(j <= i, 0.0, MASKED).astype(np.float32)
    squares = np.concatenate([eye, mean, mask_back, mask_own], axis=1)
    pick = np.zeros((P, STATES), np.float32)
    for part in range(3):
        pick[2 * STATES * part + np.arange(STATES), np.arange(STATES)] = 1.0
    f32 = np.float32
    half_idx = np.arange(0, DIM_HEAD, 2, dtype=f32)
    inv_freq = f32(1.0) / np.power(f32(10000.0), half_idx / f32(DIM_HEAD), dtype=f32)
    t = np.arange(SEQ, dtype=f32)
    freqs = (t[:, None] * inv_freq[None, :]).astype(f32)
    base = ((half_idx + f32(0.4 * DIM_HEAD)) / f32(1.4 * DIM_HEAD)).astype(f32)
    power = ((t - f32(SEQ // 2)) / f32(WINDOW // 2)).astype(f32)
    scale = np.power(base[None, :], power[:, None], dtype=f32)
    cos, sin = np.cos(freqs, dtype=f32), np.sin(freqs, dtype=f32)
    two = lambda x: np.concatenate([x, x], axis=1)
    cos, sin, scale = two(cos), np.concatenate([-sin, sin], axis=1), two(scale)
    tables = np.stack([np.stack([f32(QK_SCALE) * cos * scale, cos / scale], axis=1),
                       np.stack([f32(QK_SCALE) * sin * scale, sin / scale], axis=1)], axis=1).astype(f32)
    rotary = tables.reshape(TILES, P, 2, 2, DIM_HEAD).transpose(1, 0, 2, 3, 4)
    return {"c_squares": squares, "c_pick": pick, "c_rotary": np.ascontiguousarray(rotary)}


MIXER_STEPS = {"head": "xT xcopy stat norm hT h1 hcut xs xscopy bc bccopy cut dt soft step z zcopy silu bfirst cfirst",
               "scan": "unit bwide cwide sum",
               "tail": "last gate out res mean2 cen2 sq2 var2 dev2 xn2 h2"}
MIXER_STAGE = {step: stage for stage, steps in MIXER_STEPS.items() for step in steps.split()}
MIXER_LEAD = {"head": 1, "scan": 0, "tail": -1}
MIXER_ORDER = """
unit:0 last:29 stat:0 gate:0 cwide:1 gate:1 last:30 unit:1 gate:2 bwide:1.0 bwide:1.1 unit:2 unit:3 last:31 norm:0
sum:0 unit:4 sum:1 hT:0 sum:2 gate:3 unit:5 hT:1 h1:0 out:0 bwide:2.0 bwide:2.1 unit:6 hcut:0 res:0 sum:3 unit:7 xs:0
out:1 sum:4 xscopy:0 sum:5 xs:1 xscopy:1 unit:8 cwide:2 mean2:0 res:1 unit:9 sum:6 cen2:0 unit:10 unit:11 xscopy:2
unit:12 sq2:0 xs:2 bwide:3.0 sum:7 unit:13 xn2:0 bwide:3.1 xs:3 var2:0 sum:8 cwide:3 xT:0 sum:9 xscopy:3 xT:1 sum:10
dev2:0 xcopy:0 bwide:4.0 xcopy:1 bwide:4.1 unit:14 bccopy:0 bc:0 unit:15 unit:16 cwide:4 sum:11 dt:0 cut:0 unit:17
soft:0 sum:12 sum:13 step:0 soft:1 unit:18 h2:0 soft:2 step:1 dt:1 sum:14 sum:15 dt:2 bwide:5.0 bwide:5.1 sum:16
sum:17 dt:3 unit:19 sum:18 step:2 soft:3 unit:20 unit:21 cwide:5 unit:22 unit:23 zcopy:0 step:3 cwide:6 z:0 unit:24
bwide:6.0 bwide:6.1 zcopy:1 sum:19 sum:20 unit:25 z:1 z:2 sum:21 sum:22 zcopy:2 unit:26 z:3 unit:27 cwide:7 bwide:7.0
bwide:7.1 sum:23 unit:28 sum:24 zcopy:3 sum:25 unit:29 sum:26 unit:30 bfirst:0 sum:27 silu:0 sum:28 unit:31 cfirst:0
"""


def steps_of(order):
    return [(name, *map(int, at.split("."))) for name, _, at in (step.partition(":") for step in order.split())]


MIXER_SCHEDULE = steps_of(MIXER_ORDER)


def mixer_pass(nc, inp, mod, x1_dram, stack_dram, c_dram):
    with ExitStack() as ctx:
        def sb(name, shape, dt=F32):
            return ctx.enter_context(nc.sbuf_tensor("a_" + name, shape, dt))

        def sem(name):
            return ctx.enter_context(nc.semaphore("a_" + name))

        signals = []

        def signal(name, per_pass, unit=1):
            signals.append(Signal(sem(name), per_pass, unit))
            return signals[-1]

        b_wide = ctx.enter_context(nc.psum_tensor("a_b_wide", [P, GROUP, SEQ], F32))
        single_banks = [ctx.enter_context(nc.psum_tensor(f"a_bank{i}", [P, SEQ], F32)) for i in range(8 - GROUP)]
        banks_all = [bank[:] for bank in single_banks] + [b_wide[:, i, :] for i in range(GROUP)]

        ident = sb("ident", [P, P])
        mean_mat = sb("mean_mat", [P, P])
        pick = sb("pick", [P, STATES])
        picks = sb("picks", [P, STATES, P], BF16)
        w_in_t = [sb(f"w_in_t{i}", [P, CHUNKS, 2 * D_INNER]) for i in range(2)]
        w_dt_t = sb("w_dt_t", [P, INNER_CHUNKS, D_INNER])
        w_bc_t = sb("w_bc_t", [P, INNER_CHUNKS, 2 * STATES])
        w_out_t = sb("w_out_t", [P, INNER_CHUNKS, DIM])
        neg_a = sb("neg_a", [P, INNER_CHUNKS, STATES])
        b_dt = sb("b_dt", [P, INNER_CHUNKS])
        skip_d = sb("skip_d", [P, INNER_CHUNKS])
        ln_eps = sb("ln_eps", [P, 1])
        third, below = sb("third", [P, 1]), sb("below", [P, 1])
        waiter = sb("waiter", [P, INNER_CHUNKS])

        setup_weights(nc, inp, banks_all, ident, mean_mat, pick, picks, w_in_t, w_dt_t, w_bc_t, w_out_t,
                      neg_a, b_dt, skip_d, mod, ln_eps)

        xt = sb("xt", [P, TILES, DIM])
        x_t = [sb(f"x_t{i}", [P, CHUNKS, SEQ]) for i in range(2)]
        xn = sb("xn", [P, TILES, DIM])
        neg_mean = sb("neg_mean", [P, TILES])
        token_rate = sb("token_rate", [P, TILES])
        h_upper, h_lower = (sb(f"h_part{i}", [P, CHUNKS, SEQ]) for i in range(2))
        xs = [sb(f"xs{i}", [P, INNER_CHUNKS, SEQ]) for i in range(2)]
        sz = [sb(f"sz{i}", [P, INNER_CHUNKS, SEQ]) for i in range(2)]
        dt = [sb(f"dt{i}", [P, INNER_CHUNKS, SEQ]) for i in range(2)]
        u = [sb(f"u{i}", [P, INNER_CHUNKS, SEQ]) for i in range(2)]
        sp_e = sb("sp_e", [P, SEQ])
        sp_ln = sb("sp_ln", [P, SEQ])
        sp_relu = sb("sp_relu", [P, SEQ])
        sp_p = sb("sp_p", [P, SEQ])
        sp_mask = sb("sp_mask", [P, SEQ])
        bc_parts = [sb(f"bc_parts{i}", [P, SEQ], BF16) for i in range(2)]
        h_t = (sp_e, sp_ln)
        bc = sb("bc", [2 * STATES, SEQ])
        bc_rest = sp_p[0:2 * STATES, :]
        bc_mid = sb("bc_mid", [2 * STATES, SEQ], BF16)
        decay = [sb(f"decay{i}", [P, GROUP, SEQ]) for i in range(DECAY_SLOTS)]
        state = [sb(f"state{i}", [P, GROUP, SEQ]) for i in range(STATE_SLOTS)]
        c_wide = [sb(f"c_wide{i}", [P, GROUP, SEQ]) for i in range(2)]
        yv = u
        x1_t = sb("x1_t", [P, CHUNKS, SEQ])
        xc2 = sb("xc2", [P, CHUNKS, SEQ])
        rstd2 = sb("rstd2", [P, SEQ])
        h2_t = sb("h2_t", [P, CHUNKS, SEQ])
        sq2 = h2_t

        x_loaded = signal("x_loaded", 1, 16)
        x_t_done = signal("x_t_done", CHUNKS)
        total_done = signal("total_done", TILES)
        mean_done = signal("mean_done", 1)
        var_done = signal("var_done", TILES)
        ln_done = signal("ln_done", 1)
        rate_done = signal("rate_done", 1)
        xn_done = signal("xn_done", TILES)
        h_done = signal("h_done", CHUNKS)
        h_upper_done = signal("h_upper_done", CHUNKS)
        h_cut = signal("h_cut", CHUNKS)
        xs_done = signal("xs_done", INNER_CHUNKS)
        z_done = signal("z_done", INNER_CHUNKS)
        silu_done = signal("silu_done", 1)
        bc_done = signal("bc_done", 1)
        c_stored = signal("c_stored", 1, 16)
        parts_done = signal("parts_done", 5)
        abs_done = signal("abs_done", INNER_CHUNKS)
        exp_done = signal("exp_done", INNER_CHUNKS)
        log_done = signal("log_done", INNER_CHUNKS)
        series_begun = signal("series_begun", INNER_CHUNKS)
        series_done = signal("series_done", 4 * INNER_CHUNKS)
        dt_done = signal("dt_done", INNER_CHUNKS)
        u_done = signal("u_done", INNER_CHUNKS)
        c_loaded = [signal(f"c_loaded{i}", GROUPS // 2, 16) for i in range(2)]
        decay_done = signal("decay_done", UNITS)
        input_done = signal("input_done", UNITS)
        scan_done = signal("scan_done", UNITS)
        on_vector = [q for q in range(UNITS) if q % 8 == 7]
        on_pool = [q for q in range(UNITS) if q not in on_vector]
        cmul_pool_done = signal("cmul_pool_done", len(on_pool))
        cmul_vec_done = signal("cmul_vec_done", len(on_vector))
        sum_done = signal("sum_done", UNITS)
        skip_done = signal("skip_done", INNER_CHUNKS)
        gated_done = signal("gated_done", INNER_CHUNKS)
        x1_done = signal("x1_done", CHUNKS)
        xc2_done = signal("xc2_done", CHUNKS)
        sq2_done = signal("sq2_done", 1)
        ln2_done = signal("ln2_done", 1)
        rstd2_done = signal("rstd2_done", 1)
        xn2_done = signal("xn2_done", 1)
        h2_done = signal("h2_done", CHUNKS)
        stored = signal("stored", 2, 16)

        def b_name(g, i):
            return f"b{g}_{i}"

        uses = [(b_name(g, i), 2 + i, input_done, INNER_CHUNKS * (g + 1)) for g in range(GROUPS) for i in range(GROUP)]
        for name, k, *_ in MIXER_SCHEDULE:
            use = {"xT": (f"xT{k}", 0, x_t_done, k + 1),
                   "hT": (f"hT{k}", 0, h_done, k + 1),
                   "xs": (f"xs{k}", 0, xs_done, k + 1),
                   "z": (f"z{k}", 0, z_done, k + 1),
                   "bc": ("bc", 0, bc_done, 1),
                   "dt": (f"dt{k}", 0, abs_done, k + 1),
                   "out": (f"out{k}", 1, x1_done, k + 1),
                   "mean2": ("mean2", 1, xc2_done, CHUNKS),
                   "var2": ("var2", 1, ln2_done, 1)}.get(name)
            if use:
                uses.append(use)
        work = Banks(banks_all[0:2] + banks_all[-GROUP:], [sem(f"full{i}") for i in range(2 + GROUP)], uses)
        y_sum = banks_all[2:-GROUP]

        def cmul_until(eng, s, n):
            eng.wait_ge(cmul_pool_done.sem, cmul_pool_done.at(s, sum(q < n for q in on_pool)))
            eng.wait_ge(cmul_vec_done.sem, cmul_vec_done.at(s, sum(q < n for q in on_vector)))

        def cmul_wait(eng, s, q):
            if q in on_pool:
                eng.wait_ge(cmul_pool_done.sem, cmul_pool_done.at(s, on_pool.index(q) + 1))
            else:
                eng.wait_ge(cmul_vec_done.sem, cmul_vec_done.at(s, on_vector.index(q) + 1))

        def slot_free(eng, s, done):
            if not (isinstance(s, int) and s < 2):
                eng.wait_ge(done.sem, done.at(s - 1))

        def unit_slot_free(eng, s, q, slots, done):
            if not (isinstance(s, int) and s == 0 and q < slots):
                eng.wait_ge(done.sem, done.at(s, q - slots + 1))

        def pipeline(eng, steps):
            def one_pass(i, parity, stages):
                for name, *at in MIXER_SCHEDULE:
                    lead = MIXER_LEAD[MIXER_STAGE[name]]
                    if MIXER_STAGE[name] in stages and name in steps:
                        steps[name](i + lead, (parity + lead) % 2, *at)

            one_pass(-1, 1, ("head",))
            one_pass(0, 0, ("head", "scan"))
            with eng.Fori(0, BATCH // 2 - 1) as j:
                one_pass(2 * j + 1, 1, ("head", "scan", "tail"))
                one_pass(2 * j + 2, 0, ("head", "scan", "tail"))
            one_pass(BATCH - 1, 1, ("scan", "tail"))
            one_pass(BATCH, 0, ("tail",))

        with nc.Block() as block:
            @block.vector
            def _(dve):
                for d in decay:
                    nc.vector.memset(d[:, :, 0:1], 0.0)
                nc.vector.memset(third[:], 1.0 / 3)
                nc.vector.memset(below[:], -SERIES_BELOW)
                nc.vector.memset(neg_mean[:], 0.0)
                nc.vector.memset(token_rate[:], 0.0)

        start_signals(nc, signals)
        block = ctx.enter_context(nc.Block())

        @block.sync
        def _(sp):
            def load(s):
                sp.wait_ge(x_t_done.sem, x_t_done.at(s))
                sp.wait_ge(xn_done.sem, xn_done.at(s))
                sp.dma_start(xt[:], inp["L0_attn_x"][s].rearrange("(t p) d -> p t d", p=P)).then_inc(x_loaded.sem, 16)

            def store(s):
                sp.wait_ge(x1_done.sem, x1_done.at(s, CHUNKS))
                sp.dma_start(x1_dram[s], x1_t[:]).then_inc(stored.sem, 16)
                sp.wait_ge(h2_done.sem, h2_done.at(s, CHUNKS))
                sp.dma_start(stack_dram[s], h2_t[:]).then_inc(stored.sem, 16)

            for s in range(3):
                load(s)
            with sp.Fori(3, BATCH) as s:
                load(s)
                store(s - 3)
            for s in range(BATCH - 3, BATCH):
                store(s)
            sp.wait_ge(stored.sem, stored.at(BATCH))

        @block.tensor
        def _(pe):
            def product(s, name, weights, sources, rows=P):
                work.wait_free(pe, s, name)
                for c, source in enumerate(sources):
                    last = nc.tensor.matmul(work.tile(name)[0:rows, :], weights[c], source,
                                            start=(c == 0), stop=(c == len(sources) - 1))
                work.filled(last, name)

            def cols(weights, at, n=P):
                return [weights[:, c, at:at + n] for c in range(weights.shape[1])]

            def chunks(x):
                return [x[:, c, :] for c in range(x.shape[1])]

            means = [mean_mat[:]] * CHUNKS

            def turn_input(s, slot, c):
                pe.wait_ge(x_loaded.sem, x_loaded.at(s, 1))
                work.wait_free(pe, s, f"xT{c}")
                for t in range(TILES):
                    last = nc.tensor.transpose(work.tile(f"xT{c}")[:, t * P:(t + 1) * P], xt[:, t, c * P:(c + 1) * P], ident[:])
                work.filled(last, f"xT{c}")

            def turn_normalised(s, slot, c):
                pe.wait_ge(xn_done.sem, xn_done.at(s, TILES))
                work.wait_free(pe, s, f"hT{c}")
                for t in range(TILES):
                    last = nc.tensor.transpose(work.tile(f"hT{c}")[:, t * P:(t + 1) * P], xn[:, t, c * P:(c + 1) * P], ident[:])
                work.filled(last, f"hT{c}")

            def product_of_parts(s, name, at):
                work.wait_free(pe, s, name)
                upper, lower = w_in_t
                pairs = [(weights, x, c) for weights, x in ((upper, h_upper), (lower, h_upper), (upper, h_lower))
                         for c in range(CHUNKS)]
                for n, (weights, x, c) in enumerate(pairs):
                    last = nc.tensor.matmul(work.tile(name), weights[:, c, at:at + P].bitcast(F32R),
                                            x[:, c, :].bitcast(F32R), start=(n == 0), stop=(n == len(pairs) - 1))
                work.filled(last, name)

            def project_x(s, slot, m):
                pe.wait_ge(h_cut.sem, h_cut.at(s, CHUNKS))
                product_of_parts(s, f"xs{m}", m * P)

            def project_z(s, slot, m):
                product_of_parts(s, f"z{m}", D_INNER + m * P)

            def project_bc(s, slot, _):
                pe.wait_ge(xs_done.sem, xs_done.at(s, INNER_CHUNKS))
                product(s, "bc", cols(w_bc_t, 0, 2 * STATES), chunks(xs[slot]), rows=2 * STATES)

            def project_dt(s, slot, m):
                pe.wait_ge(xs_done.sem, xs_done.at(s, INNER_CHUNKS))
                product(s, f"dt{m}", cols(w_dt_t, m * P), chunks(xs[slot]))

            def spread_b(s, slot, g, i):
                product(s, b_name(g, i), [picks[0:96, GROUP * g + i, :]], [bc_parts[slot][0:96, :]])

            def spread_first_b(s, slot, _):
                pe.wait_ge(parts_done.sem, parts_done.at(s, 5))
                for i in range(GROUP):
                    spread_b(s, slot, 0, i)

            def sum_states(s, slot, q):
                g, d = divmod(q, INNER_CHUNKS)
                if g == 0 and not (isinstance(s, int) and s == 0):
                    pe.wait_ge(skip_done.sem, skip_done.at(s - 1, d + 1))
                cmul_wait(pe, s, q)
                for j in range(GROUP):
                    last = nc.tensor.matmul(y_sum[d][:], ident[:], state[q % STATE_SLOTS][:, j, :],
                                            start=(g == 0 and j == 0), stop=(g == GROUPS - 1 and j == GROUP - 1))
                last.then_inc(sum_done.sem, 1)

            def project_out(s, slot, m):
                pe.wait_ge(gated_done.sem, gated_done.at(s, INNER_CHUNKS))
                product(s, f"out{m}", cols(w_out_t, m * P), chunks(yv[slot]))

            def mean_tail(s, slot, _):
                pe.wait_ge(x1_done.sem, x1_done.at(s, CHUNKS))
                product(s, "mean2", means, chunks(x1_t))

            def var_tail(s, slot, _):
                pe.wait_ge(sq2_done.sem, sq2_done.at(s, 1))
                product(s, "var2", means, chunks(sq2))

            pipeline(pe, {"xT": turn_input, "hT": turn_normalised, "xs": project_x, "z": project_z, "bc": project_bc,
                          "dt": project_dt, "bfirst": spread_first_b, "bwide": spread_b, "sum": sum_states, "last": sum_states,
                          "out": project_out, "mean2": mean_tail, "var2": var_tail})

        @block.scalar
        def _(act):
            def deviation(s, name, to, read, ln, done):
                act.wait_ge(read.sem, read.at(s))
                work.wait_full(act, s, name)
                nc.scalar.activation(to[:], work.tile(name)[:], ACT.Ln, bias=ln_eps[:]).then_inc(ln.sem, 1)
                act.wait_ge(ln.sem, ln.at(s, 1))
                nc.scalar.activation(to[:], to[:], ACT.Exp, scale=-0.5).then_inc(done.sem, 1)

            def modulate(s, to, x, shift, scale, c):
                return nc.scalar.activation(to, x, ACT.Identity, bias=mod[:, 2 * shift + c, bass.ds(s, 1)],
                                            scale=mod[:, 2 * scale + c, bass.ds(s, 1)])

            def copy_input(s, slot, c):
                slot_free(act, s, x1_done)
                work.wait_full(act, s, f"xT{c}")
                nc.scalar.activation(x_t[slot][:, c, :], work.tile(f"xT{c}")[:], ACT.Copy).then_inc(x_t_done.sem, 1)

            def statistics(s, slot, _):
                act.wait_ge(xn_done.sem, xn_done.at(s))
                act.wait_ge(x_loaded.sem, x_loaded.at(s, 1))
                for t in range(TILES):
                    nc.scalar.activation(xn[:, t, :], xt[:, t, :], ACT.Copy, accum_out=neg_mean[:, t:t + 1]).then_inc(total_done.sem, 1)
                act.wait_ge(total_done.sem, total_done.at(s, TILES))
                nc.scalar.activation(neg_mean[:], neg_mean[:], ACT.Copy, scale=-1.0 / DIM).then_inc(mean_done.sem, 1)
                act.wait_ge(mean_done.sem, mean_done.at(s, 1))
                for t in range(TILES):
                    nc.scalar.activation(xn[:, t, :], xt[:, t, :], ACT.Square, bias=neg_mean[:, t:t + 1],
                                         accum_out=token_rate[:, t:t + 1]).then_inc(var_done.sem, 1)
                act.wait_ge(var_done.sem, var_done.at(s, TILES))
                nc.scalar.activation(token_rate[:], token_rate[:], ACT.Ln, scale=1.0 / DIM, bias=ln_eps[:]).then_inc(ln_done.sem, 1)
                act.wait_ge(ln_done.sem, ln_done.at(s, 1))
                nc.scalar.activation(token_rate[:], token_rate[:], ACT.Exp, scale=-0.5).then_inc(rate_done.sem, 1)

            def modulate_head(s, slot, _):
                act.wait_ge(dt_done.sem, dt_done.at(s))
                for c in range(CHUNKS):
                    work.wait_full(act, s, f"hT{c}")
                    modulate(s, h_t[c][:], work.tile(f"hT{c}")[:], MOD_SHIFT_A, MOD_SCALE_A, c).then_inc(h_done.sem, 1)
                act.wait_ge(z_done.sem, z_done.at(s))
                for c in range(CHUNKS):
                    act.wait_ge(h_done.sem, h_done.at(s, c + 1))
                    nc.scalar.activation(h_upper[:, c, :].bitcast(F32R), h_t[c][:], ACT.Copy).then_inc(h_upper_done.sem, 1)

            def copy_x(s, slot, m):
                slot_free(act, s, gated_done)
                work.wait_full(act, s, f"xs{m}")
                nc.scalar.activation(xs[slot][:, m, :], work.tile(f"xs{m}")[:], ACT.Copy).then_inc(xs_done.sem, 1)

            def copy_z(s, slot, m):
                slot_free(act, s, gated_done)
                work.wait_full(act, s, f"z{m}")
                nc.scalar.activation(sz[slot][:, m, :], work.tile(f"z{m}")[:], ACT.Copy).then_inc(z_done.sem, 1)

            def silu(s, slot, _):
                act.wait_ge(z_done.sem, z_done.at(s, INNER_CHUNKS))
                nc.scalar.activation(sz[slot][:], sz[slot][:], ACT.Silu).then_inc(silu_done.sem, 1)
                nc.scalar.preload_act_table_set(EXP_AND_LN)

            def softplus(s, slot, m):
                bias = b_dt[:, m:m + 1]
                act.wait_ge(dt_done.sem, dt_done.at(s, m))
                if m == 0:
                    act.wait_ge(h_cut.sem, h_cut.at(s, CHUNKS))
                work.wait_full(act, s, f"dt{m}")
                nc.scalar.activation(sp_relu[:], work.tile(f"dt{m}")[:], ACT.Relu, bias=bias)
                nc.scalar.activation(sp_e[:], work.tile(f"dt{m}")[:], ACT.Abs, bias=bias).then_inc(abs_done.sem, 1)
                act.wait_ge(abs_done.sem, abs_done.at(s, m + 1))
                nc.scalar.activation(sp_e[:], sp_e[:], ACT.Exp, scale=-1.0).then_inc(exp_done.sem, 1)
                act.wait_ge(exp_done.sem, exp_done.at(s, m + 1))
                if m == 0:
                    act.wait_ge(parts_done.sem, parts_done.at(s, 5))
                nc.scalar.activation(sp_p[:], sp_e[:], ACT.Identity, scale=-0.25, bias=third[:]).then_inc(series_begun.sem, 1)
                nc.scalar.activation(sp_mask[:], sp_e[:], ACT.Relu, bias=below[:])
                nc.scalar.activation(sp_ln[:], sp_e[:], ACT.Ln, bias=1.0).then_inc(log_done.sem, 1)

            def copy_bc(s, slot, _):
                act.wait_ge(c_stored.sem, c_stored.at(s))
                act.wait_ge(parts_done.sem, parts_done.at(s))
                work.wait_full(act, s, "bc")
                nc.scalar.activation(bc[:], work.tile("bc")[0:2 * STATES, :], ACT.Copy).then_inc(bc_done.sem, 1)
                act.wait_ge(bc_done.sem, bc_done.at(s, 1))
                act.dma_start(c_dram[s], bc[STATES:, :]).then_inc(c_stored.sem, 16)

            def load_c(s, slot, g):
                if g >= 2:
                    cmul_until(act, s, INNER_CHUNKS * (g - 1))
                elif not (isinstance(s, int) and s == 0):
                    cmul_until(act, s - 1, INNER_CHUNKS * (GROUPS - 1 + g))
                if g == 0:
                    act.wait_ge(c_stored.sem, c_stored.at(s, 1))
                act.dma_start(c_wide[g % 2][:], c_dram[s, GROUP * g:GROUP * (g + 1), :].unsqueeze(0).to_broadcast([P, GROUP, SEQ]))\
                    .then_inc(c_loaded[g % 2].sem, 16)

            def decays(s, slot, q):
                for k in (0, 1, 2) if q == 0 else (q + 2,) if q + 2 < UNITS else ():
                    g, d = divmod(k, INNER_CHUNKS)
                    act.wait_ge(dt_done.sem, dt_done.at(s, INNER_CHUNKS))
                    unit_slot_free(act, s, k, DECAY_SLOTS, scan_done)
                    for j in range(GROUP):
                        n = GROUP * g + j
                        last = nc.scalar.activation(decay[k % DECAY_SLOTS][:, j, 1:SEQ], dt[slot][:, d, 1:SEQ], ACT.Exp,
                                                    scale=neg_a[:, d, n:n + 1])
                    last.then_inc(decay_done.sem, 1)

            def square_tail(s, slot, _):
                act.wait_ge(stored.sem, stored.at(s))
                act.wait_ge(xc2_done.sem, xc2_done.at(s, CHUNKS))
                nc.scalar.activation(sq2[:], xc2[:], ACT.Square).then_inc(sq2_done.sem, 1)

            def deviation_tail(s, slot, _):
                deviation(s, "var2", rstd2, xn2_done, ln2_done, rstd2_done)

            def modulate_tail(s, slot, _):
                act.wait_ge(xn2_done.sem, xn2_done.at(s, 1))
                for c in range(CHUNKS):
                    modulate(s, h2_t[:, c, :], xc2[:, c, :], MOD_SHIFT_B, MOD_SCALE_B, c).then_inc(h2_done.sem, 1)

            nc.scalar.preload_act_table_set(EXP_AND_LN)
            pipeline(act, {"xcopy": copy_input, "stat": statistics, "h1": modulate_head, "xscopy": copy_x, "zcopy": copy_z,
                           "silu": silu, "soft": softplus, "bccopy": copy_bc, "cfirst": load_c, "cwide": load_c, "unit": decays,
                           "sq2": square_tail, "dev2": deviation_tail, "h2": modulate_tail})

        @block.vector
        def _(dve):
            def centre(s, name, to, source, read, done):
                dve.wait_ge(read.sem, read.at(s))
                work.wait_full(dve, s, name)
                for c in range(CHUNKS):
                    nc.vector.tensor_tensor(to[:, c, :], source[:, c, :], work.tile(name)[:], ALU.subtract).then_inc(done.sem, 1)

            def normalise(s, x, rate, rate_done, squared, done):
                dve.wait_ge(rate_done.sem, rate_done.at(s, 1))
                dve.wait_ge(squared.sem, squared.at(s, 1))
                nc.vector.tensor_tensor(x[:], x[:], rate[:].unsqueeze(1).to_broadcast([P, CHUNKS, SEQ]), ALU.mult)\
                    .then_inc(done.sem, 1)

            def normalise_head(s, slot, _):
                dve.wait_ge(rate_done.sem, rate_done.at(s, 1))
                for t in range(TILES):
                    nc.vector.tensor_scalar(xn[:, t, :], xt[:, t, :], neg_mean[:, t:t + 1], token_rate[:, t:t + 1],
                                            ALU.add, ALU.mult).then_inc(xn_done.sem, 1)

            def cut_h(s, slot, _):
                for c in range(CHUNKS):
                    dve.wait_ge(h_upper_done.sem, h_upper_done.at(s, c + 1))
                    nc.vector.tensor_tensor(h_lower[:, c, :].bitcast(F32R), h_t[c][:], h_upper[:, c, :], ALU.subtract)\
                        .then_inc(h_cut.sem, 1)

            def cut_bc(s, slot, _):
                parts = bc_parts[slot]
                slot_free(dve, s, input_done)
                dve.wait_ge(bc_done.sem, bc_done.at(s, 1))
                nc.vector.tensor_copy(parts[0:32, :], bc[:]).then_inc(parts_done.sem, 1)
                dve.wait_ge(parts_done.sem, parts_done.at(s, 1))
                nc.vector.tensor_tensor(bc_rest, bc[:], parts[0:32, :], ALU.subtract).then_inc(parts_done.sem, 1)
                dve.wait_ge(parts_done.sem, parts_done.at(s, 2))
                nc.vector.tensor_copy(bc_mid[:], bc_rest).then_inc(parts_done.sem, 1)
                nc.vector.tensor_copy(parts[32:64, :], bc_rest).then_inc(parts_done.sem, 1)
                dve.wait_ge(parts_done.sem, parts_done.at(s, 3))
                nc.vector.tensor_tensor(parts[64:96, :], bc_rest, bc_mid[:], ALU.subtract).then_inc(parts_done.sem, 1)

            def step_size(s, slot, m):
                def step(k):
                    dve.wait_ge(series_done.sem, series_done.at(s, 4 * m + k))

                if m == 0:
                    slot_free(dve, s, x1_done)
                dve.wait_ge(series_begun.sem, series_begun.at(s, m + 1))
                nc.vector.tensor_tensor(sp_p[:], sp_p[:], sp_e[:], ALU.mult).then_inc(series_done.sem, 1)
                step(1)
                nc.vector.scalar_tensor_tensor(sp_p[:], sp_p[:], -0.5, sp_e[:], ALU.add, ALU.mult).then_inc(series_done.sem, 1)
                step(2)
                nc.vector.scalar_tensor_tensor(sp_p[:], sp_p[:], 1.0, sp_e[:], ALU.add, ALU.mult).then_inc(series_done.sem, 1)
                step(3)
                dve.wait_ge(log_done.sem, log_done.at(s, m + 1))
                nc.vector.memset(waiter[:, m:m + 1], 0.0)
                nc.vector.copy_predicated(sp_p[:], sp_mask[:].bitcast(I32), sp_ln[:]).then_inc(series_done.sem, 1)
                step(4)
                nc.vector.tensor_tensor(dt[slot][:, m, :], sp_p[:], sp_relu[:], ALU.add).then_inc(dt_done.sem, 1)
                dve.wait_ge(dt_done.sem, dt_done.at(s, m + 1))
                dve.wait_ge(xs_done.sem, xs_done.at(s, INNER_CHUNKS))
                nc.vector.tensor_tensor(u[slot][:, m, :], dt[slot][:, m, :], xs[slot][:, m, :], ALU.mult).then_inc(u_done.sem, 1)

            def scan_input(s, slot, q):
                g, d = divmod(q, INNER_CHUNKS)
                dve.wait_ge(u_done.sem, u_done.at(s, INNER_CHUNKS))
                for i in range(GROUP):
                    work.wait_full(dve, s, b_name(g, i))
                unit_slot_free(dve, s, q, STATE_SLOTS, sum_done)
                nc.vector.tensor_tensor(state[q % STATE_SLOTS][:], u[slot][:, d, :].unsqueeze(1).to_broadcast([P, GROUP, SEQ]),
                                        b_wide[:], ALU.mult).then_inc(input_done.sem, 1)

            inputs_at = {q: {0: (q + 1,), 1: (q + 1, q + 2), 2: (), 3: (q + 1,)}[q % INNER_CHUNKS] for q in range(UNITS)}
            inputs_at[0], inputs_at[UNITS - 1] = (0, 1), ()

            def scan(s, slot, q):
                g, d = divmod(q, INNER_CHUNKS)
                for k in inputs_at[q]:
                    scan_input(s, slot, k)
                dve.wait_ge(decay_done.sem, decay_done.at(s, q + 1))
                dve.wait_ge(input_done.sem, input_done.at(s, q + 1))
                h = state[q % STATE_SLOTS]
                flat = h[:].rearrange("p g s -> p (g s)")
                nc.vector.tensor_tensor_scan(flat, decay[q % DECAY_SLOTS][:].rearrange("p g s -> p (g s)"), flat, 0.0,
                                             ALU.mult, ALU.add).then_inc(scan_done.sem, 1)
                if q in on_vector:
                    dve.wait_ge(scan_done.sem, scan_done.at(s, q + 1))
                    dve.wait_ge(c_loaded[g % 2].sem, c_loaded[g % 2].at(s, g // 2 + 1))
                    nc.vector.tensor_tensor(h[:], h[:], c_wide[g % 2][:], ALU.mult).then_inc(cmul_vec_done.sem, 1)

            def gate(s, slot, d):
                dve.wait_ge(sum_done.sem, sum_done.at(s, UNITS - INNER_CHUNKS + d + 1))
                dve.wait_ge(silu_done.sem, silu_done.at(s, 1))
                nc.vector.scalar_tensor_tensor(yv[slot][:, d, :], xs[slot][:, d, :], skip_d[:, d:d + 1], y_sum[d][:],
                                               ALU.mult, ALU.add).then_inc(skip_done.sem, 1)
                dve.wait_ge(skip_done.sem, skip_done.at(s, d + 1))
                nc.vector.tensor_tensor(yv[slot][:, d, :], yv[slot][:, d, :], sz[slot][:, d, :], ALU.mult).then_inc(gated_done.sem, 1)

            def residual(s, slot, m):
                dve.wait_ge(stored.sem, stored.at(s))
                work.wait_full(dve, s, f"out{m}")
                nc.vector.scalar_tensor_tensor(x1_t[:, m, :], work.tile(f"out{m}")[:], mod[:, 2 * MOD_GATE_A + m, bass.ds(s, 1)],
                                               x_t[slot][:, m, :], ALU.mult, ALU.add).then_inc(x1_done.sem, 1)

            def centre_tail(s, slot, _):
                centre(s, "mean2", xc2, x1_t, h2_done, xc2_done)

            def normalise_tail(s, slot, _):
                normalise(s, xc2, rstd2, rstd2_done, sq2_done, xn2_done)

            pipeline(dve, {"norm": normalise_head, "hcut": cut_h, "cut": cut_bc, "step": step_size, "unit": scan,
                           "gate": gate, "res": residual, "cen2": centre_tail, "xn2": normalise_tail})

        @block.gpsimd
        def _(pool):
            def times_c(s, slot, q):
                if q in on_pool:
                    g = q // INNER_CHUNKS
                    pool.wait_ge(c_loaded[g % 2].sem, c_loaded[g % 2].at(s, g // 2 + 1))
                    pool.wait_ge(scan_done.sem, scan_done.at(s, q + 1))
                    h = state[q % STATE_SLOTS]
                    nc.gpsimd.tensor_tensor(h[:], h[:], c_wide[g % 2][:], ALU.mult).then_inc(cmul_pool_done.sem, 1)

            pipeline(pool, {"unit": times_c})


STEPS = {1: "hxs pq pk psq pss prate pnorm prot padd ptr ptc v vc",
         2: "score mask exp pt att onorm ot otc",
         3: "wo add mean cen sq sqs var dev xn hn hns ga gelu gated wd fin sum turn turnc"}
STAGE = {step: stage for stage, steps in STEPS.items() for step in steps.split()}
LAST_LAYER = ("sum", "turn", "turnc")
LEAD = {1: 1, 2: 0, 3: -1}
ORDER = """
score:0.0 exp:0 psq:0 hxs:0 mask:0.0 wo:0 wo:1 add:0 score:0.1 add:1 mask:0.1 pq:0 sq:0 cen:0 prate:0 mask:1.0 mean:0
score:1.0 pss:0 pk:0 pt:0.0 pt:0.1 score:1.1 sqs:0 mask:1.1 pnorm:0 var:0 dev:0 att:0 exp:1 v:0 score:2.0 vc:0 prot:0
onorm:0 padd:0 ptr:0 xn:0 ptc:0 ot:0 otc:0 pq:1 pk:1 psq:1 mask:2.0 hn:0 pss:1 pt:1.0 pt:1.1 score:2.1 prate:1 pt:1.2
mask:2.1 pnorm:1 pt:1.3 mask:3.0 prot:1 exp:2 vc:1 padd:1 score:3.0 v:1 att:1 onorm:1 ptr:1 ptc:1 ot:1 otc:1 pss:2
pq:2 pk:2 psq:2 pt:2.0 prate:2 pt:2.1 mask:3.1 score:3.1 pt:2.2 pnorm:2 exp:3 pt:2.3 prot:2 v:2 padd:2 vc:2 ptc:2
hns:0 att:2 onorm:2 pss:3 ptr:2 pq:3 pk:3 ot:2 ga:0 psq:3 otc:2 prate:3 gated:0 gelu:0 pt:3.0 pt:3.1 pnorm:3 gated:1
gelu:1 ga:1 prot:3 pt:3.2 gelu:2 pt:3.3 v:3 ga:2 att:3 gated:2 vc:3 gelu:3 gelu:4 ptr:3 padd:3 gated:3 onorm:3 ga:3
gated:4 ga:4 ptc:3 gated:5 fin:0 gelu:5 otc:3 sum:0 ga:5 wd:0 wd:1 turnc:0 ot:3 turn:0 fin:1 sum:1 turn:1 turnc:1
"""
SCHEDULE = steps_of(ORDER)


def stack_pass(nc, inp, mod, x1_dram, stack_dram, parts_dram, out):
    SEQS = DEPTH * BATCH
    with ExitStack() as ctx:
        def sb(name, shape, dt=F32):
            return ctx.enter_context(nc.sbuf_tensor("b_" + name, shape, dt))

        def sem(name):
            return ctx.enter_context(nc.semaphore("b_" + name))

        signals = []

        def signal(name, per_pass, unit=1):
            signals.append(Signal(sem(name), per_pass, unit))
            return signals[-1]

        banks_all = [ctx.enter_context(nc.psum_tensor(f"b_bank{i}", [P, 512], F32)) for i in range(8)]
        s_banks = banks_all[4:6]

        squares = sb("squares", [P, 4, P])
        ident, mean_mat = (squares[:, i, :] for i in range(2))
        mask = squares[:, 2:4, :].rearrange("p a b -> p (a b)")
        w_qkv = [sb(f"w_qkv{i}", [P, CHUNKS, 3 * INNER]) for i in range(2)]
        w_o = sb("w_o", [P, PAIRS, DIM])
        w_1 = [sb(f"w_1{i}", [P, CHUNKS, W_1_COLS]) for i in range(2)]
        w_2 = sb("w_2", [P, HID_CHUNKS, DIM])
        rotary = [sb(f"rotary{l}", [P, TILES, 2, 2, DIM_HEAD]) for l in range(DEPTH)]
        ln_g = sb("ln_g", [P, SEQS, CHUNKS])
        ln_b = sb("ln_b", [P, SEQS, CHUNKS])
        b_1a = sb("b_1a", [P, SEQS, HID_CHUNKS])
        b_1g = sb("b_1g", [P, SEQS, HID_CHUNKS])
        b_2 = sb("b_2", [P, SEQS, CHUNKS])
        load_stack_weights(nc, inp, squares, rotary, ln_g, ln_b, b_1a, b_1g, b_2, w_qkv, w_1, parts_dram)

        eps_bias = sb("eps_bias", [P, 1])
        norm_bias = sb("norm_bias", [P, 1])
        waiter = sb("waiter", [P, TILES * PAIRS])

        hx = sb("hx", [P, CHUNKS, SEQ + 1])
        hx_upper, hx_lower = (sb(f"hx_part{i}", [P, CHUNKS, SEQ]) for i in range(2))
        qk_rate = sb("qk_rate", [P, 2, HEADS])
        qk = sb("qk", [P, 2, INNER])
        by_cos = sb("by_cos", [P, 2, INNER])
        qk_rot = sb("qk_rot", [P, 2, INNER])
        qk_sq = qk_rot
        q_t = sb("q_t", [P, PAIRS, SEQ])
        k_t = sb("k_t", [P, PAIRS, SEQ])
        v = [sb(f"v{i}", [P, TILES, INNER]) for i in range(2)]
        scores = [sb(f"scores{i}", [P, HEADS, 2 * WINDOW]) for i in range(2)]
        probs_t = [sb(f"probs_t{i}", [P, 2 * HEADS, WINDOW]) for i in range(2)]
        row_max = sb("row_max", [P, TILES, HEADS])
        row_bias = sb("row_bias", [P, TILES, HEADS])
        row_sum = sb("row_sum", [P, TILES, HEADS])
        row_rate = sb("row_rate", [P, TILES, HEADS])
        o = [sb(f"o{i}", [P, INNER]) for i in range(2)]
        o_t = sb("o_t", [P, PAIRS, SEQ])
        x_res = sb("x_res", [P, CHUNKS, SEQ])
        x2 = sb("x2", [P, CHUNKS, SEQ + 1])
        xc = sb("xc", [P, CHUNKS, SEQ])
        rstd = sb("rstd", [P, SEQ])
        x2_sum = rstd
        hn = xc
        hn_upper, hn_lower = (sb(f"hn_part{i}", [P, CHUNKS, SEQ]) for i in range(2))
        gelu = [sb(f"gelu{i}", [P, SEQ]) for i in range(2)]
        h2 = sb("h2", [P, HID_CHUNKS, SEQ])
        sq = h2[:, 0:CHUNKS, :]
        x1_t = gelu
        tokens = h2[:, CHUNKS:2 * CHUNKS, :]
        x_out = xc

        def shifted(x, c):
            return x[:, c, 0:SEQ]

        def plain(x, c):
            return x[:, c, c:c + SEQ]

        def by_head(x):
            return x[:].rearrange("p x (h d) -> p x h d", d=DIM_HEAD)

        def for_heads(table, width):
            return table.unsqueeze(2).to_broadcast([P, 2, HEADS, width])

        def tokens_of(x):
            return x.rearrange("p c s -> p (c s)").rearrange("p (t d) -> p t d", d=DIM)

        def hid_rows(m):
            return min(P, HID - m * P)

        hx_loaded = signal("hx_loaded", CHUNKS, 16)
        hx_cut = signal("hx_cut", 2)
        qk_sq_done = signal("qk_sq_done", 2 * TILES)
        qk_sum_done = signal("qk_sum_done", TILES)
        qk_floor_done = signal("qk_floor_done", TILES)
        qk_ln_done = signal("qk_ln_done", TILES)
        qk_rate_done = signal("qk_rate_done", TILES)
        qk_done = signal("qk_done", 2 * TILES)
        by_cos_done = signal("by_cos_done", TILES)
        by_sin_done = signal("by_sin_done", 2 * TILES)
        qk_rot_done = signal("qk_rot_done", TILES)
        q_t_done = signal("q_t_done", TILES)
        k_t_done = signal("k_t_done", TILES)
        v_done = signal("v_done", TILES)
        masked_done = signal("masked_done", TILES * PAIRS)
        row_bias_done = signal("row_bias_done", TILES)
        probs_done = signal("probs_done", TILES * PAIRS)
        row_rate_done = signal("row_rate_done", TILES)
        o_done = signal("o_done", TILES)
        o_t_done = signal("o_t_done", TILES)
        turn_uses = [(w, i) for w in range(TILES) for i in range(4 if w else 2)]
        on_act = [x for n, x in enumerate(turn_uses) if n % 2 == 0]
        on_dve = [x for n, x in enumerate(turn_uses) if n % 2 == 1]
        probs_t_act = signal("probs_t_act", len(on_act))
        probs_t_dve = signal("probs_t_dve", len(on_dve))
        x_res_loaded = signal("x_res_loaded", 1, 16)
        x2_done = signal("x2_done", CHUNKS)
        xc_done = signal("xc_done", CHUNKS)
        x2_added = signal("x2_added", 1)
        sq_done = signal("sq_done", 1)
        sq_added = signal("sq_added", 1)
        ln_done = signal("ln_done", 1)
        rstd_done = signal("rstd_done", 1)
        xn_done = signal("xn_done", 1)
        hn_done = signal("hn_done", CHUNKS)
        hn_cut = signal("hn_cut", 2)
        gelu_done = signal("gelu_done", HID_CHUNKS)
        h2_done = signal("h2_done", HID_CHUNKS)
        x_out_done = signal("x_out_done", CHUNKS)
        stored = signal("stored", 1, 16)
        x1_loaded = signal("x1_loaded", CHUNKS, 16)
        y_done = signal("y_done", CHUNKS)
        turned = [signal(f"turned{i}", 1) for i in range(2)]
        tokens_done = signal("tokens_done", 2)
        out_stored = signal("out_stored", 1, 16)
        qkv_loaded = [sem(f"w_{x}_loaded") for x in "qkv"]
        w_o_loaded, w_1_loaded, w_2_loaded = sem("w_o_loaded"), sem("w_1_loaded"), sem("w_2_loaded")

        def probs_t_signal(w, i):
            return (probs_t_act, on_act.index((w, i)) + 1) if (w, i) in on_act else (probs_t_dve, on_dve.index((w, i)) + 1)

        def probs_t_until(w):
            return (sum(1 for x in on_act if x[0] <= w), sum(1 for x in on_dve if x[0] <= w))

        uses, next_bank = [], {1: 0, 2: 6, 3: 2}

        def use_next(stage, name, reader, k):
            uses.append((name, next_bank[stage], reader, k))
            next_bank[stage] ^= 1

        for name, k, *i in SCHEDULE:
            if name in ("pq", "pk"):
                use_next(1, f"{name[1]}{k}", qk_done, 2 * k + (1 if name == "pq" else 2))
            elif name == "ptr":
                use_next(1, f"q_t{k}", q_t_done, k + 1)
                use_next(1, f"k_t{k}", k_t_done, k + 1)
            elif name == "v":
                use_next(1, f"v{k}", v_done, k + 1)
            elif name == "wo":
                use_next(3, f"wo{k}", x2_done, k + 1)
            elif name == "mean":
                use_next(3, "mean", xc_done, CHUNKS)
            elif name == "var":
                use_next(3, "var", ln_done, 1)
            elif name == "ga":
                use_next(3, f"g{k}", gelu_done if k < HID // P else h2_done, k + 1)
                if k < HID // P:
                    use_next(3, f"a{k}", h2_done, k + 1)
            elif name == "wd":
                use_next(3, f"wd{k}", x_out_done, k + 1)
            elif name == "score":
                g = i[0]
                uses += [(f"s{k}_{g}_{h}", 4 + h, masked_done, PAIRS * k + 2 * g + h + 1) for h in range(2)]
            elif name == "pt":
                use_next(2, f"pt{k}_{i[0]}", *probs_t_signal(k, i[0]))
            elif name == "ot":
                use_next(2, f"ot{k}", o_t_done, k + 1)
            elif name == "att":
                use_next(2, f"o{k}", o_done, k + 1)
        psum = Banks(banks_all, [sem(f"full{i}") for i in range(8)], uses)

        def blocks_of(w, i):
            return [(2 * i + h, blk) for h in range(2) for blk in range(2)] if w else [(4 * i + h, 1) for h in range(4)]

        def keys_of(w):
            return (0, 2 * WINDOW) if w else (WINDOW, 2 * WINDOW)

        def pipeline(eng, steps):
            def one_pass(i, parity, stages, layers):
                for name, *at in SCHEDULE:
                    stage, lead = STAGE[name], LEAD[STAGE[name]]
                    if stage in stages and name in steps and (name not in LAST_LAYER or layers[stage] == DEPTH - 1):
                        of = [layers[stage]] if stage in layers else []
                        steps[name](i + lead, (parity + lead) % 2, *of, *at)

            def passes(first, end, layers):
                with eng.Fori(first // 2, end // 2) as j:
                    one_pass(2 * j + 1, 1, (1, 2, 3), layers)
                    one_pass(2 * j + 2, 0, (1, 2, 3), layers)

            one_pass(-1, 1, (1,), {1: 0})
            one_pass(0, 0, (1, 2), {1: 0})
            passes(1, BATCH - 1, {1: 0, 3: 0})
            one_pass(BATCH - 1, 1, (1, 2, 3), {1: 1, 3: 0})
            one_pass(BATCH, 0, (1, 2, 3), {1: 1, 3: 0})
            passes(BATCH + 1, SEQS - 1, {1: 1, 3: 1})
            one_pass(SEQS - 1, 1, (2, 3), {3: 1})
            one_pass(SEQS, 0, (3,), {3: 1})

        with nc.Block() as block:
            @block.vector
            def _(dve):
                nc.vector.memset(eps_bias[:], LN_EPS)
                nc.vector.memset(norm_bias[:], 0.5 * float(np.log(SCREEN)))
                nc.vector.memset(hx[:, 1, 0:1], 0.0)
                nc.vector.memset(x2[:, 1, 0:1], 0.0)
                nc.vector.memset(row_sum[:], 0.0)

        start_signals(nc, signals)
        block = ctx.enter_context(nc.Block())

        @block.sync
        def _(sp):
            def load_qkv():
                for i, done in enumerate(qkv_loaded):
                    at = slice(i * INNER, (i + 1) * INNER)
                    for to, source in zip(w_qkv, parts_dram["qkv"]):
                        sp.dma_start(to[:, :, at], source[:, :, at]).then_inc(done, 16)

            def load_w_o(l):
                sp.dma_start(w_o[:], inp["L0_ffn_wo"][l].rearrange("(c p) f -> p c f", p=P)).then_inc(w_o_loaded, 16)

            def load_w_1():
                for to, source in zip(w_1, parts_dram["w_1"]):
                    sp.dma_start(to[:], source).then_inc(w_1_loaded, 16)

            def load_w_2(l):
                whole = HID // P
                sp.dma_start(w_2[:, 0:whole, :], inp["L0_ffn_w2"][l, 0:whole * P].rearrange("(c p) f -> p c f", p=P))\
                    .then_inc(w_2_loaded, 16)
                sp.dma_start(w_2[0:HID - whole * P, whole, :], inp["L0_ffn_w2"][l, whole * P:HID]).then_inc(w_2_loaded, 16)

            def load_hx(s):
                sp.wait_ge(v_done.sem, v_done.at(s))
                for c in range(CHUNKS):
                    sp.dma_start(plain(hx, c), stack_dram[s, :, c, :]).then_inc(hx_loaded.sem, 16)

            def load_res(s):
                sp.wait_ge(x2_done.sem, x2_done.at(s))
                sp.dma_start(x_res[:], stack_dram[s]).then_inc(x_res_loaded.sem, 16)

            def store(s):
                sp.wait_ge(x_out_done.sem, x_out_done.at(s, CHUNKS))
                sp.dma_start(stack_dram[s + BATCH], x_out[:]).then_inc(stored.sem, 16)

            def finish(s):
                b = s - BATCH
                sp.wait_ge(h2_done.sem, h2_done.at(s, HID_CHUNKS))
                for c in range(CHUNKS):
                    sp.dma_start(x1_t[c][:], x1_dram[b, :, c, :]).then_inc(x1_loaded.sem, 16)
                sp.wait_ge(tokens_done.sem, tokens_done.at(b, 2))
                sp.dma_start(out[b].rearrange("(t p) d -> p t d", p=P), tokens_of(tokens)).then_inc(out_stored.sem, 16)

            load_hx(0)
            load_w_o(0)
            load_w_2(0)
            load_hx(1)
            load_res(0)
            load_hx(2)
            with sp.Fori(1, BATCH - 2) as i:
                load_res(i)
                load_hx(i + 2)
                store(i - 1)
            load_res(BATCH - 2)
            sp.wait_ge(v_done.sem, v_done.at(BATCH))
            sp.wait_ge(stored.sem, stored.at(1))
            load_hx(BATCH)
            load_qkv()
            store(BATCH - 3)
            load_res(BATCH - 1)
            sp.wait_ge(stored.sem, stored.at(2))
            load_hx(BATCH + 1)
            store(BATCH - 2)
            sp.wait_ge(x2_done.sem, x2_done.at(BATCH))
            load_w_o(1)
            load_res(BATCH)
            sp.wait_ge(stored.sem, stored.at(3))
            load_hx(BATCH + 2)
            sp.wait_ge(h2_done.sem, h2_done.at(BATCH))
            load_w_1()
            store(BATCH - 1)
            load_w_2(1)
            with sp.Fori(BATCH + 1, SEQS - 2) as i:
                load_res(i)
                sp.wait_ge(stored.sem, stored.at(i + 3 - BATCH))
                load_hx(i + 2)
                finish(i - 1)
            for i in range(SEQS - 2, SEQS):
                load_res(i)
                finish(i - 1)
            finish(SEQS - 1)
            sp.wait_ge(stored.sem, stored.at(BATCH))
            sp.wait_ge(out_stored.sem, out_stored.at(BATCH))

        @block.tensor
        def _(pe):
            def product(s, name, weights, cols, sources, rows=P):
                psum.wait_free(pe, s, name)
                for c, source in enumerate(sources):
                    last = nc.tensor.matmul(psum.tile(name)[0:rows, :], weights[0:source.shape[0], c, cols:cols + rows], source,
                                            start=(c == 0), stop=(c == len(sources) - 1))
                psum.filled(last, name)

            def by_token(s, name, w, cols):
                psum.wait_free(pe, s, name)
                parts = ((hx_upper, w_qkv[0]), (hx_upper, w_qkv[1]), (hx_lower, w_qkv[0]))
                for n, (x, weights) in enumerate(parts):
                    for c in range(CHUNKS):
                        last = nc.tensor.matmul(psum.tile(name)[:], x[:, c, w * P:(w + 1) * P].bitcast(F32R),
                                                weights[:, c, cols:cols + INNER].bitcast(F32R), start=(n == 0 and c == 0),
                                                stop=(n == len(parts) - 1 and c == CHUNKS - 1))
                psum.filled(last, name)

            def project_q(s, slot, layer, w):
                if w == 0:
                    pe.wait_ge(hx_cut.sem, hx_cut.at(s, 2))
                if isinstance(s, int) and s == BATCH and w == 0:
                    pe.wait_ge(qkv_loaded[0], 16 * 2)
                by_token(s, f"q{w}", w, 0)

            def project_k(s, slot, layer, w):
                if isinstance(s, int) and s == BATCH and w == 0:
                    pe.wait_ge(qkv_loaded[1], 16 * 2)
                by_token(s, f"k{w}", w, INNER)

            def turn_qk(s, slot, layer, w):
                pe.wait_ge(qk_rot_done.sem, qk_rot_done.at(s, w + 1))
                for i, stem in enumerate("qk"):
                    psum.wait_free(pe, s, f"{stem}_t{w}")
                    for p in range(PAIRS):
                        last = nc.tensor.transpose(psum.tile(f"{stem}_t{w}")[:, p * P:(p + 1) * P],
                                                   qk_rot[:, i, p * P:(p + 1) * P], ident)
                    psum.filled(last, f"{stem}_t{w}")

            def values(s, slot, layer, w):
                if isinstance(s, int) and s == BATCH and w == 0:
                    pe.wait_ge(qkv_loaded[2], 16 * 2)
                by_token(s, f"v{w}", w, 2 * INNER)

            def score(s, slot, w, g):
                lo, hi = keys_of(w)
                if w == 0 and g == 0:
                    pe.wait_ge(q_t_done.sem, q_t_done.at(s, TILES))
                    pe.wait_ge(k_t_done.sem, k_t_done.at(s, TILES))
                first = w * WINDOW - (WINDOW - lo)
                for h in range(2):
                    psum.wait_free(pe, s, f"s{w}_{g}_{h}")
                for n in range(2):
                    for h in range(2):
                        at, p = slice(h * DIM_HEAD, (h + 1) * DIM_HEAD), 2 * g + n
                        last = nc.tensor.matmul(s_banks[h][:, n * 2 * WINDOW + lo:n * 2 * WINDOW + hi],
                                                q_t[at, p, w * WINDOW:(w + 1) * WINDOW],
                                                k_t[at, p, first:first + hi - lo], start=True, stop=True)
                        if n:
                            psum.filled(last, f"s{w}_{g}_{h}")

            def turn_probs(s, slot, w, i):
                name, blocks = f"pt{w}_{i}", blocks_of(w, i)
                psum.wait_free(pe, s, name)
                pe.wait_ge(probs_done.sem, probs_done.at(s, PAIRS * w + blocks[-1][0] // 2 + 1))
                for n, (h, blk) in enumerate(blocks):
                    last = nc.tensor.transpose(psum.tile(name)[:, n * P:(n + 1) * P],
                                               scores[w % 2][:, h, blk * WINDOW:(blk + 1) * WINDOW], ident)
                psum.filled(last, name)

            def attend(s, slot, w):
                by_act, by_dve = probs_t_until(w)
                pe.wait_ge(probs_t_act.sem, probs_t_act.at(s, by_act))
                pe.wait_ge(probs_t_dve.sem, probs_t_dve.at(s, by_dve))
                if w == 0:
                    pe.wait_ge(v_done.sem, v_done.at(s, TILES))
                psum.wait_free(pe, s, f"o{w}")
                for h in range(HEADS):
                    blocks = (0, 1) if w else (1,)
                    for blk in blocks:
                        last = nc.tensor.matmul(psum.tile(f"o{w}")[:, h * DIM_HEAD:(h + 1) * DIM_HEAD], probs_t[w % 2][:, 2 * h + blk, :],
                                                v[slot][:, w - 1 + blk, h * DIM_HEAD:(h + 1) * DIM_HEAD],
                                                start=(blk == blocks[0]), stop=(blk == 1))
                psum.filled(last, f"o{w}")

            def turn_output(s, slot, w):
                pe.wait_ge(o_done.sem, o_done.at(s, w + 1))
                psum.wait_free(pe, s, f"ot{w}")
                for p in range(PAIRS):
                    last = nc.tensor.transpose(psum.tile(f"ot{w}")[:, p * P:(p + 1) * P], o[w % 2][:, p * P:(p + 1) * P], ident)
                psum.filled(last, f"ot{w}")

            def project_out(s, slot, layer, m):
                if m == 0 and layer == DEPTH - 1:
                    pe.wait_ge(tokens_done.sem, tokens_done.at(s - BATCH))
                if m == 0:
                    pe.wait_ge(o_t_done.sem, o_t_done.at(s, TILES))
                    pe.wait_ge(w_o_loaded, 16 * (layer + 1))
                product(s, f"wo{m}", w_o, m * P, [o_t[:, p, :] for p in range(PAIRS)])

            def mean(s, slot, layer, _):
                pe.wait_ge(x2_added.sem, x2_added.at(s, 1))
                psum.wait_free(pe, s, "mean")
                psum.filled(nc.tensor.matmul(psum.tile("mean")[:], mean_mat, x2_sum[:], start=True, stop=True), "mean")

            def var(s, slot, layer, _):
                pe.wait_ge(sq_added.sem, sq_added.at(s, 1))
                psum.wait_free(pe, s, "var")
                psum.filled(nc.tensor.matmul(psum.tile("var")[:], mean_mat, sq[:, 0, :], start=True, stop=True), "var")

            def gate_and_value(s, slot, layer, m):
                if m == 0:
                    pe.wait_ge(hn_cut.sem, hn_cut.at(s, 2))
                    if layer:
                        pe.wait_ge(w_1_loaded, 16 * 2)
                whole = HID // P
                for stem, at in ((("g", whole + m), ("a", m)) if m < whole else (("g", 2 * whole),)):
                    psum.wait_free(pe, s, f"{stem}{m}")
                    parts = ((w_1[0], hn_upper), (w_1[1], hn_upper), (w_1[0], hn_lower))
                    for n, (weights, x) in enumerate(parts):
                        for c in range(CHUNKS):
                            last = nc.tensor.matmul(psum.tile(f"{stem}{m}")[:], weights[:, c, at * P:(at + 1) * P].bitcast(F32R),
                                                    x[:, c, :].bitcast(F32R), start=(n == 0 and c == 0),
                                                    stop=(n == len(parts) - 1 and c == CHUNKS - 1))
                    psum.filled(last, f"{stem}{m}")

            def project_down(s, slot, layer, m):
                psum.wait_free(pe, s, f"wd{m}")
                if m == 0:
                    pe.wait_ge(w_2_loaded, 16 * 2 * (layer + 1))
                for k in range(HID_CHUNKS):
                    pe.wait_ge(h2_done.sem, h2_done.at(s, k + 1))
                    last = nc.tensor.matmul(psum.tile(f"wd{m}")[:], w_2[0:hid_rows(k), k, m * P:(m + 1) * P],
                                            h2[0:hid_rows(k), k, :], start=(k == 0), stop=(k == HID_CHUNKS - 1))
                psum.filled(last, f"wd{m}")

            def turn_sum(s, slot, layer, i):
                pe.wait_ge(y_done.sem, y_done.at(s - BATCH, CHUNKS))
                for t in range(2):
                    for c in range(CHUNKS):
                        at, tile = t * DIM + c * P, 2 * i + t
                        last = nc.tensor.transpose(psum.tile(f"wd{i}")[:, at:at + P], x_out[:, c, tile * P:(tile + 1) * P], ident)
                last.then_inc(turned[i].sem, 1)

            pipeline(pe, {"pq": project_q, "pk": project_k, "ptr": turn_qk, "v": values, "score": score, "pt": turn_probs,
                          "att": attend, "ot": turn_output, "wo": project_out, "mean": mean, "var": var,
                          "ga": gate_and_value, "wd": project_down, "turn": turn_sum})

        @block.scalar
        def _(act):
            def square_qk(s, slot, layer, w):
                act.wait_ge(qk_sum_done.sem, qk_sum_done.at(s, w))
                for i, stem in enumerate("qk"):
                    psum.wait_full(act, s, f"{stem}{w}")
                    nc.scalar.activation(qk_sq[:, i, :], psum.tile(f"{stem}{w}")[:], ACT.Square).then_inc(qk_sq_done.sem, 1)

            def rate_qk(s, slot, layer, w):
                act.wait_ge(qk_floor_done.sem, qk_floor_done.at(s, w + 1))
                nc.scalar.activation(qk_rate[:], qk_rate[:], ACT.Ln, scale=SCREEN).then_inc(qk_ln_done.sem, 1)
                act.wait_ge(qk_ln_done.sem, qk_ln_done.at(s, w + 1))
                nc.scalar.activation(qk_rate[:], qk_rate[:], ACT.Exp, scale=-0.5, bias=norm_bias[:]).then_inc(qk_rate_done.sem, 1)

            def copy_q(s, slot, layer, w):
                if not (isinstance(s, int) and s == 0):
                    act.wait_ge(masked_done.sem, masked_done.at(s - 1, PAIRS * (w + 1)))
                psum.wait_full(act, s, f"q_t{w}")
                nc.scalar.activation(q_t[:, :, w * P:(w + 1) * P],
                                     psum.tile(f"q_t{w}")[:].rearrange("p (n c) -> p n c", c=P), ACT.Copy).then_inc(q_t_done.sem, 1)

            def values(s, slot, layer, t):
                psum.wait_full(act, s, f"v{t}")
                nc.scalar.activation(v[slot][:, t, :], psum.tile(f"v{t}")[:], ACT.Copy).then_inc(v_done.sem, 1)

            def exponentials(s, slot, w):
                lo, hi = keys_of(w)
                act.wait_ge(row_bias_done.sem, row_bias_done.at(s, w + 1))
                for h in range(HEADS):
                    e = nc.scalar.activation(scores[w % 2][:, h, lo:hi], scores[w % 2][:, h, lo:hi], ACT.Exp,
                                             bias=row_bias[:, w, h:h + 1], accum_out=row_sum[:, w, h:h + 1])
                    if h % 2:
                        e.then_inc(probs_done.sem, 1)

            def copy_turned(s, slot, w, i):
                if (w, i) in on_act:
                    name = f"pt{w}_{i}"
                    psum.wait_full(act, s, name)
                    act.wait_ge(o_done.sem, o_done.at(s, max(w - 1, 0)))
                    to = probs_t[w % 2][:, 4 * i:4 * i + 4, :] if w else probs_t[0][:, 8 * i + 1:8 * i + 8:2, :]
                    nc.scalar.activation(to, psum.tile(name)[:].rearrange("p (n c) -> p n c", c=P), ACT.Copy)\
                        .then_inc(probs_t_act.sem, 1)

            def copy_output(s, slot, w):
                psum.wait_full(act, s, f"ot{w}")
                act.wait_ge(x2_done.sem, x2_done.at(s))
                nc.scalar.activation(o_t[:, :, w * WINDOW:(w + 1) * WINDOW],
                                     psum.tile(f"ot{w}")[:].rearrange("p (n c) -> p n c", c=P), ACT.Copy).then_inc(o_t_done.sem, 1)

            def square(s, slot, layer, _):
                act.wait_ge(x_out_done.sem, x_out_done.at(s))
                act.wait_ge(xc_done.sem, xc_done.at(s, CHUNKS))
                nc.scalar.activation(sq, xc[:], ACT.Square).then_inc(sq_done.sem, 1)

            def deviation(s, slot, layer, _):
                act.wait_ge(xn_done.sem, xn_done.at(s))
                psum.wait_full(act, s, "var")
                nc.scalar.activation(rstd[:], psum.tile("var")[:], ACT.Ln, bias=eps_bias[:]).then_inc(ln_done.sem, 1)
                act.wait_ge(ln_done.sem, ln_done.at(s, 1))
                nc.scalar.activation(rstd[:], rstd[:], ACT.Exp, scale=-0.5).then_inc(rstd_done.sem, 1)

            def affine(s, slot, layer, _):
                act.wait_ge(h2_done.sem, h2_done.at(s))
                act.wait_ge(xn_done.sem, xn_done.at(s, 1))
                for c in range(CHUNKS):
                    nc.scalar.activation(hn[:, c, :], xc[:, c, :], ACT.Identity, scale=ln_g[:, bass.ds(s, 1), c],
                                         bias=ln_b[:, bass.ds(s, 1), c]).then_inc(hn_done.sem, 1)

            def gate(s, slot, layer, m):
                rows = hid_rows(m)
                act.wait_ge(h2_done.sem, h2_done.at(s, max(m - 1, 0)))
                psum.wait_full(act, s, f"g{m}")
                at = 0 if m < HID // P else G_TAIL_AT
                if m == 0 and layer == DEPTH - 1:
                    act.wait_ge(y_done.sem, y_done.at(s - BATCH))
                nc.scalar.activation(gelu[m % 2][0:rows, :], psum.tile(f"g{m}")[at:at + rows, :], ACT.Gelu,
                                     bias=b_1g[at:at + rows, bass.ds(s, 1), m]).then_inc(gelu_done.sem, 1)
                if m == HID_CHUNKS - 1:
                    nc.scalar.preload_act_table_set(EXP_AND_LN)

            def copy_tokens(s, slot, layer, i):
                act.wait_ge(turned[i].sem, turned[i].at(s - BATCH, 1))
                nc.scalar.activation(tokens_of(tokens)[:, 2 * i:2 * i + 2, :],
                                     psum.tile(f"wd{i}")[:].rearrange("p (t d) -> p t d", d=DIM), ACT.Copy).then_inc(tokens_done.sem, 1)

            nc.scalar.preload_act_table_set(EXP_AND_LN)
            pipeline(act, {"psq": square_qk, "prate": rate_qk, "ptc": copy_q, "vc": values, "exp": exponentials, "pt": copy_turned,
                           "otc": copy_output, "sq": square, "dev": deviation, "hn": affine, "gelu": gate, "turnc": copy_tokens})

        @block.gpsimd
        def _(pool):
            def times_cos(s, slot, layer, w):
                pool.wait_ge(qk_rot_done.sem, qk_rot_done.at(s, w))
                pool.wait_ge(qk_done.sem, qk_done.at(s, 2 * w + 2))
                nc.gpsimd.tensor_tensor(by_head(by_cos), by_head(qk), for_heads(rotary[layer][:, w, 0], DIM_HEAD), ALU.mult)\
                    .then_inc(by_cos_done.sem, 1)

            pipeline(pool, {"prot": times_cos})

        @block.vector
        def _(dve):
            def cut_parts(s, x, upper, lower, signal):
                x = x[:, :, 0:SEQ]
                nc.vector.tensor_copy(upper[:].bitcast(F32R), x).then_inc(signal.sem, 1)
                dve.wait_ge(signal.sem, signal.at(s, 1))
                nc.vector.tensor_tensor(lower[:].bitcast(F32R), x, upper[:], ALU.subtract).then_inc(signal.sem, 1)

            def cut_hx(s, slot, layer, _):
                dve.wait_ge(hx_loaded.sem, hx_loaded.at(s, CHUNKS))
                cut_parts(s, hx, hx_upper, hx_lower, hx_cut)

            def cut_hn(s, slot, layer, _):
                dve.wait_ge(hn_done.sem, hn_done.at(s, CHUNKS))
                cut_parts(s, hn, hn_upper, hn_lower, hn_cut)

            def sum_squares(s, slot, layer, w):
                dve.wait_ge(qk_sq_done.sem, qk_sq_done.at(s, 2 * w + 2))
                nc.vector.tensor_reduce(qk_rate[:].rearrange("p x h -> p (x h)"),
                                        qk_sq[:].rearrange("p x (h d) -> p (x h) d", d=DIM_HEAD), AX_X, ALU.add)\
                    .then_inc(qk_sum_done.sem, 1)
                dve.wait_ge(qk_sum_done.sem, qk_sum_done.at(s, w + 1))
                nc.vector.tensor_scalar(qk_rate[:], qk_rate[:], 1e-24, None, ALU.max).then_inc(qk_floor_done.sem, 1)

            def normalise_qk(s, slot, layer, w):
                dve.wait_ge(by_cos_done.sem, by_cos_done.at(s, w))
                dve.wait_ge(qk_rate_done.sem, qk_rate_done.at(s, w + 1))
                for i, stem in enumerate("qk"):
                    psum.wait_full(dve, s, f"{stem}{w}")
                    nc.vector.tensor_tensor(qk[:, i, :].rearrange("p (h d) -> p h d", d=DIM_HEAD),
                                            psum.tile(f"{stem}{w}")[:].rearrange("p (h d) -> p h d", d=DIM_HEAD),
                                            qk_rate[:, i, :].unsqueeze(2).to_broadcast([P, HEADS, DIM_HEAD]),
                                            ALU.mult).then_inc(qk_done.sem, 1)

            def times_sin(s, slot, layer, w):
                half = DIM_HEAD // 2
                dve.wait_ge(qk_done.sem, qk_done.at(s, 2 * w + 2))
                for i in range(2):
                    to, source = slice(i * half, (i + 1) * half), slice((1 - i) * half, (2 - i) * half)
                    nc.vector.tensor_tensor(by_head(qk_rot)[:, :, :, to], by_head(qk)[:, :, :, source],
                                            for_heads(rotary[layer][:, w, 1, :, to], half), ALU.mult).then_inc(by_sin_done.sem, 1)

            def add_rotated(s, slot, layer, w):
                dve.wait_ge(by_cos_done.sem, by_cos_done.at(s, w + 1))
                dve.wait_ge(by_sin_done.sem, by_sin_done.at(s, 2 * w + 2))
                nc.vector.tensor_tensor(qk_rot[:], qk_rot[:], by_cos[:], ALU.add).then_inc(qk_rot_done.sem, 1)

            def copy_k(s, slot, layer, w):
                if not (isinstance(s, int) and s == 0):
                    dve.wait_ge(masked_done.sem, masked_done.at(s - 1, PAIRS * min(w + 2, TILES)))
                psum.wait_full(dve, s, f"k_t{w}")
                nc.vector.tensor_copy(k_t[:, :, w * P:(w + 1) * P],
                                      psum.tile(f"k_t{w}")[:].rearrange("p (n c) -> p n c", c=P)).then_inc(k_t_done.sem, 1)

            def mask_scores(s, slot, w, g):
                lo, hi = keys_of(w)
                if g == 0:
                    by_act, by_dve = probs_t_until(w - 2)
                    dve.wait_ge(probs_t_act.sem, probs_t_act.at(s, by_act))
                    dve.wait_ge(probs_t_dve.sem, probs_t_dve.at(s, by_dve))
                for h in range(2):
                    psum.wait_full(dve, s, f"s{w}_{g}_{h}")
                    n = 4 * w + 2 * g + h
                    nc.vector.memset(waiter[:, n:n + 1], 0.0)
                    for n in range(2):
                        at, head = n * 2 * WINDOW, 2 * (2 * g + n) + h
                        last = nc.vector.tensor_tensor_reduce(
                            out=scores[w % 2][:, head, lo:hi], in0=s_banks[h][:, at + lo:at + hi], in1=mask[:, lo:hi],
                            scale=1.0, scalar=MASKED, op0=ALU.add, op1=ALU.max, accum_out=row_max[:, w, head:head + 1])
                    last.then_inc(masked_done.sem, 1)
                if g == 1:
                    dve.wait_ge(masked_done.sem, masked_done.at(s, PAIRS * (w + 1)))
                    nc.vector.tensor_scalar(row_bias[:, w, :], row_max[:, w, :], -1.0, None, ALU.mult).then_inc(row_bias_done.sem, 1)

            def copy_turned(s, slot, w, i):
                if (w, i) in on_dve:
                    psum.wait_full(dve, s, f"pt{w}_{i}")
                    to = probs_t[w % 2][:, 4 * i:4 * i + 4, :] if w else probs_t[0][:, 8 * i + 1:8 * i + 8:2, :]
                    nc.vector.tensor_copy(to, psum.tile(f"pt{w}_{i}")[:].rearrange("p (n c) -> p n c", c=P)).then_inc(probs_t_dve.sem, 1)

            def normalise(s, slot, w):
                dve.wait_ge(probs_done.sem, probs_done.at(s, PAIRS * (w + 1)))
                nc.vector.reciprocal(row_rate[:, w, :], row_sum[:, w, :]).then_inc(row_rate_done.sem, 1)
                dve.wait_ge(row_rate_done.sem, row_rate_done.at(s, w + 1))
                dve.wait_ge(o_t_done.sem, o_t_done.at(s, max(w - 1, 0)))
                psum.wait_full(dve, s, f"o{w}")
                nc.vector.tensor_tensor(o[w % 2][:].rearrange("p (h d) -> p h d", h=HEADS),
                                        psum.tile(f"o{w}")[:].rearrange("p (h d) -> p h d", h=HEADS),
                                        row_rate[:, w, :].unsqueeze(2).to_broadcast([P, HEADS, DIM_HEAD]),
                                        ALU.mult).then_inc(o_done.sem, 1)

            def add_residual(s, slot, layer, c):
                dve.wait_ge(x_res_loaded.sem, x_res_loaded.at(s, 1))
                psum.wait_full(dve, s, f"wo{c}")
                nc.vector.tensor_tensor(plain(x2, c), psum.tile(f"wo{c}")[:], x_res[:, c, :], ALU.add).then_inc(x2_done.sem, 1)
                if c == CHUNKS - 1:
                    dve.wait_ge(x2_done.sem, x2_done.at(s, CHUNKS))
                    dve.wait_ge(xn_done.sem, xn_done.at(s))
                    nc.vector.tensor_tensor(x2_sum[:], shifted(x2, 0), shifted(x2, 1), ALU.add).then_inc(x2_added.sem, 1)

            def add_squares(s, slot, layer, _):
                dve.wait_ge(sq_done.sem, sq_done.at(s, 1))
                nc.vector.tensor_tensor(sq[:, 0, :], sq[:, 0, :], sq[:, 1, :], ALU.add).then_inc(sq_added.sem, 1)

            def centre(s, slot, layer, _):
                dve.wait_ge(x2_done.sem, x2_done.at(s, CHUNKS))
                dve.wait_ge(stored.sem, stored.at(s if layer == 0 else BATCH))
                if layer == DEPTH - 1:
                    dve.wait_ge(tokens_done.sem, tokens_done.at(s - BATCH))
                psum.wait_full(dve, s, "mean")
                for c in range(CHUNKS):
                    nc.vector.tensor_tensor(xc[:, c, :], shifted(x2, c), psum.tile("mean")[:], ALU.subtract).then_inc(xc_done.sem, 1)

            def normalise_tokens(s, slot, layer, _):
                dve.wait_ge(rstd_done.sem, rstd_done.at(s, 1))
                dve.wait_ge(sq_done.sem, sq_done.at(s, 1))
                nc.vector.tensor_tensor(xc[:], xc[:], rstd[:].unsqueeze(1).to_broadcast([P, CHUNKS, SEQ]),
                                        ALU.mult).then_inc(xn_done.sem, 1)

            def gated(s, slot, layer, m):
                rows = hid_rows(m)
                dve.wait_ge(gelu_done.sem, gelu_done.at(s, m + 1))
                if m == CHUNKS and layer == DEPTH - 1:
                    dve.wait_ge(out_stored.sem, out_stored.at(s - BATCH))
                name = f"a{m}" if m < HID // P else f"g{m}"
                psum.wait_full(dve, s, name)
                nc.vector.scalar_tensor_tensor(h2[0:rows, m, :], psum.tile(name)[0:rows, :], b_1a[0:rows, bass.ds(s, 1), m],
                                               gelu[m % 2][0:rows, :], ALU.add, ALU.mult).then_inc(h2_done.sem, 1)

            def finish(s, slot, layer, c):
                psum.wait_full(dve, s, f"wd{c}")
                nc.vector.scalar_tensor_tensor(x_out[:, c, :], psum.tile(f"wd{c}")[:], b_2[:, bass.ds(s, 1), c],
                                               plain(x2, c), ALU.add, ALU.add).then_inc(x_out_done.sem, 1)

            def add_x1(s, slot, layer, c):
                b = s - BATCH
                dve.wait_ge(x1_loaded.sem, x1_loaded.at(b, CHUNKS))
                dve.wait_ge(x_out_done.sem, x_out_done.at(s, c + 1))
                nc.vector.scalar_tensor_tensor(x_out[:, c, :], x_out[:, c, :], mod[:, 2 * MOD_GATE_B + c, bass.ds(b, 1)],
                                               x1_t[c][:], ALU.mult, ALU.add).then_inc(y_done.sem, 1)

            pipeline(dve, {"hxs": cut_hx, "hns": cut_hn, "pss": sum_squares, "pnorm": normalise_qk, "prot": times_sin, "padd": add_rotated, "ptc": copy_k,
                           "mask": mask_scores, "pt": copy_turned, "onorm": normalise, "add": add_residual, "sqs": add_squares, "cen": centre,
                           "xn": normalise_tokens, "gated": gated, "fin": finish, "sum": add_x1})



def load_stack_weights(nc, inp, squares, rotary, ln_g, ln_b, b_1a, b_1g, b_2, w_qkv, w_1, parts_dram):
    with ExitStack() as ctx:
        loaded, b_1_loaded = ctx.enter_context(nc.semaphore("v_loaded")), ctx.enter_context(nc.semaphore("v_b_1_loaded"))
        small = [ctx.enter_context(nc.sbuf_tensor(f"v_small{i}", [P, DEPTH, x.shape[2]], F32))
                 for i, x in enumerate((ln_g, ln_b, b_2, b_1a, b_1g))]
        g, b, b2, b1a, b1g = small
        tables = ctx.enter_context(nc.sbuf_tensor("v_tables", [P, TILES, 2, 2, DIM_HEAD], F32))
        scales = ctx.enter_context(nc.sbuf_tensor("v_scales", [P, DEPTH, 2, 2, DIM_HEAD], F32))
        half, whole, rest = DIM_HEAD // 2, HID // P, HID % P
        next_qkv = [ctx.enter_context(nc.sbuf_tensor(f"v_next_qkv{i}", [P, CHUNKS, 3 * INNER], F32)) for i in range(2)]
        next_w_1 = [ctx.enter_context(nc.sbuf_tensor(f"v_next_w_1{i}", [P, CHUNKS, W_1_COLS], F32)) for i in range(2)]
        wholes = [ctx.enter_context(nc.sbuf_tensor(f"v_whole{i}", [P, CHUNKS, cols], F32))
                  for i, cols in enumerate((3 * INNER, W_1_COLS, W_1_COLS, 3 * INNER))]
        cuts = [("L0_ffn_wqkv", 1, next_qkv), ("L0_ffn_w1", 1, next_w_1), ("L0_ffn_w1", 0, w_1), ("L0_ffn_wqkv", 0, w_qkv)]
        whole_loaded = [ctx.enter_context(nc.semaphore(f"v_whole_loaded{i}")) for i in range(len(cuts))]
        padded, upper_done, lower_done, parts_stored = (ctx.enter_context(nc.semaphore("v_" + name)) for name in
                                                        ("padded", "upper_done", "lower_done", "parts_stored"))
        n_loads, n_b_1 = 2 + 6 * DEPTH + 3 * DEPTH, 4 * DEPTH
        with nc.Block() as block:
            @block.scalar
            def _(act):
                for i, (name, l, (upper, lower)) in enumerate(cuts):
                    source = inp[name][l].rearrange("(c p) f -> p c f", p=P)
                    if name == "L0_ffn_wqkv":
                        act.dma_start(wholes[i][:], source).then_inc(whole_loaded[i], 16)
                    else:
                        act.wait_ge(padded, 2)
                        for to, at, n in ((0, 0, whole * P), (whole * P, HID, whole * P), (2 * whole * P, whole * P, rest),
                                          (2 * whole * P + G_TAIL_AT, HID + whole * P, rest)):
                            act.dma_start(wholes[i][:, :, to:to + n], source[:, :, at:at + n]).then_inc(whole_loaded[i], 16)
                with nc.allow_non_contiguous_dma(reason="short vectors onto partitions"):
                    for to, at, tail in ((b1a, 0, 0), (b1g, HID, G_TAIL_AT)):
                        for l in range(DEPTH):
                            act.dma_start(to[:, l, 0:whole], inp["L0_ffn_b1"][l, at:at + whole * P]
                                          .rearrange("(c p) -> p c", p=P)).then_inc(b_1_loaded, 16)
                            act.dma_start(to[tail:tail + rest, l, whole:whole + 1],
                                          inp["L0_ffn_b1"][l, at + whole * P:at + HID]
                                          .rearrange("(p c) -> p c", c=1)).then_inc(b_1_loaded, 16)
                for i, key in enumerate(("qkv", "w_1")):
                    act.wait_ge(lower_done, i + 1)
                    for part, to in zip(cuts[i][2], parts_dram[key]):
                        act.dma_start(to, part[:]).then_inc(parts_stored, 16)
                act.wait_ge(parts_stored, 16 * 4)

            @block.sync
            def _(sp):
                with nc.allow_non_contiguous_dma(reason="short vectors onto partitions"):
                    def put(to, src):
                        sp.dma_start(to, src).then_inc(loaded, 16)

                    put(squares[:], inp["c_squares"].rearrange("p (s c) -> p s c", c=P))
                    put(tables[:], inp["c_rotary"])
                    for l in range(DEPTH):
                        for i, name in enumerate(("L0_ffn_q_scale", "L0_ffn_k_scale")):
                            row = inp[name][l:l + 1]
                            put(scales[:, l, 0, i, :], row.to_broadcast([P, DIM_HEAD]))
                            put(scales[:, l, 1, i, 0:half], row[:, half:].to_broadcast([P, half]))
                            put(scales[:, l, 1, i, half:], row[:, 0:half].to_broadcast([P, half]))
                    for to, name in ((g, "L0_ffn_ln_g"), (b, "L0_ffn_ln_b"), (b2, "L0_ffn_b2")):
                        for l in range(DEPTH):
                            put(to[:, l, :], inp[name][l].rearrange("(c p) -> p c", p=P))

            @block.vector
            def _(dve):
                for i in (1, 2):
                    nc.vector.memset(wholes[i][:, :, 2 * whole * P:], 0.0).then_inc(padded, 1)
                for i, (name, l, (upper, lower)) in enumerate(cuts):
                    dve.wait_ge(whole_loaded[i], 16 if name == "L0_ffn_wqkv" else 16 * 4)
                    nc.vector.tensor_copy(upper[:].bitcast(F32R), wholes[i][:]).then_inc(upper_done, 1)
                    dve.wait_ge(upper_done, i + 1)
                    nc.vector.tensor_tensor(lower[:].bitcast(F32R), wholes[i][:], upper[:], ALU.subtract).then_inc(lower_done, 1)
                dve.wait_ge(loaded, 16 * n_loads)
                dve.wait_ge(b_1_loaded, 16 * n_b_1)
                for l in range(DEPTH):
                    nc.vector.tensor_tensor(rotary[l][:].rearrange("p w a b d -> p w (a b d)"),
                                            tables[:].rearrange("p w a b d -> p w (a b d)"),
                                            scales[:, l].rearrange("p a b d -> p (a b d)").unsqueeze(1)
                                            .to_broadcast([P, TILES, 4 * DIM_HEAD]), ALU.mult)
                for to, src in ((ln_g, g), (ln_b, b), (b_2, b2)):
                    for l in range(DEPTH):
                        part = to[:, l * BATCH:(l + 1) * BATCH, :]
                        nc.vector.tensor_copy(part, src[:, l, :].unsqueeze(1).to_broadcast(list(part.shape)))
                for to, src, tail in ((b_1a, b1a, 0), (b_1g, b1g, G_TAIL_AT)):
                    for l in range(DEPTH):
                        part = to[:, l * BATCH:(l + 1) * BATCH, 0:whole]
                        nc.vector.tensor_copy(part, src[:, l, 0:whole].unsqueeze(1).to_broadcast(list(part.shape)))
                        part = to[tail:tail + rest, l * BATCH:(l + 1) * BATCH, whole:whole + 1]
                        nc.vector.tensor_copy(part, src[tail:tail + rest, l, whole:whole + 1].unsqueeze(1)
                                              .to_broadcast(list(part.shape)))


def setup_weights(nc, inp, banks, ident, mean_mat, pick, picks, w_in_t, w_dt_t, w_bc_t, w_out_t,
                  neg_a, b_dt, skip_d, mod, ln_eps):
    with ExitStack() as ctx:
        def sb(name, shape, dt=F32):
            return ctx.enter_context(nc.sbuf_tensor("s_" + name, shape, dt))

        def sem(name):
            return ctx.enter_context(nc.semaphore("s_" + name))

        w_in = sb("w_in", [P, 8, DIM])
        w_dt = sb("w_dt", [P, INNER_CHUNKS, D_INNER])
        w_out = sb("w_out", [P, CHUNKS, D_INNER])
        w_bc = sb("w_bc", [2 * STATES, D_INNER])
        cond = sb("cond", [BATCH, DIM])
        cond_t = sb("cond_t", [P, CHUNKS, BATCH])
        w_mod = sb("w_mod", [P, CHUNKS, 6 * DIM])
        a_log = sb("a_log", [P, INNER_CHUNKS, STATES])
        gate = sb("gate", [P, 1])
        sign = sb("sign", [P, 2 * CHUNKS, BATCH])
        size = sb("size", [P, 2 * CHUNKS, BATCH])

        squares_loaded, w_in_loaded, w_dt_loaded = sem("squares_loaded"), sem("w_in_loaded"), sem("w_dt_loaded")
        w_out_loaded, w_bc_loaded, small_loaded = sem("w_out_loaded"), sem("w_bc_loaded"), sem("small_loaded")
        cond_loaded, w_mod_loaded = sem("cond_loaded"), sem("w_mod_loaded")
        turned, copied, upper_done = sem("turned"), sem("copied"), sem("upper_done")
        silu_done, cond_turned, cond_copied = sem("silu_done"), sem("cond_turned"), sem("cond_copied")
        mod_full, mod_copied, gate_step = sem("mod_full"), sem("mod_copied"), sem("gate_step")
        mod_step, a_step = sem("mod_step"), sem("a_step")

        turns = []
        for c in range(CHUNKS):
            for half in range(2):
                turns.append((w_in_loaded, [w_in[:, 4 * half + m, c * P:(c + 1) * P] for m in range(4)],
                              [part[:, c, half * 512:(half + 1) * 512] for part in w_in_t], P))
        for k in range(INNER_CHUNKS):
            turns.append((w_dt_loaded, [w_dt[:, m, k * P:(k + 1) * P] for m in range(4)], [w_dt_t[:, k, :]], P))
        for k in range(INNER_CHUNKS):
            turns.append((w_out_loaded, [w_out[:, o, k * P:(k + 1) * P] for o in range(CHUNKS)], [w_out_t[:, k, :]], P))
        for k in range(INNER_CHUNKS):
            turns.append((w_bc_loaded, [w_bc[:, k * P:(k + 1) * P]], [w_bc_t[:, k, :]], 2 * STATES))

        with nc.Block() as block:
            @block.sync
            def _(sp):
                sp.dma_start(ident[:], inp["c_squares"][:, 0:P]).then_inc(squares_loaded, 16)
                sp.dma_start(mean_mat[:], inp["c_squares"][:, P:2 * P]).then_inc(squares_loaded, 16)
                sp.dma_start(w_in[:], inp["L0_attn_W_in"].rearrange("(m p) d -> p m d", p=P)).then_inc(w_in_loaded, 16)
                sp.dma_start(cond[:], inp["L0_c"]).then_inc(cond_loaded, 16)
                sp.dma_start(w_dt[:], inp["L0_attn_W_dt"].rearrange("(m p) d -> p m d", p=P)).then_inc(w_dt_loaded, 16)
                sp.dma_start(w_out[:], inp["L0_attn_W_out"].rearrange("(m p) d -> p m d", p=P)).then_inc(w_out_loaded, 16)
                sp.dma_start(w_bc[0:STATES, :], inp["L0_attn_W_B"]).then_inc(w_bc_loaded, 16)
                sp.dma_start(w_bc[STATES:, :], inp["L0_attn_W_C"]).then_inc(w_bc_loaded, 16)
                sp.dma_start(w_mod[:], inp["L0_wmod"].rearrange("(c p) f -> p c f", p=P)).then_inc(w_mod_loaded, 16)

            @block.scalar
            def _(act):
                act.dma_start(pick[:], inp["c_pick"]).then_inc(small_loaded, 16)
                act.dma_start(a_log[:], inp["L0_attn_A_log"].rearrange("(c p) n -> p c n", p=P)).then_inc(small_loaded, 16)
                with nc.allow_non_contiguous_dma(reason="three short vectors"):
                    act.dma_start(b_dt[:], inp["L0_attn_b_dt"].rearrange("(c p) -> p c", p=P)).then_inc(small_loaded, 16)
                    act.dma_start(skip_d[:], inp["L0_attn_D"].rearrange("(c p) -> p c", p=P)).then_inc(small_loaded, 16)
                    act.dma_start(gate[:], inp["L0_attn_output_gate"].rearrange("(a b) -> a b", a=1)
                                  .to_broadcast([P, 1])).then_inc(small_loaded, 16)
                act.wait_ge(cond_loaded, 16)
                nc.scalar.activation(cond[:], cond[:], ACT.Silu).then_inc(silu_done, 1)
                act.wait_ge(small_loaded, 16 * 5)
                nc.scalar.activation(gate[:], gate[:], ACT.Sigmoid).then_inc(gate_step, 1)
                nc.scalar.activation(a_log[:], a_log[:], ACT.Exp).then_inc(a_step, 1)

            @block.tensor
            def _(pe):
                pe.wait_ge(squares_loaded, 32)
                pe.wait_ge(silu_done, 1)
                for c in range(CHUNKS):
                    last = nc.tensor.transpose(banks[7][:, c * BATCH:(c + 1) * BATCH], cond[:, c * P:(c + 1) * P],
                                               ident[0:BATCH, 0:BATCH])
                last.then_inc(cond_turned, 1)
                for i, (loaded, sources, _, rows) in enumerate(turns):
                    pe.wait_ge(loaded, 32 if loaded is w_bc_loaded else 16)
                    if i >= 6:
                        pe.wait_ge(copied, i - 5)
                    for m, s in enumerate(sources):
                        last = nc.tensor.transpose(banks[i % 6][:, m * rows:(m + 1) * rows], s, ident[0:rows, 0:rows])
                    last.then_inc(turned, 1)
                pe.wait_ge(w_mod_loaded, 16)
                pe.wait_ge(cond_copied, 1)
                for f in range(12):
                    for c in range(CHUNKS):
                        last = nc.tensor.matmul(banks[6][:, f * BATCH:(f + 1) * BATCH], w_mod[:, c, f * P:(f + 1) * P],
                                                cond_t[:, c, :], start=(c == 0), stop=(c == CHUNKS - 1))
                last.then_inc(mod_full, 1)

            @block.vector
            def _(dve):
                nc.vector.memset(ln_eps[:], LN_EPS)
                dve.wait_ge(cond_turned, 1)
                nc.vector.tensor_copy(cond_t[:].rearrange("p c b -> p (c b)"), banks[7][:, 0:CHUNKS * BATCH]).then_inc(cond_copied, 1)
                for i, (_, sources, targets, rows) in enumerate(turns):
                    dve.wait_ge(turned, i + 1)
                    full = banks[i % 6][:, 0:len(sources) * rows]
                    if len(targets) == 1:
                        nc.vector.tensor_copy(targets[0], full).then_inc(copied, 1)
                    else:
                        upper, lower = targets
                        nc.vector.tensor_copy(upper.bitcast(F32R), full).then_inc(upper_done, 1)
                        dve.wait_ge(upper_done, i + 1)
                        nc.vector.tensor_tensor(lower.bitcast(F32R), full, upper, ALU.subtract).then_inc(copied, 1)
                dve.wait_ge(a_step, 1)
                nc.vector.tensor_scalar(neg_a[:], a_log[:], -1.0, None, ALU.mult)
                nc.vector.tensor_copy(picks[0:96], pick[0:96].unsqueeze(2).to_broadcast([96, STATES, P]))
                dve.wait_ge(mod_full, 1)
                nc.vector.tensor_copy(mod[:].rearrange("p f b -> p (f b)"), banks[6][:, 0:12 * BATCH]).then_inc(mod_copied, 1)
                dve.wait_ge(mod_copied, 1)
                for s in (MOD_SCALE_A, MOD_SCALE_B):
                    part = mod[:, 2 * s:2 * s + 2, :]
                    nc.vector.tensor_scalar(part, part, 1.0, None, ALU.add)
                for i, g in enumerate((MOD_GATE_A, MOD_GATE_B)):
                    part, at = mod[:, 2 * g:2 * g + 2, :], slice(2 * i, 2 * i + 2)
                    nc.vector.tensor_scalar(sign[:, at], part, 0.0, 2.0, ALU.is_ge, ALU.mult).then_inc(mod_step, 1)
                    nc.vector.scalar_tensor_tensor(size[:, at], part, -1.0, part, ALU.mult, ALU.max).then_inc(mod_step, 1)
                dve.wait_ge(mod_step, 4)
                nc.vector.tensor_scalar(sign[:], sign[:], 1.0, None, ALU.subtract).then_inc(mod_step, 1)
                nc.vector.tensor_scalar(size[:], size[:], 0.25, None, ALU.max).then_inc(mod_step, 1)
                dve.wait_ge(mod_step, 6)
                dve.wait_ge(gate_step, 1)
                nc.vector.scalar_tensor_tensor(mod[:, 2 * MOD_GATE_A:2 * MOD_GATE_A + 2, :], sign[:, 0:2], gate[:, 0:1],
                                               size[:, 0:2], ALU.mult, ALU.mult)
                nc.vector.tensor_tensor(mod[:, 2 * MOD_GATE_B:2 * MOD_GATE_B + 2, :], sign[:, 2:4], size[:, 2:4], ALU.mult)


def build(nc, inp, out):
    x1_dram = nc.dram_tensor("x1_rows", (BATCH, P, CHUNKS, SEQ), F32, kind="Internal").ap()
    c_dram = nc.dram_tensor("c_rows", (BATCH, STATES, SEQ), F32, kind="Internal").ap()
    stack_dram = nc.dram_tensor("stack_rows", (DEPTH * BATCH, P, CHUNKS, SEQ), F32, kind="Internal").ap()
    parts_dram = {key: [nc.dram_tensor(f"{key}_part{i}", (P, CHUNKS, cols), F32, kind="Internal").ap() for i in range(2)]
                  for key, cols in (("qkv", 3 * INNER), ("w_1", W_1_COLS))}
    with nc.sbuf_tensor("mod", [P, 12, BATCH], F32) as mod:
        mixer_pass(nc, inp, mod, x1_dram, stack_dram, c_dram)
        stack_pass(nc, inp, mod, x1_dram, stack_dram, parts_dram, out)


NAMES = ["L0_attn_x", "L0_attn_W_in", "L0_attn_A_log", "L0_attn_W_B", "L0_attn_W_C", "L0_attn_W_dt", "L0_attn_b_dt",
         "L0_attn_D", "L0_attn_output_gate", "L0_attn_W_out", "L0_ffn_wqkv", "L0_ffn_q_scale", "L0_ffn_k_scale",
         "L0_ffn_wo", "L0_ffn_ln_g", "L0_ffn_ln_b", "L0_ffn_w1", "L0_ffn_b1", "L0_ffn_w2", "L0_ffn_b2", "L0_c", "L0_wmod"]


def kernel(**inputs):
    import concourse.bacc as bacc
    from concourse.bass_utils import run_bass_kernel_spmd

    nc = bacc.Bacc("TRN2", target_bir_lowering=False, num_devices=1)
    arrays = {name: np.ascontiguousarray(inputs[name]) for name in NAMES}
    arrays.update(host_constants())
    inp = {name: nc.dram_tensor("in_" + name, a.shape, mybir.dt.from_np(a.dtype), kind="ExternalInput").ap()
           for name, a in arrays.items()}
    out = nc.dram_tensor("out_rows", (BATCH, SEQ, DIM), F32, kind="ExternalOutput").ap()
    build(nc, inp, out)
    result = run_bass_kernel_spmd(nc, [{"in_" + name: a for name, a in arrays.items()}], core_ids=[0])
    return result.results[0]["out_rows"]
```
